# Optimizing a Trainium2 kernel written in Bass

```python
import numpy as np
import jax
import jax.numpy as jnp

def _softmax(x, axis=-1):
    return jax.nn.softmax(x, axis=axis)

def _gelu(x):
    return jax.nn.gelu(x, approximate=True)

def _silu(x):
    return jax.nn.silu(x)

def _sigmoid(x):
    return jax.nn.sigmoid(x)

def _layernorm(x, axis=-1, eps=1e-05):
    m = jnp.mean(x, axis=axis, keepdims=True)
    v = jnp.var(x, axis=axis, keepdims=True)
    return (x - m) / jnp.sqrt(v + eps)

def _scatter_add(tgt, idx, src, axis=0):
    return tgt.at[idx].add(src)

def _segment_sum(src, seg, n):
    return jax.ops.segment_sum(src, seg, n)
kernel_name = 'mk_vit_tower_cls_d2_tok_img512_r4_6ce8b3'

def setup_inputs(seed: int=0):
    np.random.seed(seed)
    _w = jnp.asarray

    def _rec_inputs():
        import jax
        import jax.numpy as jnp
        _rk = jax.random.key(seed)
        x = 7.57192e-06 + 1.00007 * jax.random.normal(jax.random.fold_in(_rk, 1), (64, 3, 224, 224), jnp.float32)
        cls_tok = 0.02 * jax.random.normal(jax.random.fold_in(_rk, 5), (1, 1, 128), jnp.float32)
        return (x, cls_tok)
    x, cls_tok = _rec_inputs()

    def _L0_tok_setup():
        import jax, jax.numpy as jnp
        import numpy as np
        DEPTH = 4
        HEADS = 8
        DIM = 128
        HID = 256
        P = 16
        IMG = 224
        GRID = IMG // P
        NPATCH = GRID * GRID
        NTOK = NPATCH + 1
        BATCH = 64
        EPS = 1e-05

        def layernorm(x, w, b):
            mu = jnp.mean(x, axis=-1, keepdims=True)
            var = jnp.mean(jnp.square(x - mu), axis=-1, keepdims=True)
            return (x - mu) * jax.lax.rsqrt(var + EPS) * w + b
        key = jax.random.key(seed)
        ks = jax.random.split(key, 12)
        s = 0.02
        inp = {'x': jax.random.normal(ks[0], (BATCH, 3, IMG, IMG), jnp.float32), 'conv_w': jax.random.normal(ks[1], (3 * P * P, DIM), jnp.float32) * s, 'conv_b': jnp.zeros((DIM,), jnp.float32), 'cls_token': jax.random.normal(ks[2], (1, 1, DIM), jnp.float32) * s, 'pos_embed': jax.random.normal(ks[3], (1, NTOK, DIM), jnp.float32) * s, 'ln1_w': jnp.ones((DEPTH, DIM), jnp.float32), 'ln1_b': jnp.zeros((DEPTH, DIM), jnp.float32), 'qkv_w': jax.random.normal(ks[4], (DEPTH, DIM, 3 * DIM), jnp.float32) * s, 'qkv_b': jnp.zeros((DEPTH, 3 * DIM), jnp.float32), 'proj_w': jax.random.normal(ks[5], (DEPTH, DIM, DIM), jnp.float32) * s, 'proj_b': jnp.zeros((DEPTH, DIM), jnp.float32), 'ln2_w': jnp.ones((DEPTH, DIM), jnp.float32), 'ln2_b': jnp.zeros((DEPTH, DIM), jnp.float32), 'fc1_w': jax.random.normal(ks[6], (DEPTH, DIM, HID), jnp.float32) * s, 'fc1_b': jnp.zeros((DEPTH, HID), jnp.float32), 'fc2_w': jax.random.normal(ks[7], (DEPTH, HID, DIM), jnp.float32) * s, 'fc2_b': jnp.zeros((DEPTH, DIM), jnp.float32), 'norm_w': jnp.ones((DIM,), jnp.float32), 'norm_b': jnp.zeros((DIM,), jnp.float32)}
        return inp
    _L0_tok_all = _L0_tok_setup()
    _L0_tok_in = {k: v for k, v in _L0_tok_all.items() if k in ('conv_w', 'conv_b', 'cls_token', 'pos_embed', 'ln1_w', 'ln1_b', 'qkv_w', 'qkv_b', 'proj_w', 'proj_b', 'ln2_w', 'ln2_b', 'fc1_w', 'fc1_b', 'fc2_w', 'fc2_b', 'norm_w', 'norm_b')}
    del _L0_tok_all

    def _L0_attn_setup():
        import jax, jax.numpy as jnp
        import numpy as np
        GAMMA = 0.96
        key = jax.random.key(seed)
        k1, k2, k3, k4 = jax.random.split(key, 4)
        B, S, D_IN, D_OUT = (4, 1024, 128, 128)
        x = jax.random.normal(k1, (B, S, D_IN), dtype=jnp.float32)
        scale = 1.0 / np.sqrt(D_IN)
        Wq = jax.random.normal(k2, (D_IN, D_OUT), dtype=jnp.float32) * scale
        Wk = jax.random.normal(k3, (D_IN, D_OUT), dtype=jnp.float32) * scale
        Wv = jax.random.normal(k4, (D_IN, D_OUT), dtype=jnp.float32) * scale
        return {'x': x, 'Wq': Wq, 'Wk': Wk, 'Wv': Wv}
    _L0_attn_all = _L0_attn_setup()
    _L0_attn_in = {k: v for k, v in _L0_attn_all.items() if k in ('Wq', 'Wk', 'Wv')}
    del _L0_attn_all

    def _L0_ffn_setup():
        import jax, jax.numpy as jnp
        import numpy as np
        EPS = 1e-05
        TOP_K = 2

        def layer_norm(x, g, b):
            m = x.mean(-1, keepdims=True)
            v = ((x - m) ** 2).mean(-1, keepdims=True)
            return (x - m) / jnp.sqrt(v + EPS) * g + b
        key = jax.random.key(seed)
        ks = jax.random.split(key, 8)
        B, S, D, E, H = (8, 128, 128, 8, 512)
        x = jax.random.normal(ks[0], (B, S, D), dtype=jnp.float32)
        Wg = jax.random.normal(ks[1], (D, E), dtype=jnp.float32) * 0.02
        W1 = jax.random.normal(ks[2], (E, D, H), dtype=jnp.float32) * 0.02
        b1 = jnp.zeros((E, H), dtype=jnp.float32)
        W2 = jax.random.normal(ks[3], (E, H, D), dtype=jnp.float32) * 0.02
        b2 = jnp.zeros((E, D), dtype=jnp.float32)
        ln_g = jnp.ones((D,), dtype=jnp.float32)
        ln_b = jnp.zeros((D,), dtype=jnp.float32)
        out_g = jnp.ones((D,), dtype=jnp.float32)
        out_b = jnp.zeros((D,), dtype=jnp.float32)
        return {'x': x, 'Wg': Wg, 'W1': W1, 'b1': b1, 'W2': W2, 'b2': b2, 'ln_g': ln_g, 'ln_b': ln_b, 'out_g': out_g, 'out_b': out_b}
    _L0_ffn_all = _L0_ffn_setup()
    _L0_ffn_in = {k: v for k, v in _L0_ffn_all.items() if k in ('Wg', 'W1', 'b1', 'W2', 'b2', 'ln_g', 'ln_b', 'out_g', 'out_b')}
    del _L0_ffn_all

    def _L1_attn_setup():
        import jax, jax.numpy as jnp
        import numpy as np
        EPS = 1e-12

        def _l2norm(x):
            n = jnp.sqrt(jnp.sum(x * x, axis=-1, keepdims=True))
            return x / jnp.maximum(n, EPS)
        key = jax.random.key(seed)
        ks = jax.random.split(key, 8)
        B, T, V = (4, 512, 128)
        C, H, NB = (128, 4, 64)
        return {'x': jax.random.normal(ks[0], (B, T, V), dtype=jnp.float32), 'basis': jax.random.normal(ks[1], (V, 2 * NB), dtype=jnp.float32), 'shared_q_w': jax.random.normal(ks[2], (V, C), dtype=jnp.float32) * 0.02, 'shared_k_w': jax.random.normal(ks[3], (V, C), dtype=jnp.float32) * 0.02, 'v_coeffs': jax.random.normal(ks[4], (C, 2 * NB), dtype=jnp.float32) * 0.02, 'o_coeffs': jax.random.normal(ks[5], (C, 2 * NB), dtype=jnp.float32) * 0.02, 'decay_logits': jnp.linspace(1.0, 5.0, H, dtype=jnp.float32), 'out_scale': jnp.float32(0.1)}
    _L1_attn_all = _L1_attn_setup()
    _L1_attn_in = {k: v for k, v in _L1_attn_all.items() if k in ('basis', 'shared_q_w', 'shared_k_w', 'v_coeffs', 'o_coeffs', 'decay_logits', 'out_scale')}
    del _L1_attn_all

    def _L1_ffn_setup():
        import jax, jax.numpy as jnp
        import numpy as np
        B, S, H, E, K = (8, 1024, 128, 8, 2)
        key = jax.random.key(seed)
        ks = jax.random.split(key, 7)
        s_h = 1.0 / np.sqrt(H)
        s_2h = 1.0 / np.sqrt(2 * H)
        return {'x': jax.random.normal(ks[0], (B, S, H), dtype=jnp.float32), 'gate_w': jax.random.uniform(ks[1], (H, E), minval=-s_h, maxval=s_h, dtype=jnp.float32), 'gate_b': jax.random.uniform(ks[2], (E,), minval=-s_h, maxval=s_h, dtype=jnp.float32), 'w1': jax.random.uniform(ks[3], (E, H, 2 * H), minval=-s_h, maxval=s_h, dtype=jnp.float32), 'b1': jax.random.uniform(ks[4], (E, 2 * H), minval=-s_h, maxval=s_h, dtype=jnp.float32), 'w2': jax.random.uniform(ks[5], (E, 2 * H, H), minval=-s_2h, maxval=s_2h, dtype=jnp.float32), 'b2': jax.random.uniform(ks[6], (E, H), minval=-s_2h, maxval=s_2h, dtype=jnp.float32)}
    _L1_ffn_all = _L1_ffn_setup()
    _L1_ffn_in = {k: v for k, v in _L1_ffn_all.items() if k in ('gate_w', 'gate_b', 'w1', 'b1', 'w2', 'b2')}
    del _L1_ffn_all
    return {'x': x, 'cls_tok': cls_tok, 'L0_tok_conv_w': _L0_tok_in['conv_w'], 'L0_tok_conv_b': _L0_tok_in['conv_b'], 'L0_tok_cls_token': _L0_tok_in['cls_token'], 'L0_tok_pos_embed': _L0_tok_in['pos_embed'], 'L0_tok_ln1_w': _L0_tok_in['ln1_w'], 'L0_tok_ln1_b': _L0_tok_in['ln1_b'], 'L0_tok_qkv_w': _L0_tok_in['qkv_w'], 'L0_tok_qkv_b': _L0_tok_in['qkv_b'], 'L0_tok_proj_w': _L0_tok_in['proj_w'], 'L0_tok_proj_b': _L0_tok_in['proj_b'], 'L0_tok_ln2_w': _L0_tok_in['ln2_w'], 'L0_tok_ln2_b': _L0_tok_in['ln2_b'], 'L0_tok_fc1_w': _L0_tok_in['fc1_w'], 'L0_tok_fc1_b': _L0_tok_in['fc1_b'], 'L0_tok_fc2_w': _L0_tok_in['fc2_w'], 'L0_tok_fc2_b': _L0_tok_in['fc2_b'], 'L0_tok_norm_w': _L0_tok_in['norm_w'], 'L0_tok_norm_b': _L0_tok_in['norm_b'], 'L0_attn_Wq': _L0_attn_in['Wq'], 'L0_attn_Wk': _L0_attn_in['Wk'], 'L0_attn_Wv': _L0_attn_in['Wv'], 'L0_ffn_Wg': _L0_ffn_in['Wg'], 'L0_ffn_W1': _L0_ffn_in['W1'], 'L0_ffn_b1': _L0_ffn_in['b1'], 'L0_ffn_W2': _L0_ffn_in['W2'], 'L0_ffn_b2': _L0_ffn_in['b2'], 'L0_ffn_ln_g': _L0_ffn_in['ln_g'], 'L0_ffn_ln_b': _L0_ffn_in['ln_b'], 'L0_ffn_out_g': _L0_ffn_in['out_g'], 'L0_ffn_out_b': _L0_ffn_in['out_b'], 'L1_attn_basis': _L1_attn_in['basis'], 'L1_attn_shared_q_w': _L1_attn_in['shared_q_w'], 'L1_attn_shared_k_w': _L1_attn_in['shared_k_w'], 'L1_attn_v_coeffs': _L1_attn_in['v_coeffs'], 'L1_attn_o_coeffs': _L1_attn_in['o_coeffs'], 'L1_attn_decay_logits': _L1_attn_in['decay_logits'], 'L1_attn_out_scale': _L1_attn_in['out_scale'], 'L1_ffn_gate_w': _L1_ffn_in['gate_w'], 'L1_ffn_gate_b': _L1_ffn_in['gate_b'], 'L1_ffn_w1': _L1_ffn_in['w1'], 'L1_ffn_b1': _L1_ffn_in['b1'], 'L1_ffn_w2': _L1_ffn_in['w2'], 'L1_ffn_b2': _L1_ffn_in['b2']}

def reference(x, cls_tok, L0_tok_conv_w, L0_tok_conv_b, L0_tok_cls_token, L0_tok_pos_embed, L0_tok_ln1_w, L0_tok_ln1_b, L0_tok_qkv_w, L0_tok_qkv_b, L0_tok_proj_w, L0_tok_proj_b, L0_tok_ln2_w, L0_tok_ln2_b, L0_tok_fc1_w, L0_tok_fc1_b, L0_tok_fc2_w, L0_tok_fc2_b, L0_tok_norm_w, L0_tok_norm_b, L0_attn_Wq, L0_attn_Wk, L0_attn_Wv, L0_ffn_Wg, L0_ffn_W1, L0_ffn_b1, L0_ffn_W2, L0_ffn_b2, L0_ffn_ln_g, L0_ffn_ln_b, L0_ffn_out_g, L0_ffn_out_b, L1_attn_basis, L1_attn_shared_q_w, L1_attn_shared_k_w, L1_attn_v_coeffs, L1_attn_o_coeffs, L1_attn_decay_logits, L1_attn_out_scale, L1_ffn_gate_w, L1_ffn_gate_b, L1_ffn_w1, L1_ffn_b1, L1_ffn_w2, L1_ffn_b2):
    import jax
    import jax.numpy as jnp

    def _L0_tok_ref(x, conv_w, conv_b, cls_token, pos_embed, ln1_w, ln1_b, qkv_w, qkv_b, proj_w, proj_b, ln2_w, ln2_b, fc1_w, fc1_b, fc2_w, fc2_b, norm_w, norm_b):
        import jax, jax.numpy as jnp
        import numpy as np
        DEPTH = 4
        HEADS = 8
        DIM = 128
        HID = 256
        P = 16
        IMG = 224
        GRID = IMG // P
        NPATCH = GRID * GRID
        NTOK = NPATCH + 1
        BATCH = 64
        EPS = 1e-05

        def layernorm(x, w, b):
            mu = jnp.mean(x, axis=-1, keepdims=True)
            var = jnp.mean(jnp.square(x - mu), axis=-1, keepdims=True)
            return (x - mu) * jax.lax.rsqrt(var + EPS) * w + b
        B = x.shape[0]
        hd = DIM // HEADS
        scale = hd ** (-0.5)
        patches = x.reshape(B, 3, GRID, P, GRID, P)
        patches = patches.transpose(0, 2, 4, 1, 3, 5).reshape(B, NPATCH, 3 * P * P)
        tok = patches @ conv_w + conv_b
        cls = jnp.broadcast_to(cls_token, (B, 1, DIM))
        h = jnp.concatenate([cls, tok], axis=1) + pos_embed
        for i in range(DEPTH):
            y = layernorm(h, ln1_w[i], ln1_b[i])
            qkv = (y @ qkv_w[i] + qkv_b[i]).reshape(B, NTOK, 3, HEADS, hd)
            qkv = qkv.transpose(2, 0, 3, 1, 4)
            q, k, v = (qkv[0], qkv[1], qkv[2])
            attn = jax.nn.softmax(jnp.einsum('bhnd,bhmd->bhnm', q, k) * scale, axis=-1)
            o = jnp.einsum('bhnm,bhmd->bhnd', attn, v)
            o = o.transpose(0, 2, 1, 3).reshape(B, NTOK, DIM)
            h = h + (o @ proj_w[i] + proj_b[i])
            y = layernorm(h, ln2_w[i], ln2_b[i])
            y = jax.nn.gelu(y @ fc1_w[i] + fc1_b[i], approximate=False)
            h = h + (y @ fc2_w[i] + fc2_b[i])
        return layernorm(h, norm_w, norm_b)

    def _L0_attn_ref(x, Wq, Wk, Wv):
        import jax, jax.numpy as jnp
        import numpy as np
        GAMMA = 0.96
        B, S, _ = x.shape
        d_out = Wq.shape[1]
        q = x @ Wq
        k = x @ Wk
        v = x @ Wv
        scores = jnp.einsum('bqd,bkd->bqk', q, k) / jnp.sqrt(jnp.float32(d_out))
        i = jnp.arange(S)[:, None]
        j = jnp.arange(S)[None, :]
        powers = (i - j).astype(jnp.float32)
        log_mask = jnp.where(powers >= 0, powers * jnp.log(jnp.float32(GAMMA)), -jnp.inf)
        scores = scores + log_mask[None, :, :]
        attn = jax.nn.softmax(scores, axis=-1)
        return jnp.einsum('bqk,bkd->bqd', attn, v)

    def _L0_ffn_ref(x, Wg, W1, b1, W2, b2, ln_g, ln_b, out_g, out_b):
        import jax, jax.numpy as jnp
        import numpy as np
        EPS = 1e-05
        TOP_K = 2

        def layer_norm(x, g, b):
            m = x.mean(-1, keepdims=True)
            v = ((x - m) ** 2).mean(-1, keepdims=True)
            return (x - m) / jnp.sqrt(v + EPS) * g + b
        xn = layer_norm(x, ln_g, ln_b)
        logits = jnp.einsum('bsd,de->bse', xn, Wg)
        probs = jax.nn.softmax(logits, axis=-1)
        top_p, top_i = jax.lax.top_k(probs, TOP_K)
        conf = top_p / top_p.sum(-1, keepdims=True)
        h = jax.nn.gelu(jnp.einsum('bsd,edh->bseh', xn, W1) + b1)
        o = jnp.einsum('bseh,ehd->bsed', h, W2) + b2
        sel = jnp.take_along_axis(o, top_i[..., None], axis=2)
        combined = jnp.einsum('bskd,bsk->bsd', sel, conf)
        return layer_norm(x + combined, out_g, out_b)

    def _L1_attn_ref(x, basis, shared_q_w, shared_k_w, v_coeffs, o_coeffs, decay_logits, out_scale):
        import jax, jax.numpy as jnp
        import numpy as np
        EPS = 1e-12

        def _l2norm(x):
            n = jnp.sqrt(jnp.sum(x * x, axis=-1, keepdims=True))
            return x / jnp.maximum(n, EPS)
        B, T, V = x.shape
        H = decay_logits.shape[0]
        C = shared_q_w.shape[1]
        D = C // H
        v_w = basis @ v_coeffs.T
        o_w = basis @ o_coeffs.T
        q = _l2norm(x @ shared_q_w)
        k = _l2norm(x @ shared_k_w)
        v = x @ v_w
        q = q.reshape(B, T, H, D).transpose(0, 2, 1, 3)
        k = k.reshape(B, T, H, D).transpose(0, 2, 1, 3)
        v = v.reshape(B, T, H, D).transpose(0, 2, 1, 3)
        scores = jnp.einsum('bhqd,bhkd->bhqk', q, k)
        decay = jax.nn.sigmoid(decay_logits)
        pos = jnp.arange(T)
        diff = pos[None, :] - pos[:, None]
        mask = (diff > 0).astype(scores.dtype)
        expo = jnp.clip(diff.astype(jnp.float32) - 1.0, 0.0, None)
        decay_w = decay[:, None, None] ** expo[None] * mask[None]
        scores = scores * decay_w[None].astype(scores.dtype)
        retrieved = jnp.einsum('bhqk,bhkd->bhqd', scores, v)
        retrieved = retrieved.transpose(0, 2, 1, 3).reshape(B, T, C)
        return retrieved @ o_w.T * out_scale

    def _L1_ffn_ref(x, gate_w, gate_b, w1, b1, w2, b2):
        import jax, jax.numpy as jnp
        import numpy as np
        B, S, H, E, K = (8, 1024, 128, 8, 2)
        logits = jnp.einsum('bsh,he->bse', x, gate_w) + gate_b
        topk_vals, topk_idx = jax.lax.top_k(logits, K)
        topk_weights = jax.nn.softmax(topk_vals, axis=-1)
        mask = jax.nn.one_hot(topk_idx, E, dtype=topk_weights.dtype)
        weights = jnp.einsum('bske,bsk->bse', mask, topk_weights)
        h = jax.nn.relu(jnp.einsum('bsh,ehf->bsef', x, w1) + b1)
        expert_out = jnp.einsum('bsef,efh->bseh', h, w2) + b2
        return jnp.einsum('bseh,bse->bsh', expert_out, weights)
    h = _L0_tok_ref(x, L0_tok_conv_w, L0_tok_conv_b, L0_tok_cls_token, L0_tok_pos_embed, L0_tok_ln1_w, L0_tok_ln1_b, L0_tok_qkv_w, L0_tok_qkv_b, L0_tok_proj_w, L0_tok_proj_b, L0_tok_ln2_w, L0_tok_ln2_b, L0_tok_fc1_w, L0_tok_fc1_b, L0_tok_fc2_w, L0_tok_fc2_b, L0_tok_norm_w, L0_tok_norm_b)
    h = jnp.concatenate([jnp.broadcast_to(cls_tok, (h.shape[0], 1, h.shape[2])), h], axis=1)
    h = h + _L0_attn_ref(_layernorm(h, axis=-1), L0_attn_Wq, L0_attn_Wk, L0_attn_Wv)
    h = h + _L0_ffn_ref(_layernorm(h, axis=-1), L0_ffn_Wg, L0_ffn_W1, L0_ffn_b1, L0_ffn_W2, L0_ffn_b2, L0_ffn_ln_g, L0_ffn_ln_b, L0_ffn_out_g, L0_ffn_out_b)
    h = h + _L1_attn_ref(_layernorm(h, axis=-1), L1_attn_basis, L1_attn_shared_q_w, L1_attn_shared_k_w, L1_attn_v_coeffs, L1_attn_o_coeffs, L1_attn_decay_logits, L1_attn_out_scale)
    h = h + _L1_ffn_ref(_layernorm(h, axis=-1), L1_ffn_gate_w, L1_ffn_gate_b, L1_ffn_w1, L1_ffn_b1, L1_ffn_w2, L1_ffn_b2)
    return h

_drawn_inputs = setup_inputs


def setup_inputs(seed=0):
    import zlib

    import numpy as np

    out = dict(_drawn_inputs(seed))
    spreads = {'L0_tok_conv_b': (0.0, 0.1),
     'L0_tok_ln1_w': (1.0, 0.6),
     'L0_tok_ln1_b': (0.0, 0.339),
     'L0_tok_qkv_b': (0.0, 0.1),
     'L0_tok_proj_b': (0.0, 0.1),
     'L0_tok_ln2_w': (1.0, 0.573),
     'L0_tok_ln2_b': (0.0, 0.432),
     'L0_tok_fc1_b': (0.0, 0.1),
     'L0_tok_fc2_b': (0.0, 0.1),
     'L0_tok_norm_w': (1.0, 0.2),
     'L0_tok_norm_b': (0.0, 0.1),
     'L0_ffn_b1': (0.0, 0.8),
     'L0_ffn_b2': (0.0, 0.1),
     'L0_ffn_ln_g': (1.0, 0.6),
     'L0_ffn_ln_b': (0.0, 0.538),
     'L0_ffn_out_g': (1.0, 0.2),
     'L0_ffn_out_b': (0.0, 0.1)}
    factors = {'L0_tok_cls_token': 8.0,
     'L0_ffn_W1': 2.759,
     'L1_ffn_gate_b': 3.225,
     'L1_ffn_b1': 8.0,
     'L1_ffn_b2': 4.892}
    for name, (base, spread) in spreads.items():
        noise = np.random.default_rng([zlib.crc32(name.encode()), seed]).standard_normal(out[name].shape)
        drawn = base * np.exp(spread * noise) if base else spread * noise
        out[name] = jnp.asarray(drawn.astype(out[name].dtype))
    for name, factor in factors.items():
        out[name] = (out[name] * factor).astype(out[name].dtype)
    return out
```

```python
from contextlib import ExitStack
from math import log, sqrt

import concourse.bass as bass
import numpy as np
from concourse import mybir

F32, BF16, U32 = mybir.dt.float32, mybir.dt.bfloat16, mybir.dt.uint32
ALU = mybir.AluOpType
ACT = mybir.ActivationFunctionType
X = mybir.AxisListType.X

BATCH, CH, IMG, PATCH, D = 64, 3, 224, 16, 128
GRID = IMG // PATCH
DEPTH, HEADS, HD, MLP = 4, 8, 16, 256
TOK = GRID * GRID + 2
TT = TOK // 2
NB = 2
NG = 2
NC = NB * TOK
U = 2 * NB
ITERS = BATCH // (NB * NG)
E = 8
F0, F1 = 512 // D, 256 // D
HALF = PATCH // 2
XW = IMG - HALF
CK = 2 * CH * PATCH
EPS = 1e-5
TINY = 1e-24
LIFT = 2.0 ** 20
RING = 6
LH = 4
TW = 3 * TT

VEC = {}
_at = 0
for _n, _w in (("conv_b", 1), ("cls_in", 1), ("cls_out", 1), ("norm_w", 1), ("norm_b", 1), ("ln1_w", DEPTH),
               ("ln1_b", DEPTH), ("ln2_w", DEPTH), ("ln2_b", DEPTH), ("proj_b", DEPTH), ("fc2_b", DEPTH),
               ("fc1_b", 2 * DEPTH), ("qk_b", 4 * DEPTH), ("v_b", 2 * DEPTH), ("ln_g", 1), ("ln_b", 1),
               ("out_g", 1), ("out_b", 1), ("m0_b1", E * F0), ("m0_b2", E), ("m1_b1", E * F1), ("m1_b2", E),
               ("out_scale", 1)):
    VEC[_n] = (_at, _w)
    _at += _w
NV = _at


def constants():
    p = np.arange(TT)[:, None]
    n = np.arange(TOK)[None, :]
    lg = log(0.96)
    c = {}
    c["ident"] = np.eye(D, dtype=np.float32)
    c["center"] = np.eye(D, dtype=np.float32) - np.float32(1.0 / D)
    c["mean"] = np.full((D, D), 1.0 / D, np.float32)
    c["ones"] = np.ones((D, D), np.float32)
    k = np.arange(D)
    c["headsum"] = ((k[:, None] % 32 == 16) & (k[:, None] // 32 == k[None, :] // 32)).astype(np.float32)
    c["expert"] = np.stack([np.repeat(((k % 32 == e) & (k < 96))[:, None], D, 1) for e in range(E)], 1).astype(np.float32)
    c["mask_qk"] = np.stack([np.where(n > p + TT * t, -1e30, -n * lg * sqrt(D)) for t in range(2)], 1).astype(np.float32)
    c["mask_kq"] = np.stack([np.where(n < p + TT * t, -1e30, 0.0 * n) for t in range(2)], 1).astype(np.float32)
    c["key_decay"] = np.concatenate([-(p + TT * t) * lg for t in range(2)], 1).astype(np.float32)
    diff = p - (np.arange(TW)[None, :] - TT)
    c["steps"] = np.maximum(diff - 1, 0).astype(np.float32)
    c["future"] = (diff > 0).astype(np.float32)
    c["iota"] = np.broadcast_to(np.arange(E, dtype=np.float32), (TT, E)).copy()
    return c


class Group:
    pass


def schedule():
    steps = [("conv", 0)]
    for l in range(DEPTH):
        steps += [("ln_h", l), ("qkv", l), ("smax", l), ("sexp", l), ("norm", l), ("proj", l), ("ln_h", l), ("mlp", l)]
    steps += [("ln_h", 0), ("tower_out", 0), ("ln_full", 0), ("retention", 0), ("ln_full", 1), ("ln_z", 0), ("moe", 0),
              ("moe0_out", 0), ("ln_full", 2), ("linear", 0), ("ln_full", 3), ("moe", 1), ("moe1_out", 0)]
    return steps


def signals(kind, n):
    ln = {"sq": 1, "stat_psum": 1, "log": 1, "rstd": 1, "z": 1}
    ft = F0 if n == 0 else F1
    return {
        "conv": {"conv_psum": NB, "h": NB + 1, "zeroed": 1},
        "ln_h": ln,
        "ln_z": ln,
        "ln_full": ln | {"cen_psum": 1, "cen": 1},
        "qkv": {"qk_psum": 4, "q": 2, "q_bf": 2, "k": HEADS, "k_bf": HEADS, "v_psum": 1, "v": 1},
        "smax": {"smax_psum": HEADS, "max": HEADS, "mt_hi": 1, "mt": 1, "mrow_psum": 2, "q_aug": 2},
        "sexp": {"st_psum": HEADS * NB, "exp": HEADS * NB, "av_psum": 2 * NB},
        "norm": {"o": 2, "sum_psum": 2, "log": 2, "rsum": 2, "o_norm": 2},
        "proj": {"proj_psum": 1, "h": 1},
        "mlp": {"fc1_psum": 2, "hid": 2, "fc2_psum": 1, "h": 1},
        "tower_out": {"affine": 1, "h": 1},
        "retention": {"qk_psum": 2, "q": 2, "q_bf": 2, "v_psum": 1, "v": 1, "smax_psum": NB, "max": NB, "mt_hi": 1,
                      "mt": 1, "st_psum": NB, "exp": NB, "av_psum": 1, "sum_psum": 1, "log": 1, "rsum": 1,
                      "o_norm": 1, "h": 1},
        "linear": {"qk_psum": 2, "sq": 2, "stat_psum": 2, "floor": 2, "log": 2, "rstd": 2, "q": 1, "k": LH,
                   "v_psum": 1, "v": 1, "st_psum": LH * NB, "decayed": LH * NB, "av_psum": NB, "o": 1, "proj_psum": 1,
                   "h": 1},
        "moe": {"gate_psum": 1, "logit": 1, "top": U, "topi": U, "gap": 1, "egap": 1, "g": 9, "mid": 1, "parts": 1,
                "gateT_psum": 1, "gateT": 1, "up_psum": E * (ft + 1), "up_read": E * (ft + 1), "down": E * ft,
                "term": E, "acc": E - 1},
        "moe0_out": {"s": 1, "sq": 1, "stat_psum": 1, "log": 1, "rstd": 1, "z": 1, "affine": 1, "h": 1},
        "moe1_out": {"h": 1, "out_psum": 1, "out_sb": 1},
    }[kind]


def counted():
    at, table = {}, []
    for kind, n in schedule():
        table.append((kind, n, dict(at)))
        for name, k in signals(kind, n).items():
            at[name] = at.get(name, 0) + k
    return table, sorted(at)


def tower_kernel(nc, x, conv_w, pos_t, vecs, w_qk, w_v, w_v_pad, w_p, w_fc1, w_fc2, w_ret, w_lin, coef, gates, gate_b,
                 decay_logits, m0_w1, m0_w2, m1_w1, m1_w2, consts, out):
    TABLE, NAMES = counted()
    ORDER = [(g, *step) for step in TABLE for g in range(NG)]

    with ExitStack() as ctx:
        def sb(name, shape, dt=F32):
            return ctx.enter_context(nc.sbuf_tensor(name, shape, dt))

        def sem(name):
            return ctx.enter_context(nc.semaphore(name))

        cw = sb("cw", [CK, HALF, D])
        vec = sb("vec", [D, NV])
        wqk = sb("wqk", [D, DEPTH, 4, D])
        wv = sb("wv", [D, DEPTH, D])
        wp = sb("wp", [D, DEPTH, 2, D])
        fc1 = sb("fc1", [D, DEPTH, MLP])
        fc2 = sb("fc2", [D, DEPTH, 2, D])
        wret = sb("wret", [D, 3, D])
        wlin = sb("wlin", [D, 2, D])
        wvb = sb("wvb", [D, D])
        wob = sb("wob", [D, D])
        wg = sb("wg", [D, 2, E])
        gb = sb("gb", [TT, 2, E])
        w1 = [sb("w1_0", [D, E * F0, D]), sb("w1_1", [D, E * F1, D])]
        w2 = [sb("w2_0", [D, E * F0, D]), sb("w2_1", [D, E * F1, D])]
        posb = sb("posb", [D, TOK])
        ident = sb("ident", [D, D])
        identb = sb("identb", [D, D], BF16)
        center = sb("center", [D, D])
        meanm = sb("meanm", [D, D])
        ones = sb("ones", [D, D])
        headsum = sb("headsum", [D, D])
        expertb = sb("expertb", [D, E, D], BF16)
        mask_qk = sb("mask_qk", [TT, 2, TOK], BF16)
        mask_kq = sb("mask_kq", [TT, 2, TOK], BF16)
        key_decay = sb("key_decay", [TT, 2])
        decay = sb("decay", [TT, LH, TW])
        iota = sb("iota", [TT, E])
        eps = sb("eps", [D, 2])
        row99 = sb("row99", [D, 16])

        def v(name, k=0, n=1):
            return vec[:, VEC[name][0] + k:VEC[name][0] + k + n]

        KW, PW = HEADS * NC, RING * 2 * TOK
        ARENA = KW + PW + 2 * NC
        groups = []
        for g in range(NG):
            G = Group()
            groups.append(G)
            t = "AB"[g]
            G.arena = sb(f"arena{t}", [D, ARENA])
            G.k = G.arena[:, 0:KW].rearrange("p (h n) -> p h n", h=HEADS)
            G.p = G.arena[:, KW:KW + PW].rearrange("p (s n) -> p s n", s=RING)
            G.o = G.arena[:, KW + PW:ARENA].rearrange("p (g n) -> p g n", g=2)
            assert NB * GRID * XW <= ARENA
            G.x = G.arena[:, 0:NB * GRID * XW].rearrange("p (b y w) -> p b y w", b=NB, y=GRID)
            G.k_bf = sb(f"k_bf{t}", [D, HEADS, NC], BF16)
            G.q = sb(f"q{t}", [D, 2, NC])
            G.cb = G.q
            G.q_bf = sb(f"q_bf{t}", [D, 2, NC], BF16)
            G.acc = G.q_bf[:, :, :].rearrange("p g n -> p (g n)").bitcast(F32)
            G.h = sb(f"h{t}", [D, NC])
            G.z = sb(f"z{t}", [D, NC])
            G.u = sb(f"u{t}", [D, NC])
            G.sq = sb(f"sq{t}", [D, NC])
            G.va = sb(f"va{t}", [TT, U, HEADS, 32])
            G.hid = sb(f"hid{t}", [D, 4, NC])
            hflat = G.hid[:, :, :].rearrange("p f n -> p (f n)")
            G.vr = hflat[0:TT, 0:U * D].rearrange("p (u d) -> p u d", u=U)
            G.ob = hflat[0:TT, U * D:2 * U * D].rearrange("p (u d) -> p u d", u=U)
            G.negm = sb(f"negm{t}", [TT, HEADS, NB, 2])
            G.mt = sb(f"mt{t}", [TT, U, 2, D], BF16)
            G.lg = sb(f"lg{t}", [TT, 7, U, E])
            G.ix = sb(f"ix{t}", [TT, U, E], U32)
            G.sc = sb(f"sc{t}", [TT, 5, U, 2])
            G.cc = sb(f"cc{t}", [TT, U, D], BF16)
            G.ct = sb(f"ct{t}", [D, NC], BF16)
            G.ps = ctx.enter_context(nc.psum_tensor(f"ps{t}", [D, 4, 512], F32))
            G.x_in = sem(f"x_in_{t}")
            G.s = {n: sem(f"{n}_{t}") for n in NAMES}
            G.out_done = sem(f"out_done_{t}")
            assert G.out_done.num - G.x_in.num == len(NAMES) + 1
        s_load, s_fold, s_ps, s_const = sem("load"), sem("fold"), sem("fold_psum"), sem("const")

        def load_images(eng, G, g, i):
            for b in range(NB):
                for half in range(2):
                    for c in range(CH):
                        p = (half * CH + c) * PATCH
                        src = x[i * (NB * NG) + g * NB + b, c].rearrange("(y r) w -> r y w", r=PATCH)
                        eng.dma_start(G.x[p:p + PATCH, b], src[:, :, half * HALF:half * HALF + XW]).then_inc(G.x_in, 16)

        XWAIT = NB * 2 * CH * 16

        st_expert = groups[1].arena[:, 0:E * D].rearrange("p (e d) -> p e d", e=E)
        st_mqk = groups[1].arena[0:TT, 1024:1024 + 2 * TOK].rearrange("p (t n) -> p t n", t=2)
        st_mkq = groups[1].arena[0:TT, 1424:1424 + 2 * TOK].rearrange("p (t n) -> p t n", t=2)
        st_pos = groups[1].arena[:, 1824:1824 + TOK]
        st_steps = groups[1].arena[0:TT, 2024:2024 + TW]
        st_future = groups[1].arena[0:TT, 2324:2324 + TW]
        st_wvp = groups[1].arena[:, 2624:2624 + DEPTH * 2 * D].rearrange("p (l g d) -> p l g d", l=DEPTH, g=2)
        st_coef = groups[1].arena[:, 3648:3648 + 3 * D].rearrange("p (c d) -> p c d", c=3)
        st_mean = groups[1].arena[:, 4032:4032 + 64]
        st_dl = groups[1].arena[0:TT, 4096:4096 + 3 * LH].rearrange("p (k h) -> p k h", k=3)
        st_vb = groups[1].arena[:, 4112:4112 + 2 * DEPTH]
        psA, psB = groups[0].ps, groups[1].ps

        with nc.Block() as block:
            @block.sync
            def _(sp):
                n = 0
                for half in range(2):
                    src = conv_w.rearrange("(k h j) d -> h k j d", h=2, j=HALF)[half]
                    sp.dma_start(cw[half * CK // 2:(half + 1) * CK // 2], src).then_inc(s_load, 16)
                for dst, src in ((vec[:, :], vecs), (wqk[:, :, :, :], w_qk), (wv[:, :, :], w_v), (st_wvp, w_v_pad),
                                 (wp[:, :, :, :], w_p), (fc1[:, :, :], w_fc1), (fc2[:, :, :, :], w_fc2),
                                 (wret[:, :, :], w_ret), (wlin[:, :, :], w_lin), (st_coef, coef), (wg[:, :, :], gates),
                                 (gb[:, 1, :], gate_b), (st_dl[:, 0], decay_logits),
                                 (w1[0][:, :, :], m0_w1), (w2[0][:, :, :], m0_w2), (w1[1][:, :, :], m1_w1),
                                 (w2[1][:, :, :], m1_w2), (ident[:, :], consts["ident"]),
                                 (center[:, :], consts["center"]), (meanm[:, :], consts["mean"]),
                                 (ones[:, :], consts["ones"]), (headsum[:, :], consts["headsum"]),
                                 (st_expert, consts["expert"]), (st_mqk, consts["mask_qk"]),
                                 (st_mkq, consts["mask_kq"]), (key_decay[:, :], consts["key_decay"]),
                                 (st_steps, consts["steps"]), (st_future, consts["future"]),
                                 (iota[:, :], consts["iota"]), (st_pos[:, 1:TOK], pos_t)):
                    sp.dma_start(dst, src).then_inc(s_load, 16)
                    n += 1
                load_images(sp, groups[0], 0, 0)
                sp.wait_ge(s_load, 16 * (n + 2))
                sp.wait_ge(groups[0].x_in, XWAIT)

            @block.gpsimd
            def _(pool):
                for G in groups:
                    pool.memset(G.k_bf[:, :, :], 0.0)
                    pool.memset(G.va[:, :, :, :], 0.0)
                    pool.memset(G.mt[:, :, :, :], 0.0)
                    pool.memset(G.cc[:, :, :], 0.0)
                pool.memset(eps[:, 0:1], EPS)
                pool.memset(eps[:, 1:2], 0.5 * log(LIFT)).then_inc(s_const, 1)
                pool.wait_ge(s_const, 1)

        with nc.Block() as block:
            @block.vector
            def _(dve):
                for G in groups:
                    dve.memset(G.va[:, :, :, HD:HD + 1], 1.0).then_inc(s_const, 1)
                dve.wait_ge(s_const, 3)
                for G in groups:
                    for b in range(NB):
                        dve.memset(G.va[0:1, 2 * b, :, :], 0.0)
                dve.tensor_copy(identb[:, :], ident[:, :])
                dve.tensor_copy(expertb[:, :, :], st_expert)
                dve.tensor_copy(mask_qk[:, :, :], st_mqk)
                dve.tensor_copy(mask_kq[:, :, :], st_mkq)
                for w, n, at in ((cw[:, :, :], HALF, 0), (wp[:, :, :, :].rearrange("p l g d -> p (l g) d"), 2 * DEPTH, 8),
                                 (fc2[:, :, :, :].rearrange("p l g d -> p (l g) d"), 2 * DEPTH, 16),
                                 (w2[0][:, :, :], E * F0, 24)):
                    k = w.shape[0]
                    dve.tensor_reduce(st_mean[0:k, at:at + n], w, X, ALU.add).then_inc(s_fold, 1)
                dve.wait_ge(s_fold, 4)
                dve.tensor_scalar(st_mean[:, 8:56], st_mean[:, 8:56], 1.0 / D, None, ALU.mult)
                dve.tensor_scalar(st_mean[0:CK, 0:8], st_mean[0:CK, 0:8], 1.0 / D, None, ALU.mult).then_inc(s_fold, 1)
                dve.wait_ge(s_fold, 5)
                for w, n, at in ((cw[:, :, :], HALF, 0), (wp[:, :, :, :].rearrange("p l g d -> p (l g) d"), 2 * DEPTH, 8),
                                 (fc2[:, :, :, :].rearrange("p l g d -> p (l g) d"), 2 * DEPTH, 16),
                                 (w2[0][:, :, :], E * F0, 24)):
                    k = w.shape[0]
                    dve.tensor_tensor(w, w, st_mean[0:k, at:at + n].unsqueeze(2).to_broadcast([k, n, D]), ALU.subtract)
                dve.tensor_scalar(st_pos[:, 2:TOK], st_pos[:, 2:TOK], v("conv_b"), None, ALU.add)
                dve.tensor_tensor(st_pos[:, 1:2], st_pos[:, 1:2], v("cls_in"), ALU.add)
                dve.memset(st_pos[:, 0:1], 0.0).then_inc(s_fold, 1)
                dve.wait_ge(s_fold, 6)

            @block.scalar
            def _(act):
                act.preload_act_table_set("natural_log_exp_and_others")
                act.activation(st_dl[:, 1], st_dl[:, 0], ACT.Exp, scale=-1.0).then_inc(s_ps, 1)
                act.wait_ge(s_ps, 1)
                act.activation(st_dl[:, 2], st_dl[:, 1], ACT.Ln, bias=ones[0:TT, 0:1]).then_inc(s_ps, 1)
                act.wait_ge(s_ps, 2)
                act.activation(st_dl[:, 1], st_dl[:, 2], ACT.Copy, scale=-1.0).then_inc(s_ps, 1)
                act.wait_ge(s_ps, 3)
                for h in range(LH):
                    act.activation(decay[:, h, :], st_steps, ACT.Exp, scale=st_dl[:, 1, h:h + 1]).then_inc(s_ps, 1)
                act.wait_ge(s_ps, 3 + LH)

        with nc.Block() as block:
            @block.tensor
            def _(pe):
                col = 0
                for l in range(DEPTH):
                    for g in range(4):
                        pe.matmul(psA[:, 0, col:col + 1], wqk[:, l, g, :], v("ln1_b", l), start=True, stop=True)
                        col += 1
                for l in range(DEPTH):
                    for g in range(2):
                        pe.matmul(psA[:, 0, col:col + 1], st_wvp[:, l, g, :], v("ln1_b", l), start=True, stop=True)
                        col += 1
                for l in range(DEPTH):
                    for f in range(2):
                        pe.matmul(psA[:, 0, col:col + 1], fc1[:, l, f * D:(f + 1) * D], v("ln2_b", l), start=True, stop=True)
                        col += 1
                for f in range(E * F0):
                    pe.matmul(psA[:, 0, col:col + 1], w1[0][:, f, :], v("ln_b"), start=True, stop=True)
                    col += 1
                pe.matmul(psA[:, 1, 0:TOK], center[:, :], st_pos, start=True, stop=True)
                pe.matmul(psA[0:TT, 2, 0:E], v("ln_b").to_broadcast([D, TT]), wg[:, 0, :], start=True, stop=True)
                pe.matmul(psA[:, 3, 0:E], center[:, :], v("m0_b2", 0, E), start=True, stop=True)
                pe.matmul(psB[:, 0, 0:DEPTH], center[:, :], v("fc2_b", 0, DEPTH), start=True, stop=True)
                pe.matmul(psB[:, 1, 0:D], st_coef[:, 0, :], st_coef[:, 1, :], start=True, stop=True)
                pe.matmul(psB[:, 2, 0:D], st_coef[:, 2, :], st_coef[:, 0, :], start=True, stop=True).then_inc(s_ps, 1)
                pe.wait_ge(s_ps, 4 + LH)

            @block.vector
            def _(dve):
                for h in range(LH):
                    last = dve.tensor_tensor(decay[:, h, :], decay[:, h, :], st_future, ALU.mult)
                last.then_inc(s_fold, 1)
                dve.wait_ge(s_fold, 7)

        with nc.Block() as block:
            @block.vector
            def _(dve):
                n = 4 * DEPTH
                dve.tensor_tensor(v("qk_b", 0, n), v("qk_b", 0, n), psA[:, 0, 0:n], ALU.add)
                dve.tensor_tensor(st_vb, v("v_b", 0, 2 * DEPTH), psA[:, 0, n:n + 2 * DEPTH], ALU.add)
                n += 2 * DEPTH
                dve.tensor_tensor(v("fc1_b", 0, 2 * DEPTH), v("fc1_b", 0, 2 * DEPTH), psA[:, 0, n:n + 2 * DEPTH], ALU.add)
                n += 2 * DEPTH
                dve.tensor_tensor(v("m0_b1", 0, E * F0), v("m0_b1", 0, E * F0), psA[:, 0, n:n + E * F0], ALU.add)
                dve.tensor_copy(posb[:, :], psA[:, 1, 0:TOK])
                dve.tensor_copy(gb[:, 0, :], psA[0:TT, 2, 0:E])
                dve.tensor_copy(v("m0_b2", 0, E), psA[:, 3, 0:E])
                dve.tensor_copy(v("fc2_b", 0, DEPTH), psB[:, 0, 0:DEPTH])
                dve.tensor_copy(wvb[:, :], psB[:, 1, 0:D])
                dve.tensor_scalar(wob[:, :], psB[:, 2, 0:D], v("out_scale"), None, ALU.mult)
                for l in range(DEPTH):
                    dve.tensor_scalar(wqk[:, l, :, :], wqk[:, l, :, :], v("ln1_w", l), None, ALU.mult)
                    dve.tensor_scalar(wv[:, l, :], wv[:, l, :], v("ln1_w", l), None, ALU.mult)
                    dve.tensor_scalar(fc1[:, l, :], fc1[:, l, :], v("ln2_w", l), None, ALU.mult)
                dve.tensor_scalar(wg[:, 0, :], wg[:, 0, :], v("ln_g"), None, ALU.mult)
                dve.tensor_scalar(w1[0][:, :, :], w1[0][:, :, :], v("ln_g"), None, ALU.mult).then_inc(s_fold, 1)
                dve.wait_ge(s_fold, 8)

        with nc.Block() as block:
            @block.tensor
            def _(pe):
                for l in range(DEPTH):
                    o = psA[:, 0, l:l + 1]
                    pe.matmul(o, wp[:, l, 0, :], st_vb[:, 2 * l:2 * l + 1], start=True, stop=False)
                    pe.matmul(o, wp[:, l, 1, :], st_vb[:, 2 * l + 1:2 * l + 2], start=False, stop=False)
                    last = pe.matmul(o, center[:, :], v("proj_b", l), start=False, stop=True)
                last.then_inc(s_ps, 1)
                pe.wait_ge(s_ps, 5 + LH)

        with nc.Block() as block:
            @block.vector
            def _(dve):
                dve.tensor_copy(v("proj_b", 0, DEPTH), psA[:, 0, 0:DEPTH]).then_inc(s_fold, 1)
                dve.wait_ge(s_fold, 9)

            @block.sync
            def _(sp):
                load_images(sp, groups[1], 1, 0)
                sp.wait_ge(groups[1].x_in, XWAIT)

        with nc.Block() as block:
            @block.gpsimd
            def _(pool):
                for G in groups:
                    pool.sem_clear(G.x_in)

        def wait(eng, sem_, count):
            if count > 0:
                eng.wait_ge(sem_, count)

        def real(ap):
            return ap.rearrange("p (b n) -> p b n", b=NB)[:, :, 1:TOK]

        def bank(G, k):
            return G.ps[:, k, 0:NC]

        with nc.Fori(0, ITERS) as it:
            with nc.Block() as block:
                @block.tensor
                def _(pe):
                    def stat(G, at, c):
                        pe.wait_ge(G.s["sq"], at["sq"] + 1)
                        pe.matmul(bank(G, 0), meanm[:, :], G.sq[:, :], start=True, stop=True).then_inc(G.s["stat_psum"], 1)

                    def st_unit(G, at, l, k):
                        grp, rest = divmod(k, 4 * NB)
                        b, j = divmod(rest, 4)
                        h = 4 * grp + j
                        if k >= 2:
                            pe.wait_ge(G.s["exp"], at["exp"] + k - 1)
                        for kt in range(2):
                            mm = pe.matmul(G.ps[0:TT, k % 2, kt * TOK:(kt + 1) * TOK],
                                           G.k[:, h, b * TOK + kt * TT:b * TOK + (kt + 1) * TT],
                                           G.q[:, grp, b * TOK:(b + 1) * TOK], start=True, stop=True)
                        mm.then_inc(G.s["st_psum"], 1)

                    def av_set(G, at, s):
                        grp, b = divmod(s, NB)
                        pe.wait_ge(G.s["exp"], at["exp"] + 4 * s + 4)
                        for kt in range(2):
                            for j in range(4):
                                mm = pe.matmul(G.ps[32 * j:32 * j + 32, 2 + grp, b * TOK:(b + 1) * TOK],
                                               G.va[:, 2 * b + kt, 4 * grp + j, :],
                                               G.p[0:TT, (4 * s + j) % RING, kt * TOK:(kt + 1) * TOK],
                                               start=(kt == 0), stop=(kt == 1))
                        mm.then_inc(G.s["av_psum"], 1)

                    for g, kind, n, at in ORDER:
                        G, S = groups[g], groups[g].s
                        at = {name: at.get(name, 0) for name in NAMES}
                        if kind == "conv":
                            for b in range(NB):
                                for j in range(HALF):
                                    mm = pe.matmul(G.ps[:, b, 0:GRID * GRID], cw[:, j, :],
                                                   G.x[0:CK, b, :, j:j + PATCH * (GRID - 1) + 1:PATCH],
                                                   start=(j == 0), stop=(j == HALF - 1))
                                mm.then_inc(S["conv_psum"], 1)
                        elif kind in ("ln_h", "ln_z"):
                            stat(G, at, 0)
                        elif kind == "ln_full":
                            pe.wait_ge(S["h"], at["h"])
                            pe.matmul(bank(G, 1), center[:, :], G.h[:, :], start=True, stop=True).then_inc(S["cen_psum"], 1)
                            stat(G, at, 0)
                        elif kind == "qkv":
                            pe.wait_ge(S["z"], at["z"])
                            for k in range(4):
                                pe.matmul(bank(G, k), wqk[:, n, k, :], G.z[:, :], start=True, stop=True)\
                                    .then_inc(S["qk_psum"], 1)
                            pe.wait_ge(S["q"], at["q"] + 1)
                            for u in range(U):
                                mm = pe.matmul(G.ps[0:TT, 0, u * D:(u + 1) * D], G.z[:, u * TT:(u + 1) * TT], wv[:, n, :],
                                               start=True, stop=True)
                            mm.then_inc(S["v_psum"], 1)
                        elif kind == "smax":
                            pe.wait_ge(S["v"], at["v"])
                            pe.wait_ge(S["k"], at["k"])
                            pe.wait_ge(S["q_bf"], at["q_bf"])
                            for h in range(HEADS):
                                pe.wait_ge(S["k_bf"], at["k_bf"] - HEADS + h + 1)
                                if h * NB >= 4:
                                    pe.wait_ge(S["max"], at["max"] + h - 4 // NB + 1)
                                for b in range(NB):
                                    for qt in range(2):
                                        mm = pe.matmul(G.ps[0:TT, (h * NB + b) % 4, qt * TOK:(qt + 1) * TOK],
                                                       G.q_bf[:, h // 4, b * TOK + qt * TT:b * TOK + (qt + 1) * TT],
                                                       G.k_bf[:, h, b * TOK:(b + 1) * TOK], start=True, stop=True)
                                mm.then_inc(S["smax_psum"], 1)
                            pe.wait_ge(S["mt"], at["mt"] + 1)
                            for grp in range(2):
                                for u in range(U):
                                    mm = pe.matmul(G.ps[:, grp, u * TT:(u + 1) * TT], G.mt[:, u, grp, :],
                                                   identb[0:TT, 0:TT], start=True, stop=True)
                                mm.then_inc(S["mrow_psum"], 1)
                        elif kind == "sexp":
                            pe.wait_ge(S["q_aug"], at["q_aug"])
                            pe.wait_ge(S["v"], at["v"])
                            for k in range(HEADS * NB):
                                st_unit(G, at, n, k)
                                if k >= 5 and k % 4 == 1:
                                    av_set(G, at, (k - 5) // 4)
                            av_set(G, at, 2 * NB - 1)
                        elif kind == "norm":
                            for grp in range(2):
                                pe.wait_ge(S["o"], at["o"] + grp + 1)
                                pe.matmul(bank(G, grp), headsum[:, :], G.o[:, grp, :], start=True, stop=True)\
                                    .then_inc(S["sum_psum"], 1)
                        elif kind == "proj":
                            for grp in range(2):
                                pe.wait_ge(S["o_norm"], at["o_norm"] - 1 + grp)
                                mm = pe.matmul(bank(G, 2), wp[:, n, grp, :], G.o[:, grp, :], start=(grp == 0), stop=(grp == 1))
                            mm.then_inc(S["proj_psum"], 1)
                        elif kind == "mlp":
                            pe.wait_ge(S["z"], at["z"])
                            for f in range(2):
                                pe.matmul(bank(G, f), fc1[:, n, f * D:(f + 1) * D], G.z[:, :], start=True, stop=True)\
                                    .then_inc(S["fc1_psum"], 1)
                            for f in range(2):
                                pe.wait_ge(S["hid"], at["hid"] + f + 1)
                                mm = pe.matmul(bank(G, 2), fc2[:, n, f, :], G.hid[:, f, :], start=(f == 0), stop=(f == 1))
                            mm.then_inc(S["fc2_psum"], 1)
                        elif kind == "retention":
                            pe.wait_ge(S["z"], at["z"])
                            for k in range(2):
                                pe.matmul(bank(G, k), wret[:, k, :], G.z[:, :], start=True, stop=True).then_inc(S["qk_psum"], 1)
                            for u in range(U):
                                mm = pe.matmul(G.ps[0:TT, 2, u * D:(u + 1) * D], G.z[:, u * TT:(u + 1) * TT], wret[:, 2, :],
                                               start=True, stop=True)
                            mm.then_inc(S["v_psum"], 1)
                            pe.wait_ge(S["q_bf"], at["q_bf"] + 2)
                            pe.wait_ge(S["q"], at["q"] + 2)
                            for b in range(NB):
                                for qt in range(2):
                                    o = G.ps[0:TT, b, qt * TOK:(qt + 1) * TOK]
                                    pe.matmul(o, G.q_bf[:, 0, b * TOK + qt * TT:b * TOK + (qt + 1) * TT],
                                              G.q_bf[:, 1, b * TOK:(b + 1) * TOK], start=True, stop=False)
                                    mm = pe.matmul(o, identb[0:TT, 0:TT], mask_qk[:, qt, :], start=False, stop=True)
                                mm.then_inc(S["smax_psum"], 1)
                            pe.wait_ge(S["v"], at["v"] + 1)
                            pe.wait_ge(S["mt"], at["mt"] + 1)
                            for b in range(NB):
                                for kt in range(2):
                                    o = G.ps[0:TT, 2 + b, kt * TOK:(kt + 1) * TOK]
                                    pe.matmul(o, G.q[:, 1, b * TOK + kt * TT:b * TOK + (kt + 1) * TT],
                                              G.q[:, 0, b * TOK:(b + 1) * TOK], start=True, stop=False)
                                    pe.matmul(o, identb[0:TT, 0:TT], mask_kq[:, kt, :], start=False, stop=False)
                                    for qt in range(2):
                                        for part in range(2):
                                            mm = pe.matmul(o[:, qt * TT:(qt + 1) * TT],
                                                           G.mt[:, 2 * b + qt, 0, 16 + part:17 + part].to_broadcast([TT, TT]),
                                                           identb[0:TT, 0:TT], start=False, stop=(qt == 1 and part == 1))
                                mm.then_inc(S["st_psum"], 1)
                            for b in range(NB):
                                pe.wait_ge(S["exp"], at["exp"] + b + 1)
                                for kt in range(2):
                                    mm = pe.matmul(G.ps[:, 0, b * TOK:(b + 1) * TOK], G.vr[:, 2 * b + kt, :],
                                                   G.p[0:TT, b, kt * TOK:(kt + 1) * TOK], start=(kt == 0), stop=(kt == 1))
                            mm.then_inc(S["av_psum"], 1)
                            for b in range(NB):
                                for kt in range(2):
                                    mm = pe.matmul(G.ps[:, 1, b * TOK:(b + 1) * TOK], ones[0:TT, :],
                                                   G.p[0:TT, b, kt * TOK:(kt + 1) * TOK], start=(kt == 0), stop=(kt == 1))
                            mm.then_inc(S["sum_psum"], 1)
                        elif kind == "moe":
                            ft = F0 if n == 0 else F1
                            src = G.u if n == 0 else G.z
                            pe.wait_ge(S["z"], at["z"])
                            for u in range(U):
                                mm = pe.matmul(G.ps[0:TT, 3, u * E:(u + 1) * E], src[:, u * TT:(u + 1) * TT], wg[:, n, :],
                                               start=True, stop=True)
                            mm.then_inc(S["gate_psum"], 1)

                            def down(m):
                                e, f = divmod(m, ft)
                                pe.wait_ge(S["up_read"], at["up_read"] + m + e + 1)
                                if f == 0 and e >= 2:
                                    pe.wait_ge(S["term"], at["term"] + e - 1)
                                pe.matmul(bank(G, 2 + e % 2), w2[n][:, m, :], G.hid[:, m % 4, :], start=(f == 0),
                                          stop=(f == ft - 1)).then_inc(S["down"], 1)

                            r = 0
                            for e in range(E):
                                for f in range(ft):
                                    m = e * ft + f
                                    if r >= 2:
                                        pe.wait_ge(S["up_read"], at["up_read"] + r - 1)
                                    pe.matmul(bank(G, r % 2), w1[n][:, m, :], src[:, :], start=True, stop=True)\
                                        .then_inc(S["up_psum"], 1)
                                    r += 1
                                    if m >= 2:
                                        down(m - 2)
                                    if m == 1:
                                        pe.wait_ge(S["parts"], at["parts"] + 1)
                                        for u in range(U):
                                            mm = pe.matmul(G.ps[:, 3, u * TT:(u + 1) * TT], G.cc[:, u, :],
                                                           identb[0:TT, 0:TT], start=True, stop=True)
                                        mm.then_inc(S["gateT_psum"], 1)
                                        pe.wait_ge(S["gateT"], at["gateT"] + 1)
                                pe.wait_ge(S["up_read"], at["up_read"] + r - 1)
                                pe.matmul(bank(G, r % 2), expertb[:, e, :], G.ct[:, :], start=True, stop=True)\
                                    .then_inc(S["up_psum"], 1)
                                r += 1
                            down(E * ft - 2)
                            down(E * ft - 1)
                        elif kind == "moe0_out":
                            stat(G, at, 0)
                        elif kind == "linear":
                            pe.wait_ge(S["z"], at["z"])
                            for k in range(2):
                                pe.matmul(bank(G, k), wlin[:, k, :], G.z[:, :], start=True, stop=True).then_inc(S["qk_psum"], 1)
                            for u in range(U):
                                mm = pe.matmul(G.ps[0:TT, 2, u * D:(u + 1) * D], G.z[:, u * TT:(u + 1) * TT], wvb[:, :],
                                               start=True, stop=True)
                            mm.then_inc(S["v_psum"], 1)
                            for k in range(2):
                                pe.wait_ge(S["sq"], at["sq"] + k + 1)
                                if k == 1:
                                    pe.wait_ge(S["floor"], at["floor"] + 1)
                                pe.matmul(bank(G, 3), ones[:, :], G.sq[:, :], start=True, stop=True).then_inc(S["stat_psum"], 1)
                            pe.wait_ge(S["q"], at["q"] + 1)
                            pe.wait_ge(S["k"], at["k"] + LH)
                            for k in range(LH * NB):
                                b, h = divmod(k, LH)
                                if k >= 2:
                                    pe.wait_ge(S["decayed"], at["decayed"] + k - 1)
                                for kt in range(2):
                                    mm = pe.matmul(G.ps[0:TT, k % 2, kt * TOK:(kt + 1) * TOK],
                                                   G.k[:, h, b * TOK + kt * TT:b * TOK + (kt + 1) * TT],
                                                   G.q[:, 0, b * TOK:(b + 1) * TOK], start=True, stop=True)
                                mm.then_inc(S["st_psum"], 1)
                                if h == LH - 1:
                                    pe.wait_ge(S["v"], at["v"] + 1)
                                    pe.wait_ge(S["decayed"], at["decayed"] + k + 1)
                                    for kt in range(2):
                                        for j in range(LH):
                                            mm = pe.matmul(G.ps[32 * j:32 * j + 32, 2, b * TOK:(b + 1) * TOK],
                                                           G.vr[:, 2 * b + kt, 32 * j:32 * j + 32],
                                                           G.p[0:TT, j, kt * TOK:(kt + 1) * TOK],
                                                           start=(kt == 0), stop=(kt == 1))
                                    mm.then_inc(S["av_psum"], 1)
                            pe.wait_ge(S["o"], at["o"] + 1)
                            pe.matmul(bank(G, 3), wob[:, :], G.q[:, 1, :], start=True, stop=True).then_inc(S["proj_psum"], 1)
                        elif kind == "moe1_out":
                            pe.wait_ge(S["h"], at["h"] + 1)
                            for u in range(U):
                                mm = pe.transpose(G.ps[0:TT, 0, u * D:(u + 1) * D], G.h[:, u * TT:(u + 1) * TT], ident[:, :])
                            mm.then_inc(S["out_psum"], 1)

                @block.scalar
                def _(act):
                    loaded = None

                    def rstd(G, at, k=0, out=None):
                        act.wait_ge(G.s["stat_psum"], at["stat_psum"] + k + 1)
                        act.activation(bank(G, 0), bank(G, 0), ACT.Ln, bias=eps[:, 0:1]).then_inc(G.s["log"], 1)
                        act.wait_ge(G.s["log"], at["log"] + k + 1)
                        act.activation(bank(G, 0), bank(G, 0), ACT.Exp, scale=-0.5).then_inc(G.s["rstd"], 1)

                    for g, kind, n, at in ORDER:
                        G, S = groups[g], groups[g].s
                        at = {name: at.get(name, 0) for name in NAMES}
                        wants = "gelu" if kind == "mlp" else "lnexp"
                        if wants != loaded and wants == "lnexp":
                            act.preload_act_table_set("natural_log_exp_and_others")
                        loaded = wants
                        if kind == "ln_h":
                            act.wait_ge(S["h"], at["h"])
                            wait(act, S["stat_psum"], at["stat_psum"])
                            act.activation(G.sq[:, :], G.h[:, :], ACT.Square).then_inc(S["sq"], 1)
                            rstd(G, at)
                        elif kind == "ln_z":
                            act.wait_ge(S["z"], at["z"])
                            act.wait_ge(S["stat_psum"], at["stat_psum"])
                            act.activation(G.sq[:, :], G.z[:, :], ACT.Square).then_inc(S["sq"], 1)
                            rstd(G, at)
                        elif kind == "ln_full":
                            act.wait_ge(S["cen_psum"], at["cen_psum"] + 1)
                            act.activation(G.u[:, :], bank(G, 1), ACT.Copy).then_inc(S["cen"], 1)
                            act.activation(G.sq[:, :], bank(G, 1), ACT.Square).then_inc(S["sq"], 1)
                            rstd(G, at)
                        elif kind == "qkv":
                            if n == 0:
                                act.wait_ge(S["zeroed"], 1)
                            for k in range(2):
                                act.wait_ge(S["qk_psum"], at["qk_psum"] + k + 1)
                                act.activation(G.q[:, k, :], bank(G, k), ACT.Identity, bias=v("qk_b", 4 * n + k))\
                                    .then_inc(S["q"], 1)
                            for h in range(HEADS):
                                r = slice(32 * (h % 4), 32 * (h % 4) + 32)
                                act.wait_ge(S["qk_psum"], at["qk_psum"] + 3 + h // 4)
                                act.activation(real(G.k[r, h, :]), real(bank(G, 2 + h // 4)[r]), ACT.Identity,
                                               bias=v("qk_b", 4 * n + 2 + h // 4)[r]).then_inc(S["k"], 1)
                            act.wait_ge(S["v_psum"], at["v_psum"] + 1)
                            act.activation(G.va[:, :, :, 0:HD].rearrange("p u h d -> p (u h) d"),
                                           G.ps[0:TT, 0, 0:U * D].rearrange("p (uh d) -> p uh d", d=HD), ACT.Copy)\
                                .then_inc(S["v"], 1)
                        elif kind == "sexp":
                            for k in range(HEADS * NB):
                                act.wait_ge(S["st_psum"], at["st_psum"] + k + 1)
                                if k >= RING:
                                    act.wait_ge(S["av_psum"], at["av_psum"] + (k - RING) // 4 + 1)
                                act.activation(G.p[0:TT, k % RING, :], G.ps[0:TT, k % 2, 0:2 * TOK], ACT.Exp,
                                               scale=HD ** -0.5).then_inc(S["exp"], 1)
                        elif kind == "norm":
                            for grp in range(2):
                                act.wait_ge(S["av_psum"], at["av_psum"] - 2 * NB + NB * (grp + 1))
                                act.activation(G.o[:, grp, :], bank(G, 2 + grp), ACT.Copy).then_inc(S["o"], 1)
                            for grp in range(2):
                                act.wait_ge(S["sum_psum"], at["sum_psum"] + grp + 1)
                                act.activation(bank(G, grp), bank(G, grp), ACT.Ln).then_inc(S["log"], 1)
                                act.wait_ge(S["log"], at["log"] + grp + 1)
                                act.activation(bank(G, grp), bank(G, grp), ACT.Exp, scale=-1.0).then_inc(S["rsum"], 1)
                        elif kind == "mlp":
                            for f in range(2):
                                act.wait_ge(S["fc1_psum"], at["fc1_psum"] + f + 1)
                                act.activation(G.hid[:, f, :], bank(G, f), ACT.Gelu, bias=v("fc1_b", 2 * n + f))\
                                    .then_inc(S["hid"], 1)
                        elif kind == "retention":
                            for k in range(2):
                                act.wait_ge(S["qk_psum"], at["qk_psum"] + k + 1)
                                act.activation(G.q[:, k, :], bank(G, k), ACT.Copy).then_inc(S["q"], 1)
                            act.wait_ge(S["v_psum"], at["v_psum"] + 1)
                            act.activation(G.vr[:, :, :], G.ps[0:TT, 2, 0:U * D].rearrange("p (u d) -> p u d", u=U),
                                           ACT.Copy).then_inc(S["v"], 1)
                            for b in range(NB):
                                act.wait_ge(S["st_psum"], at["st_psum"] + b + 1)
                                for kt in range(2):
                                    ex = act.activation(G.p[0:TT, b, kt * TOK:(kt + 1) * TOK],
                                                        G.ps[0:TT, 2 + b, kt * TOK:(kt + 1) * TOK], ACT.Exp,
                                                        bias=key_decay[:, kt:kt + 1], scale=D ** -0.5)
                                ex.then_inc(S["exp"], 1)
                            act.wait_ge(S["sum_psum"], at["sum_psum"] + 1)
                            act.activation(bank(G, 1), bank(G, 1), ACT.Ln).then_inc(S["log"], 1)
                            act.wait_ge(S["log"], at["log"] + 1)
                            act.activation(G.sq[:, :], bank(G, 1), ACT.Exp, scale=-1.0).then_inc(S["rsum"], 1)
                        elif kind == "moe":
                            ft = F0 if n == 0 else F1
                            act.wait_ge(S["gap"], at["gap"] + 1)
                            act.activation(G.sc[:, 1, :, 0], G.sc[:, 0, :, 0], ACT.Exp).then_inc(S["egap"], 1)
                            r = 0
                            for e in range(E):
                                for f in range(ft):
                                    m = e * ft + f
                                    act.wait_ge(S["up_psum"], at["up_psum"] + r + 1)
                                    if m >= 4:
                                        act.wait_ge(S["down"], at["down"] + m - 3)
                                    act.activation(G.hid[:, m % 4, :], bank(G, r % 2),
                                                   ACT.Gelu_apprx_tanh if n == 0 else ACT.Relu,
                                                   bias=v("m0_b1" if n == 0 else "m1_b1", m)).then_inc(S["up_read"], 1)
                                    r += 1
                                    if m == 1:
                                        act.wait_ge(S["gateT_psum"], at["gateT_psum"] + 1)
                                        act.activation(G.ct[:, :], bank(G, 3), ACT.Copy).then_inc(S["gateT"], 1)
                                act.wait_ge(S["up_psum"], at["up_psum"] + r + 1)
                                if e >= 2:
                                    act.wait_ge(S["term"], at["term"] + e - 1)
                                act.activation(G.cb[:, e % 2, :], bank(G, r % 2), ACT.Copy).then_inc(S["up_read"], 1)
                                r += 1
                            if n == 0:
                                loaded = "gelu_tanh"
                        elif kind == "moe0_out":
                            act.wait_ge(S["s"], at["s"] + 1)
                            act.activation(G.sq[:, :], G.z[:, :], ACT.Square).then_inc(S["sq"], 1)
                            rstd(G, at)
                            act.wait_ge(S["z"], at["z"] + 1)
                            act.activation(G.sq[:, :], G.z[:, :], ACT.Identity, bias=v("out_b"), scale=v("out_g"))\
                                .then_inc(S["affine"], 1)
                        elif kind == "linear":
                            for k in range(2):
                                act.wait_ge(S["qk_psum"], at["qk_psum"] + k + 1)
                                if k == 1:
                                    act.wait_ge(S["stat_psum"], at["stat_psum"] + 1)
                                act.activation(G.sq[:, :], bank(G, k), ACT.Square).then_inc(S["sq"], 1)
                                if k == 0:
                                    act.wait_ge(S["v_psum"], at["v_psum"] + 1)
                                    act.activation(G.vr[:, :, :], G.ps[0:TT, 2, 0:U * D].rearrange("p (u d) -> p u d", u=U),
                                                   ACT.Copy).then_inc(S["v"], 1)
                            for k in range(2):
                                t = G.p[:, 4 + k, 0:NC]
                                act.wait_ge(S["floor"], at["floor"] + k + 1)
                                act.activation(t, t, ACT.Ln).then_inc(S["log"], 1)
                                act.wait_ge(S["log"], at["log"] + k + 1)
                                act.activation(t, t, ACT.Exp, bias=eps[:, 1:2], scale=-0.5).then_inc(S["rstd"], 1)
                            act.wait_ge(S["av_psum"], at["av_psum"] + NB)
                            act.activation(G.q[:, 1, :], bank(G, 2), ACT.Copy).then_inc(S["o"], 1)
                        elif kind == "moe1_out":
                            act.wait_ge(S["out_psum"], at["out_psum"] + 1)
                            act.activation(G.ob[:, :, :], G.ps[0:TT, 0, 0:U * D].rearrange("p (u d) -> p u d", u=U), ACT.Copy)\
                                .then_inc(S["out_sb"], 1)

                @block.vector
                def _(dve):
                    def scaled(G, at, dst, src):
                        dve.wait_ge(G.s["rstd"], at["rstd"] + 1)
                        dve.tensor_tensor(dst, src, bank(G, 0), ALU.mult).then_inc(G.s["z"], 1)

                    def add_h(G, ps, bias):
                        return dve.scalar_tensor_tensor(out=real(G.h[:, :]), in0=real(ps), scalar=bias, in1=real(G.h[:, :]),
                                                        op0=ALU.add, op1=ALU.add).then_inc(G.s["h"], 1)

                    for g, kind, n, at in ORDER:
                        G, S = groups[g], groups[g].s
                        at = {name: at.get(name, 0) for name in NAMES}
                        if kind == "conv":
                            hv = G.h[:, :].rearrange("p (b n) -> p b n", b=NB)
                            dve.tensor_copy(hv[:, :, 0:2], posb[:, 0:2].unsqueeze(1).to_broadcast([D, NB, 2]))\
                                .then_inc(S["h"], 1)
                            for b in range(NB):
                                dve.wait_ge(S["conv_psum"], b + 1)
                                dve.tensor_tensor(hv[:, b, 2:TOK], G.ps[:, b, 0:GRID * GRID], posb[:, 2:TOK], ALU.add)\
                                    .then_inc(S["h"], 1)
                        elif kind == "ln_h":
                            dve.wait_ge(S["h"], at["h"])
                            scaled(G, at, G.z[:, :], G.h[:, :])
                        elif kind == "ln_z":
                            dve.wait_ge(S["z"], at["z"])
                            scaled(G, at, G.u[:, :], G.z[:, :])
                        elif kind == "ln_full":
                            dve.wait_ge(S["cen"], at["cen"] + 1)
                            scaled(G, at, G.z[:, :], G.u[:, :])
                        elif kind == "qkv":
                            for k in range(2):
                                dve.wait_ge(S["q"], at["q"] + k + 1)
                                dve.tensor_copy(G.q_bf[:, k, :], G.q[:, k, :]).then_inc(S["q_bf"], 1)
                            for h in range(HEADS):
                                r = slice(32 * (h % 4), 32 * (h % 4) + 32)
                                dve.wait_ge(S["k"], at["k"] + h + 1)
                                dve.tensor_copy(real(G.k_bf[r, h, :]), real(G.k[r, h, :])).then_inc(S["k_bf"], 1)
                        elif kind == "smax":
                            for h in range(HEADS):
                                dve.wait_ge(S["smax_psum"], at["smax_psum"] + h + 1)
                                b0 = (h * NB) % 4
                                src = G.ps[0:TT, b0:b0 + NB, 0:2 * TOK].rearrange("p b (t n) -> p b t n", t=2)[:, :, :, 1:TOK]
                                dve.tensor_reduce(G.negm[:, h], src, X, ALU.max, negate=True).then_inc(S["max"], 1)
                            dve.wait_ge(S["max"], at["max"] + HEADS)
                            src = G.negm[:, :, :, :].rearrange("p (g j) b t -> p (b t) g j", g=2)
                            hi, lo = (G.mt[:, :, :, 16 + k::32] for k in range(2))
                            dve.tensor_copy(hi, src).then_inc(S["mt_hi"], 1)
                            dve.wait_ge(S["mt_hi"], at["mt_hi"] + 1)
                            dve.tensor_tensor(lo, src, hi, ALU.subtract).then_inc(S["mt"], 1)
                            for grp in range(2):
                                dve.wait_ge(S["mrow_psum"], at["mrow_psum"] + grp + 1)
                                dve.tensor_tensor(G.q[:, grp, :], G.q[:, grp, :], bank(G, grp), ALU.add)\
                                    .then_inc(S["q_aug"], 1)
                        elif kind == "norm":
                            for grp in range(2):
                                dve.wait_ge(S["rsum"], at["rsum"] + grp + 1)
                                dve.tensor_tensor(G.o[:, grp, :], G.o[:, grp, :], bank(G, grp), ALU.mult)\
                                    .then_inc(S["o_norm"], 1)
                        elif kind == "proj":
                            dve.wait_ge(S["proj_psum"], at["proj_psum"] + 1)
                            add_h(G, bank(G, 2), v("proj_b", n))
                        elif kind == "mlp":
                            dve.wait_ge(S["fc2_psum"], at["fc2_psum"] + 1)
                            add_h(G, bank(G, 2), v("fc2_b", n))
                        elif kind == "tower_out":
                            dve.wait_ge(S["z"], at["z"])
                            dve.tensor_scalar(G.h[:, :], G.z[:, :], v("norm_w"), v("norm_b"), ALU.mult, ALU.add)\
                                .then_inc(S["affine"], 1)
                            dve.wait_ge(S["affine"], at["affine"] + 1)
                            hv = G.h[:, :].rearrange("p (b n) -> p b n", b=NB)
                            dve.tensor_copy(hv[:, :, 0:1], v("cls_out").unsqueeze(1).to_broadcast([D, NB, 1]))\
                                .then_inc(S["h"], 1)
                        elif kind == "retention":
                            for k in range(2):
                                dve.wait_ge(S["q"], at["q"] + k + 1)
                                dve.tensor_copy(G.q_bf[:, k, :], G.q[:, k, :]).then_inc(S["q_bf"], 1)
                            for b in range(NB):
                                dve.wait_ge(S["smax_psum"], at["smax_psum"] + b + 1)
                                dve.tensor_reduce(G.negm[:, 0, b], G.ps[0:TT, b, 0:2 * TOK].rearrange("p (t n) -> p t n", t=2),
                                                  X, ALU.max, negate=True).then_inc(S["max"], 1)
                            dve.wait_ge(S["max"], at["max"] + NB)
                            src = G.negm[:, 0, :, :].rearrange("p b t -> p (b t)")
                            dve.tensor_copy(G.mt[:, :, 0, 16], src).then_inc(S["mt_hi"], 1)
                            dve.wait_ge(S["mt_hi"], at["mt_hi"] + 1)
                            dve.tensor_tensor(G.mt[:, :, 0, 17], src, G.mt[:, :, 0, 16], ALU.subtract).then_inc(S["mt"], 1)
                            dve.wait_ge(S["rsum"], at["rsum"] + 1)
                            dve.wait_ge(S["av_psum"], at["av_psum"] + 1)
                            dve.tensor_tensor(G.z[:, :], bank(G, 0), G.sq[:, :], ALU.mult).then_inc(S["o_norm"], 1)
                            dve.wait_ge(S["o_norm"], at["o_norm"] + 1)
                            dve.tensor_tensor(G.h[:, :], G.h[:, :], G.z[:, :], ALU.add).then_inc(S["h"], 1)
                        elif kind == "moe":
                            done = [0]

                            def link(ins):
                                done[0] += 1
                                ins.then_inc(S["g"], 1)
                                dve.wait_ge(S["g"], at["g"] + done[0])

                            L, mx, gt, c1, c2, r1, r2 = (G.lg[:, k] for k in range(7))
                            gap, egap, total, wa, wb = (G.sc[:, k, :, 0:1] for k in range(5))
                            dve.wait_ge(S["gate_psum"], at["gate_psum"] + 1)
                            dve.tensor_tensor(L, G.ps[0:TT, 3, 0:U * E].rearrange("p (u e) -> p u e", u=U),
                                              gb[:, n, :].unsqueeze(1).to_broadcast([TT, U, E]), ALU.add)\
                                .then_inc(S["logit"], 1)
                            dve.wait_ge(S["logit"], at["logit"] + 1)
                            for u in range(U):
                                dve.max(mx[:, u], L[:, u]).then_inc(S["top"], 1)
                            dve.wait_ge(S["top"], at["top"] + U)
                            for u in range(U):
                                dve.max_index(G.ix[:, u], mx[:, u], L[:, u]).then_inc(S["topi"], 1)
                            dve.tensor_tensor(gap, mx[:, :, 1:2], mx[:, :, 0:1], ALU.subtract).then_inc(S["gap"], 1)
                            dve.wait_ge(S["topi"], at["topi"] + U)
                            link(dve.tensor_copy(r1[:, :, 0:2], G.ix[:, :, 0:2]))
                            dve.wait_ge(S["egap"], at["egap"] + 1)
                            link(dve.tensor_scalar(total, egap, 1.0, None, ALU.add))
                            link(dve.reciprocal(wa, total))
                            link(dve.tensor_tensor(wb, wa, egap, ALU.mult))
                            io = iota[:, :].unsqueeze(1).to_broadcast([TT, U, E])
                            dve.tensor_tensor(c1, io, r1[:, :, 0:1].to_broadcast([TT, U, E]), ALU.is_equal)
                            link(dve.tensor_tensor(c2, io, r1[:, :, 1:2].to_broadcast([TT, U, E]), ALU.is_equal))
                            dve.tensor_tensor(c1, c1, wa.to_broadcast([TT, U, E]), ALU.mult)
                            link(dve.tensor_tensor(c2, c2, wb.to_broadcast([TT, U, E]), ALU.mult))
                            link(dve.tensor_tensor(gt, c1, c2, ALU.add))
                            p1, p2, p3 = (G.cc[:, :, 32 * k:32 * k + E] for k in range(3))
                            link(dve.tensor_copy(p1, gt))
                            link(dve.tensor_tensor(r2, gt, p1, ALU.subtract))
                            dve.tensor_copy(p2, r2).then_inc(S["mid"], 1)
                            dve.wait_ge(S["mid"], at["mid"] + 1)
                            dve.tensor_tensor(p3, r2, p2, ALU.subtract).then_inc(S["parts"], 1)
                            ft = F0 if n == 0 else F1
                            b2 = "m0_b2" if n == 0 else "m1_b2"
                            for e in range(E):
                                dve.wait_ge(S["down"], at["down"] + (e + 1) * ft)
                                dve.wait_ge(S["up_read"], at["up_read"] + (e + 1) * (ft + 1))
                                if e > 1:
                                    dve.wait_ge(S["acc"], at["acc"] + e - 1)
                                dve.scalar_tensor_tensor(out=G.acc if e == 0 else G.sq[:, :], in0=bank(G, 2 + e % 2),
                                                         scalar=v(b2, e), in1=G.cb[:, e % 2, :], op0=ALU.add, op1=ALU.mult)\
                                    .then_inc(S["term"], 1)
                                if e == 0:
                                    continue
                                dve.wait_ge(S["term"], at["term"] + e + 1)
                                dve.tensor_tensor(G.acc, G.acc, G.sq[:, :], ALU.add).then_inc(S["acc"], 1)
                        elif kind == "moe0_out":
                            dve.wait_ge(S["acc"], at["acc"])
                            dve.tensor_tensor(G.z[:, :], G.z[:, :], G.acc, ALU.add).then_inc(S["s"], 1)
                            dve.wait_ge(S["s"], at["s"] + 1)
                            scaled(G, at, G.z[:, :], G.z[:, :])
                            dve.wait_ge(S["affine"], at["affine"] + 1)
                            dve.tensor_tensor(G.h[:, :], G.h[:, :], G.sq[:, :], ALU.add).then_inc(S["h"], 1)
                        elif kind == "linear":
                            for k in range(2):
                                dve.wait_ge(S["stat_psum"], at["stat_psum"] + k + 1)
                                dve.tensor_scalar(G.p[:, 4 + k, 0:NC], bank(G, 3), TINY, LIFT, ALU.max, ALU.mult)\
                                    .then_inc(S["floor"], 1)
                            dve.wait_ge(S["rstd"], at["rstd"] + 1)
                            dve.tensor_tensor(G.q[:, 0, :], bank(G, 0), G.p[:, 4, 0:NC], ALU.mult).then_inc(S["q"], 1)
                            dve.wait_ge(S["rstd"], at["rstd"] + 2)
                            for h in range(LH):
                                r = slice(32 * h, 32 * h + 32)
                                dve.tensor_tensor(G.k[r, h, :], bank(G, 1)[r], G.p[r, 5, 0:NC], ALU.mult).then_inc(S["k"], 1)
                            for k in range(LH * NB):
                                b, h = divmod(k, LH)
                                dve.wait_ge(S["st_psum"], at["st_psum"] + k + 1)
                                if b > 0:
                                    dve.wait_ge(S["av_psum"], at["av_psum"] + b)
                                for kt in range(2):
                                    c = TT - kt * TT
                                    dx = dve.tensor_tensor(G.p[0:TT, h, kt * TOK:(kt + 1) * TOK],
                                                           G.ps[0:TT, k % 2, kt * TOK:(kt + 1) * TOK],
                                                           decay[:, h, c:c + TOK], ALU.mult)
                                dx.then_inc(S["decayed"], 1)
                            dve.wait_ge(S["proj_psum"], at["proj_psum"] + 1)
                            dve.tensor_tensor(G.h[:, :], G.h[:, :], bank(G, 3), ALU.add).then_inc(S["h"], 1)
                        elif kind == "moe1_out":
                            dve.wait_ge(S["acc"], at["acc"])
                            dve.tensor_tensor(G.h[:, :], G.h[:, :], G.acc, ALU.add).then_inc(S["h"], 1)

                @block.gpsimd
                def _(pool):
                    for G in groups:
                        pool.wait_ge(G.s["conv_psum"], NB)
                        pool.memset(G.arena[:, 0:KW], 0.0).then_inc(G.s["zeroed"], 1)

                @block.sync
                def _(sp):
                    nxt = (it + 1) % ITERS
                    for g, G in enumerate(groups):
                        lin = next(at for kind, _, at in TABLE if kind == "moe" and _ == 1)
                        sp.wait_ge(G.s["h"], lin["h"])
                        load_images(sp, G, g, nxt)
                    for g, G in enumerate(groups):
                        sp.wait_ge(G.s["out_sb"], 1)
                        first = it * (NB * NG) + g * NB
                        sp.dma_start(out[bass.ds(first, NB)].rearrange("b (t p) d -> p (b t) d", t=2), G.ob[:, :, :])\
                            .then_inc(G.out_done, 16)
                    for G in groups:
                        sp.wait_ge(G.x_in, XWAIT)
                        sp.wait_ge(G.out_done, 16)

            with nc.Block() as block:
                @block.gpsimd
                def _(pool):
                    for G in groups:
                        pool.sem_clear(range(G.x_in.num, G.out_done.num + 1))


def _layout(inputs):
    a = {k: np.asarray(v) for k, v in inputs.items()}
    t = {k[len("L0_tok_"):]: v for k, v in a.items() if k.startswith("L0_tok_")}
    f32 = np.float32

    def pad_heads(w):
        o = np.zeros((*w.shape[:-1], 2, 4, 32), f32)
        o[..., 0:HD] = w.reshape(*w.shape[:-1], 2, 4, HD)
        return o.reshape(*w.shape[:-1], 2, D)

    qkv = t["qkv_w"].reshape(DEPTH, D, 3, D)
    qkv_b = t["qkv_b"].reshape(DEPTH, 3, D)
    qk_b = pad_heads(qkv_b[:, 0:2])
    qk_b.reshape(DEPTH, 2, 2, 4, 32)[:, 1, :, :, HD:HD + 2] = 1.0
    cols = {
        "conv_b": t["conv_b"], "cls_in": t["cls_token"].reshape(-1), "cls_out": a["cls_tok"].reshape(-1),
        "norm_w": t["norm_w"], "norm_b": t["norm_b"], "ln1_w": t["ln1_w"].T, "ln1_b": t["ln1_b"].T,
        "ln2_w": t["ln2_w"].T, "ln2_b": t["ln2_b"].T, "proj_b": t["proj_b"].T, "fc2_b": t["fc2_b"].T,
        "fc1_b": t["fc1_b"].reshape(DEPTH * 2, D).T, "qk_b": qk_b.reshape(DEPTH * 4, D).T,
        "v_b": pad_heads(qkv_b[:, 2]).reshape(DEPTH * 2, D).T,
        "ln_g": a["L0_ffn_ln_g"], "ln_b": a["L0_ffn_ln_b"], "out_g": a["L0_ffn_out_g"], "out_b": a["L0_ffn_out_b"],
        "m0_b1": a["L0_ffn_b1"].reshape(E * F0, D).T, "m0_b2": a["L0_ffn_b2"].T,
        "m1_b1": a["L1_ffn_b1"].reshape(E * F1, D).T, "m1_b2": a["L1_ffn_b2"].T,
        "out_scale": np.broadcast_to(a["L1_attn_out_scale"].reshape(1), (D,)),
    }
    vecs = np.concatenate([np.reshape(cols[n], (D, w)) for n, (_, w) in VEC.items()], 1)
    o = {
        "x": a["x"], "conv_w": t["conv_w"], "pos_t": t["pos_embed"][0].T, "vecs": vecs,
        "w_qk": pad_heads(qkv[:, :, 0:2]).transpose(1, 0, 2, 3, 4).reshape(D, DEPTH, 4, D),
        "w_v": qkv[:, :, 2].transpose(1, 0, 2),
        "w_v_pad": pad_heads(qkv[:, :, 2]).transpose(1, 0, 2, 3),
        "w_p": pad_heads(t["proj_w"].transpose(0, 2, 1)).transpose(3, 0, 2, 1),
        "w_fc1": t["fc1_w"].transpose(1, 0, 2),
        "w_fc2": t["fc2_w"].reshape(DEPTH, 2, D, D).transpose(2, 0, 1, 3),
        "w_ret": np.stack([a["L0_attn_Wq"], a["L0_attn_Wk"], a["L0_attn_Wv"]], 1),
        "w_lin": np.stack([a["L1_attn_shared_q_w"], a["L1_attn_shared_k_w"]], 1),
        "coef": np.stack([a["L1_attn_basis"].T, a["L1_attn_v_coeffs"].T, a["L1_attn_o_coeffs"].T], 1),
        "gates": np.stack([a["L0_ffn_Wg"], a["L1_ffn_gate_w"]], 1),
        "gate_b": np.broadcast_to(a["L1_ffn_gate_b"], (TT, E)),
        "decay_logits": np.broadcast_to(a["L1_attn_decay_logits"], (TT, LH)),
        "m0_w1": a["L0_ffn_W1"].reshape(E, D, F0, D).transpose(1, 0, 2, 3).reshape(D, E * F0, D),
        "m0_w2": a["L0_ffn_W2"].reshape(E * F0, D, D).transpose(1, 0, 2),
        "m1_w1": a["L1_ffn_w1"].reshape(E, D, F1, D).transpose(1, 0, 2, 3).reshape(D, E * F1, D),
        "m1_w2": a["L1_ffn_w2"].reshape(E * F1, D, D).transpose(1, 0, 2),
    }
    return {k: np.ascontiguousarray(v) for k, v in o.items()}


def kernel(**inputs):
    import concourse.bacc as _bacc
    from concourse.bass_utils import run_bass_kernel_spmd as _run

    nc = _bacc.Bacc("TRN2", target_bir_lowering=False, num_devices=1)
    data, consts = _layout(inputs), constants()
    arrays, args = {}, {}
    for name, a in (*data.items(), *(("c_" + k, c) for k, c in consts.items())):
        arrays["in_" + name] = a
        args[name] = nc.dram_tensor("in_" + name, a.shape, mybir.dt.from_np(a.dtype), kind="ExternalInput").ap()
    out = nc.dram_tensor("out_0", (BATCH, TOK, D), F32, kind="ExternalOutput").ap()
    tower_kernel(nc, *(args[n] for n in data), {k: args["c_" + k] for k in consts}, out)
    r = _run(nc, [arrays], core_ids=[0])
    return r.results[0]["out_0"]
```

```python
from contextlib import ExitStack
from math import log, sqrt

import concourse.bass as bass
import numpy as np
from concourse import mybir

F32, BF16, U32 = mybir.dt.float32, mybir.dt.bfloat16, mybir.dt.uint32
ALU = mybir.AluOpType
ACT = mybir.ActivationFunctionType
X = mybir.AxisListType.X

BATCH, CH, IMG, PATCH, D = 64, 3, 224, 16, 128
GRID = IMG // PATCH
DEPTH, HEADS, HD, MLP = 4, 8, 16, 256
TOK = GRID * GRID + 2
TT = TOK // 2
NB = 2
NG = 2
NC = NB * TOK
U = 2 * NB
ROUNDS = 2
ITERS = BATCH // (NB * NG * ROUNDS)
E = 8
F0, F1 = 512 // D, 256 // D
HALF = PATCH // 2
XW = IMG - HALF
CK = 2 * CH * PATCH
EPS = 1e-5
TINY = 1e-24
LIFT = 2.0 ** 20
RING = 6
LH = 4
TW = 3 * TT

VEC = {}
_at = 0
for _n, _w in (("conv_b", 1), ("cls_in", 1), ("cls_out", 1), ("norm_w", 1), ("norm_b", 1), ("ln1_w", DEPTH),
               ("ln1_b", DEPTH), ("ln2_w", DEPTH), ("ln2_b", DEPTH), ("proj_b", DEPTH), ("fc2_b", DEPTH),
               ("fc1_b", 2 * DEPTH), ("qk_b", 4 * DEPTH), ("v_b", 2 * DEPTH), ("ln_g", 1), ("ln_b", 1),
               ("out_g", 1), ("out_b", 1), ("m0_b1", E * F0), ("m0_b2", E), ("m1_b1", E * F1), ("m1_b2", E),
               ("out_scale", 1)):
    VEC[_n] = (_at, _w)
    _at += _w
NV = _at


def constants():
    p = np.arange(TT)[:, None]
    n = np.arange(TOK)[None, :]
    lg = log(0.96)
    c = {}
    c["ident"] = np.eye(D, dtype=np.float32)
    c["center"] = np.eye(D, dtype=np.float32) - np.float32(1.0 / D)
    c["mean"] = np.full((D, D), 1.0 / D, np.float32)
    c["ones"] = np.ones((D, D), np.float32)
    k = np.arange(D)
    c["headsum"] = ((k[:, None] % 32 == 16) & (k[:, None] // 32 == k[None, :] // 32)).astype(np.float32)
    c["expert"] = np.stack([np.repeat(((k % 32 == e) & (k < 96))[:, None], D, 1) for e in range(E)], 1).astype(np.float32)
    c["mask_qk"] = np.stack([np.where(n > p + TT * t, -1e30, -n * lg * sqrt(D)) for t in range(2)], 1).astype(np.float32)
    c["mask_kq"] = np.stack([np.where(n < p + TT * t, -1e30, 0.0 * n) for t in range(2)], 1).astype(np.float32)
    c["key_decay"] = np.concatenate([-(p + TT * t) * lg for t in range(2)], 1).astype(np.float32)
    diff = p - (np.arange(TW)[None, :] - TT)
    c["steps"] = np.maximum(diff - 1, 0).astype(np.float32)
    c["future"] = (diff > 0).astype(np.float32)
    c["iota"] = np.broadcast_to(np.arange(E, dtype=np.float32), (TT, E)).copy()
    return c


class Group:
    pass


LONG, SHORT, LOW = 0.67, 0.34, 0.1
WIDE_A, READ_A, WIDE_V = 0.47, 0.38, 0.48


def normalized(add, after, square=True):
    if square:
        after = add("act", "square", 0, WIDE_A, after)
    return add("dve", "scale", 0, WIDE_V, add("act", "rstd", 0, 0.99, add("pe", "stat", 0, LONG, after)))


def centered(add, after):
    after = add("act", "center_read", 0, 0.76, add("pe", "center", 0, LONG, after))
    return normalized(add, after, square=False)


def conv_ops(add, last, n):
    for b in range(NB):
        last = add("dve", "conv_h", b, 0.4, add("pe", "conv", b, 2.7, last))
    return last


def qkv_ops(add, last, n):
    prod = [add("pe", "qk", k, LONG, last) for k in range(4)]
    q = [add("act", "q_read", k, WIDE_A, prod[k]) for k in range(2)]
    vp = add("pe", "v", 0, 0.87, q[0])
    k = [add("act", "k_read", h, WIDE_A, prod[2 + h // 4]) for h in range(4)]
    v = add("act", "v_read", 0, 0.48, vp)
    k += [add("act", "k_read", h, WIDE_A, prod[2 + h // 4]) for h in range(4, HEADS)]
    qb = [add("dve", "q_round", i, 0.27, q[i]) for i in range(2)]
    kb = [add("dve", "k_round", h, 0.27, k[h]) for h in range(HEADS)]
    ends, mx = [], []
    for h in range(HEADS):
        free = [v] if h == 0 else [k[-1]] if h == 1 else [mx[h - 4 // NB]]
        p = add("pe", "smax", h, 0.34, kb[h], qb[h // 4], *free)
        mx.append(add("dve", "max", h, 0.88, p))
    mt = add("dve", "max_parts", 0, 0.31, mx[-1])
    rows = add("pe", "max_rows", 0, 0.35, mt)
    return [add("dve", "q_shift", g, WIDE_V, rows) for g in range(2)][1]


def attn_ops(add, last, n):
    e, av, oread, dn = [], [], [], []
    K = HEADS * NB
    for k in range(K):
        st = add("pe", "st", k, 2 * SHORT, last, *e[k - 2:k - 1] if k >= 2 else [])
        e.append(add("act", "exp", k, READ_A, st, *([av[(k - RING) // 4]] if k >= RING else [])))
        if k >= 5 and k % 4 == 1:
            av.append(add("pe", "av", (k - 5) // 4, 0.82, e[k - 2]))
        if k == 4 * NB + 3:
            oread.append(add("act", "o_read", 0, READ_A, av[NB - 1]))
        if k == 4 * NB + 5:
            dn.append(add("pe", "headsum", 0, LONG, oread[0]))
        if k == 4 * NB + 7:
            r = add("act", "rsum", 0, 0.9, dn[0])
            on0 = add("dve", "o_scale", 0, WIDE_V, r)
    av.append(add("pe", "av", 2 * NB - 1, 0.82, e[-1]))
    oread.append(add("act", "o_read", 1, READ_A, av[-1]))
    p0 = add("pe", "proj", 0, LONG, on0, e[-2])
    dn.append(add("pe", "headsum", 1, LONG, oread[1]))
    r = add("act", "rsum", 1, 0.9, dn[1])
    on1 = add("dve", "o_scale", 1, WIDE_V, r)
    p1 = add("pe", "proj", 1, LONG, on1)
    return add("dve", "proj_add", 0, 0.55, p1)


def mlp_ops(add, last, n):
    up = [add("pe", "fc1", f, LONG, last) for f in range(2)]
    g = add("act", "gelu", 0, 0.95, up[1])
    dn = [add("pe", "fc2", f, LONG, g) for f in range(2)]
    return add("dve", "fc2_add", 0, 0.55, dn[1])


def retention_ops(add, last, n):
    p = [add("pe", "qk", k, LONG, last) for k in range(2)]
    q = [add("act", "q_read", k, WIDE_A, p[k]) for k in range(2)]
    v = add("act", "v_read", 0, 0.48, add("pe", "v", 0, 0.87, last))
    qb = [add("dve", "q_round", k, 0.27, q[k]) for k in range(2)]
    m = [add("dve", "max", b, 0.45, add("pe", "smax", b, 4 * LOW, qb[1])) for b in range(NB)]
    mt = add("dve", "max_parts", 0, 0.2, m[-1])
    e = [add("act", "exp", b, 0.6, add("pe", "st", b, 2 * SHORT + 8 * 0.06, mt, v)) for b in range(NB)]
    av = add("pe", "av", 0, 4 * SHORT, e[-1])
    sm = add("pe", "probsum", 0, 4 * SHORT, e[-1])
    r = add("act", "rsum", 0, 0.9, sm)
    return add("dve", "o_scale", 0, 1.0, r, av)


def linear_ops(add, last, n):
    p = [add("pe", "qk", k, LONG, last) for k in range(2)]
    vp = add("pe", "v", 0, 0.87, last)
    s0 = add("act", "qk_square", 0, WIDE_A, p[0])
    v = add("act", "v_read", 0, 0.48, vp)
    n0 = add("pe", "norm", 0, LONG, s0)
    s1 = add("act", "qk_square", 1, WIDE_A, n0)
    f0 = add("dve", "floor", 0, WIDE_V, n0)
    n1 = add("pe", "norm", 1, LONG, s1, f0)
    f1 = add("dve", "floor", 1, WIDE_V, n1)
    r0 = add("act", "rnorm", 0, 1.08, f0)
    r1 = add("act", "rnorm", 1, 1.08, f1)
    q = add("dve", "q_scale", 0, WIDE_V, r0)
    k = add("dve", "k_scale", 0, 4 * WIDE_V, r1)
    d, av = [], []
    for i in range(LH * NB):
        st = add("pe", "st", i, 2 * SHORT, k, *d[i - 2:i - 1] if i >= 2 else [])
        d.append(add("dve", "decay", i, 0.55, st, *av[-1:]))
        if i % LH == LH - 1:
            av.append(add("pe", "av", i // LH, 0.82, d[-1], v))
    o = add("act", "o_read", 0, READ_A, av[-1])
    return add("dve", "proj_add", 0, WIDE_V, add("pe", "proj", 0, LONG, o))


def moe_ops(add, last, n):
    ft = F0 if n == 0 else F1
    up_name = "hid_tanh" if n == 0 else "hid_relu"
    gate = add("pe", "gate", 0, 0.59, last)
    gap = add("dve", "top", 0, 1.04, gate)
    eg = add("act", "gap_exp", 0, 0.12, gap)
    parts = add("dve", "gates", 0, 2.46, eg)
    ring, hid, down, term = [], [], [], []

    def bank_free():
        return ring[-2:-1]

    def fill_down(m):
        e = m // ft
        down.append(add("pe", "down", m, LONG, hid[m], *([term[e - 2]] if e >= 2 else [])))
        if m % ft == ft - 1:
            t = add("dve", "term", e, 0.55, down[-1], cb[e])
            term.append(t if e == 0 else add("dve", "acc", e, WIDE_V, t))

    cb = []
    for e in range(E):
        for f in range(ft):
            m = e * ft + f
            u = add("pe", "up", m, LONG, last, *bank_free())
            hid.append(add("act", up_name, m, WIDE_A, u, *([down[m - 4]] if m >= 4 else [])))
            ring.append(hid[-1])
            if m >= 2:
                fill_down(m - 2)
            if m == 1:
                ct = add("act", "ct_read", 0, READ_A, add("pe", "gateT", 0, 0.17, parts))
        c = add("pe", "spread", e, 0.18, ct, *bank_free())
        cb.append(add("act", "spread_read", e, READ_A, c, *([term[e - 2]] if e >= 2 else [])))
        ring.append(cb[-1])
    fill_down(E * ft - 2)
    fill_down(E * ft - 1)
    return term[-1]


def signals(kind, n):
    ln = {"sq": 1, "stat_psum": 1, "log": 1, "rstd": 1, "z": 1}
    ft = F0 if n == 0 else F1
    return {
        "conv": {"conv_psum": NB, "h": NB + 1, "zeroed": 1},
        "ln_h": ln,
        "ln_z": ln,
        "ln_full": ln | {"cen_psum": 1, "cen": 1},
        "qkv": {"qk_psum": 4, "q": 2, "q_bf": 2, "k": HEADS, "k_bf": HEADS, "v_psum": 1, "v": 1,
                "smax_psum": HEADS, "max": HEADS, "mt_hi": 1, "mt": 1, "mrow_psum": 2, "q_aug": 2},
        "attn": {"st_psum": HEADS * NB, "exp": HEADS * NB, "av_psum": 2 * NB, "o": 2, "sum_psum": 2, "log": 2,
                 "rsum": 2, "o_norm": 2, "proj_psum": 1, "h": 1},
        "mlp": {"fc1_psum": 2, "hid": 2, "fc2_psum": 1, "h": 1},
        "tower_out": {"affine": 1, "h": 1},
        "retention": {"qk_psum": 2, "q": 2, "q_bf": 2, "v_psum": 1, "v": 1, "smax_psum": NB, "max": NB, "mt_hi": 1,
                      "mt": 1, "st_psum": NB, "exp": NB, "av_psum": 1, "sum_psum": 1, "log": 1, "rsum": 1,
                      "o_norm": 1, "h": 1},
        "linear": {"qk_psum": 2, "sq": 2, "stat_psum": 2, "floor": 2, "log": 2, "rstd": 2, "q": 1, "k": LH,
                   "v_psum": 1, "v": 1, "st_psum": LH * NB, "decayed": LH * NB, "av_psum": NB, "o": 1, "proj_psum": 1,
                   "h": 1},
        "moe": {"gate_psum": 1, "logit": 1, "top": U, "topi": U, "gap": 1, "egap": 1, "g": 9, "mid": 1, "parts": 1,
                "gateT_psum": 1, "gateT": 1, "up_psum": E * (ft + 1), "up_read": E * (ft + 1), "down": E * ft,
                "term": E, "acc": E - 1},
        "moe0_out": {"s": 1, "sq": 1, "stat_psum": 1, "log": 1, "rstd": 1, "z": 1, "affine": 1, "h": 1},
        "moe1_out": {"h": 1, "out_psum": 1, "out_sb": 1},
    }[kind]


def stream():
    ops, at, last = [], {}, None

    def step(kind, n, rnd, build):
        nonlocal last
        begins = dict(at)

        def add(engine, name, i, us, *follows):
            ops.append((engine, name, i, us, [f for f in follows if f is not None], kind, n, rnd, begins))
            return len(ops) - 1

        last = build(add)
        for name, k in signals(kind, n).items():
            at[name] = at.get(name, 0) + k

    for rnd in range(ROUNDS):
        step("conv", 0, rnd, lambda add: conv_ops(add, last, 0))
        for l in range(DEPTH):
            step("ln_h", l, rnd, lambda add: normalized(add, last))
            step("qkv", l, rnd, lambda add: qkv_ops(add, last, l))
            step("attn", l, rnd, lambda add: attn_ops(add, last, l))
            step("ln_h", l, rnd, lambda add: normalized(add, last))
            step("mlp", l, rnd, lambda add: mlp_ops(add, last, l))
        step("ln_h", 0, rnd, lambda add: normalized(add, last))
        step("tower_out", 0, rnd, lambda add: add("dve", "tower_out", 0, 0.5, last))
        step("ln_full", 0, rnd, lambda add: centered(add, last))
        step("retention", 0, rnd, lambda add: retention_ops(add, last, 0))
        step("ln_full", 1, rnd, lambda add: centered(add, last))
        step("ln_z", 0, rnd, lambda add: normalized(add, last))
        step("moe", 0, rnd, lambda add: moe_ops(add, last, 0))
        step("moe0_out", 0, rnd, lambda add: add(
            "dve", "out_add", 0, WIDE_V, add("act", "affine", 0, WIDE_A, normalized(add, add("dve", "sum_z", 0, WIDE_V, last)))))
        step("ln_full", 2, rnd, lambda add: centered(add, last))
        step("linear", 0, rnd, lambda add: linear_ops(add, last, 0))
        step("ln_full", 3, rnd, lambda add: centered(add, last))
        step("moe", 1, rnd, lambda add: moe_ops(add, last, 1))
        step("moe1_out", 0, rnd, lambda add: add(
            "act", "out_read", 0, 0.6, add("pe", "out_turn", 0, 0.43, add("dve", "out_add", 0, WIDE_V, last))))
    return ops, sorted(at)


TABLES = {"rstd": "log", "exp": "log", "rsum": "log", "rnorm": "log", "gap_exp": "log", "gelu": "gelu", "hid_tanh": "tanh"}


HANDOVER = {("pe", "act"): 0.2, ("pe", "dve"): 0.2, ("act", "pe"): 0.28, ("dve", "pe"): 0.28, ("act", "dve"): 0.15,
            ("dve", "act"): 0.15, ("dve", "dve"): 0.13, ("act", "act"): 0.05, ("pe", "pe"): 0.0}
YIELD = 0.2
AHEAD = 12.0


def merged(ops):
    path = [op[3] for op in ops]
    for i in range(len(ops) - 1, -1, -1):
        for f in ops[i][4]:
            path[f] = max(path[f], ops[f][3] + HANDOVER[ops[f][0], ops[i][0]] + path[i])
    queues = [{e: [i for i, op in enumerate(ops) if op[0] == e] for e in ("pe", "act", "dve")} for _ in range(NG)]
    end = [{} for _ in range(NG)]
    free, table, order = {"pe": 0.0, "act": 0.0, "dve": 0.0}, None, []
    while any(q for qs in queues for q in qs.values()):
        heads = []
        for g in range(NG):
            for e, q in queues[g].items():
                if not q or any(f not in end[g] for f in ops[q[0]][4]):
                    continue
                ready = max([end[g][f] + HANDOVER[ops[f][0], e] for f in ops[q[0]][4]], default=0.0)
                need = TABLES.get(ops[q[0]][1])
                switch = 1.4 if e == "act" and need and need != table else 0.0
                heads.append((max(free[e], ready) + switch, g, e, need, path[q[0]] + (AHEAD if g == 0 else 0.0)))
        best = min(heads)
        for other in heads:
            us = ops[queues[best[1]][best[2]][0]][3]
            if other[2] == best[2] and other[0] < best[0] + YIELD * us + 1e-9 and other[4] > best[4]:
                best = other
        start, g, e, need, _ = best
        i = queues[g][e].pop(0)
        free[e] = end[g][i] = start + ops[i][3]
        if e == "act" and need:
            table = need
        order.append((g, ops[i]))
    return order


def tower_kernel(nc, x, conv_w, pos_t, vecs, w_qk, w_v, w_v_pad, w_p, w_fc1, w_fc2, w_ret, w_lin, coef, gates, gate_b,
                 decay_logits, m0_w1, m0_w2, m1_w1, m1_w2, consts, out):
    OPS, NAMES = stream()
    ORDER = merged(OPS)

    with ExitStack() as ctx:
        def sb(name, shape, dt=F32):
            return ctx.enter_context(nc.sbuf_tensor(name, shape, dt))

        def sem(name):
            return ctx.enter_context(nc.semaphore(name))

        cw = sb("cw", [CK, HALF, D])
        vec = sb("vec", [D, NV])
        wqk = sb("wqk", [D, DEPTH, 4, D])
        wv = sb("wv", [D, DEPTH, D])
        wp = sb("wp", [D, DEPTH, 2, D])
        fc1 = sb("fc1", [D, DEPTH, MLP])
        fc2 = sb("fc2", [D, DEPTH, 2, D])
        wret = sb("wret", [D, 3, D])
        wlin = sb("wlin", [D, 2, D])
        wvb = sb("wvb", [D, D])
        wob = sb("wob", [D, D])
        wg = sb("wg", [D, 2, E])
        gb = sb("gb", [TT, 2, E])
        w1 = [sb("w1_0", [D, E * F0, D]), sb("w1_1", [D, E * F1, D])]
        w2 = [sb("w2_0", [D, E * F0, D]), sb("w2_1", [D, E * F1, D])]
        posb = sb("posb", [D, TOK])
        ident = sb("ident", [D, D])
        identb = sb("identb", [D, D], BF16)
        center = sb("center", [D, D])
        meanm = sb("meanm", [D, D])
        ones = sb("ones", [D, D])
        headsum = sb("headsum", [D, D])
        expertb = sb("expertb", [D, E, D], BF16)
        mask_qk = sb("mask_qk", [TT, 2, TOK], BF16)
        mask_kq = sb("mask_kq", [TT, 2, TOK], BF16)
        key_decay = sb("key_decay", [TT, 2])
        decay = sb("decay", [TT, LH, TW])
        iota = sb("iota", [TT, E])
        eps = sb("eps", [D, 2])
        row99 = sb("row99", [D, 16])

        def v(name, k=0, n=1):
            return vec[:, VEC[name][0] + k:VEC[name][0] + k + n]

        KW, PW = HEADS * NC, RING * 2 * TOK
        ARENA = KW + PW + 2 * NC
        groups = []
        for g in range(NG):
            G = Group()
            groups.append(G)
            t = "AB"[g]
            G.arena = sb(f"arena{t}", [D, ARENA])
            G.k = G.arena[:, 0:KW].rearrange("p (h n) -> p h n", h=HEADS)
            G.p = G.arena[:, KW:KW + PW].rearrange("p (s n) -> p s n", s=RING)
            G.o = G.arena[:, KW + PW:ARENA].rearrange("p (g n) -> p g n", g=2)
            assert NB * GRID * XW <= ARENA
            G.x = G.arena[:, 0:NB * GRID * XW].rearrange("p (b y w) -> p b y w", b=NB, y=GRID)
            G.k_bf = sb(f"k_bf{t}", [D, HEADS, NC], BF16)
            G.q = sb(f"q{t}", [D, 2, NC])
            G.cb = G.q
            G.q_bf = sb(f"q_bf{t}", [D, 2, NC], BF16)
            G.acc = G.q_bf[:, :, :].rearrange("p g n -> p (g n)").bitcast(F32)
            G.h = sb(f"h{t}", [D, NC])
            G.z = sb(f"z{t}", [D, NC])
            G.u = sb(f"u{t}", [D, NC])
            G.sq = sb(f"sq{t}", [D, NC])
            G.va = sb(f"va{t}", [TT, U, HEADS, 32])
            G.hid = sb(f"hid{t}", [D, 4, NC])
            hflat = G.hid[:, :, :].rearrange("p f n -> p (f n)")
            G.vr = hflat[0:TT, 0:U * D].rearrange("p (u d) -> p u d", u=U)
            G.ob = hflat[0:TT, U * D:2 * U * D].rearrange("p (u d) -> p u d", u=U)
            G.negm = sb(f"negm{t}", [TT, HEADS, NB, 2])
            G.mt = sb(f"mt{t}", [TT, U, 2, D], BF16)
            G.lg = sb(f"lg{t}", [TT, 7, U, E])
            G.ix = sb(f"ix{t}", [TT, U, E], U32)
            G.sc = sb(f"sc{t}", [TT, 5, U, 2])
            G.cc = sb(f"cc{t}", [TT, U, D], BF16)
            G.ct = sb(f"ct{t}", [D, NC], BF16)
            G.ps = ctx.enter_context(nc.psum_tensor(f"ps{t}", [D, 4, 512], F32))
            G.x_in = sem(f"x_in_{t}")
            G.s = {n: sem(f"{n}_{t}") for n in NAMES}
            G.out_done = sem(f"out_done_{t}")
            assert G.out_done.num - G.x_in.num == len(NAMES) + 1
        s_load, s_fold, s_ps, s_const = sem("load"), sem("fold"), sem("fold_psum"), sem("const")

        def load_images(eng, G, i):
            for b in range(NB):
                for half in range(2):
                    for c in range(CH):
                        p = (half * CH + c) * PATCH
                        src = x[i * NB + b, c].rearrange("(y r) w -> r y w", r=PATCH)
                        eng.dma_start(G.x[p:p + PATCH, b], src[:, :, half * HALF:half * HALF + XW]).then_inc(G.x_in, 16)

        XWAIT = NB * 2 * CH * 16

        st_expert = groups[1].arena[:, 0:E * D].rearrange("p (e d) -> p e d", e=E)
        st_mqk = groups[1].arena[0:TT, 1024:1024 + 2 * TOK].rearrange("p (t n) -> p t n", t=2)
        st_mkq = groups[1].arena[0:TT, 1424:1424 + 2 * TOK].rearrange("p (t n) -> p t n", t=2)
        st_pos = groups[1].arena[:, 1824:1824 + TOK]
        st_steps = groups[1].arena[0:TT, 2024:2024 + TW]
        st_future = groups[1].arena[0:TT, 2324:2324 + TW]
        st_wvp = groups[1].arena[:, 2624:2624 + DEPTH * 2 * D].rearrange("p (l g d) -> p l g d", l=DEPTH, g=2)
        st_coef = groups[1].arena[:, 3648:3648 + 3 * D].rearrange("p (c d) -> p c d", c=3)
        st_mean = groups[1].arena[:, 4032:4032 + 64]
        st_dl = groups[1].arena[0:TT, 4096:4096 + 3 * LH].rearrange("p (k h) -> p k h", k=3)
        st_vb = groups[1].arena[:, 4112:4112 + 2 * DEPTH]
        psA, psB = groups[0].ps, groups[1].ps

        with nc.Block() as block:
            @block.sync
            def _(sp):
                n = 0
                for half in range(2):
                    src = conv_w.rearrange("(k h j) d -> h k j d", h=2, j=HALF)[half]
                    sp.dma_start(cw[half * CK // 2:(half + 1) * CK // 2], src).then_inc(s_load, 16)
                for dst, src in ((vec[:, :], vecs), (wqk[:, :, :, :], w_qk), (wv[:, :, :], w_v), (st_wvp, w_v_pad),
                                 (wp[:, :, :, :], w_p), (fc1[:, :, :], w_fc1), (fc2[:, :, :, :], w_fc2),
                                 (wret[:, :, :], w_ret), (wlin[:, :, :], w_lin), (st_coef, coef), (wg[:, :, :], gates),
                                 (gb[:, 1, :], gate_b), (st_dl[:, 0], decay_logits),
                                 (w1[0][:, :, :], m0_w1), (w2[0][:, :, :], m0_w2), (w1[1][:, :, :], m1_w1),
                                 (w2[1][:, :, :], m1_w2), (ident[:, :], consts["ident"]),
                                 (center[:, :], consts["center"]), (meanm[:, :], consts["mean"]),
                                 (ones[:, :], consts["ones"]), (headsum[:, :], consts["headsum"]),
                                 (st_expert, consts["expert"]), (st_mqk, consts["mask_qk"]),
                                 (st_mkq, consts["mask_kq"]), (key_decay[:, :], consts["key_decay"]),
                                 (st_steps, consts["steps"]), (st_future, consts["future"]),
                                 (iota[:, :], consts["iota"]), (st_pos[:, 1:TOK], pos_t)):
                    sp.dma_start(dst, src).then_inc(s_load, 16)
                    n += 1
                load_images(sp, groups[0], 0)
                sp.wait_ge(s_load, 16 * (n + 2))
                sp.wait_ge(groups[0].x_in, XWAIT)

            @block.gpsimd
            def _(pool):
                for G in groups:
                    pool.memset(G.k_bf[:, :, :], 0.0)
                    pool.memset(G.va[:, :, :, :], 0.0)
                    pool.memset(G.mt[:, :, :, :], 0.0)
                    pool.memset(G.cc[:, :, :], 0.0)
                pool.memset(eps[:, 0:1], EPS)
                pool.memset(eps[:, 1:2], 0.5 * log(LIFT)).then_inc(s_const, 1)
                pool.wait_ge(s_const, 1)

        with nc.Block() as block:
            @block.vector
            def _(dve):
                for G in groups:
                    dve.memset(G.va[:, :, :, HD:HD + 1], 1.0).then_inc(s_const, 1)
                dve.wait_ge(s_const, 3)
                for G in groups:
                    for b in range(NB):
                        dve.memset(G.va[0:1, 2 * b, :, :], 0.0)
                dve.tensor_copy(identb[:, :], ident[:, :])
                dve.tensor_copy(expertb[:, :, :], st_expert)
                dve.tensor_copy(mask_qk[:, :, :], st_mqk)
                dve.tensor_copy(mask_kq[:, :, :], st_mkq)
                for w, n, at in ((cw[:, :, :], HALF, 0), (wp[:, :, :, :].rearrange("p l g d -> p (l g) d"), 2 * DEPTH, 8),
                                 (fc2[:, :, :, :].rearrange("p l g d -> p (l g) d"), 2 * DEPTH, 16),
                                 (w2[0][:, :, :], E * F0, 24)):
                    k = w.shape[0]
                    dve.tensor_reduce(st_mean[0:k, at:at + n], w, X, ALU.add).then_inc(s_fold, 1)
                dve.wait_ge(s_fold, 4)
                dve.tensor_scalar(st_mean[:, 8:56], st_mean[:, 8:56], 1.0 / D, None, ALU.mult)
                dve.tensor_scalar(st_mean[0:CK, 0:8], st_mean[0:CK, 0:8], 1.0 / D, None, ALU.mult).then_inc(s_fold, 1)
                dve.wait_ge(s_fold, 5)
                for w, n, at in ((cw[:, :, :], HALF, 0), (wp[:, :, :, :].rearrange("p l g d -> p (l g) d"), 2 * DEPTH, 8),
                                 (fc2[:, :, :, :].rearrange("p l g d -> p (l g) d"), 2 * DEPTH, 16),
                                 (w2[0][:, :, :], E * F0, 24)):
                    k = w.shape[0]
                    dve.tensor_tensor(w, w, st_mean[0:k, at:at + n].unsqueeze(2).to_broadcast([k, n, D]), ALU.subtract)
                dve.tensor_scalar(st_pos[:, 2:TOK], st_pos[:, 2:TOK], v("conv_b"), None, ALU.add)
                dve.tensor_tensor(st_pos[:, 1:2], st_pos[:, 1:2], v("cls_in"), ALU.add)
                dve.memset(st_pos[:, 0:1], 0.0).then_inc(s_fold, 1)
                dve.wait_ge(s_fold, 6)

            @block.scalar
            def _(act):
                act.preload_act_table_set("natural_log_exp_and_others")
                act.activation(st_dl[:, 1], st_dl[:, 0], ACT.Exp, scale=-1.0).then_inc(s_ps, 1)
                act.wait_ge(s_ps, 1)
                act.activation(st_dl[:, 2], st_dl[:, 1], ACT.Ln, bias=ones[0:TT, 0:1]).then_inc(s_ps, 1)
                act.wait_ge(s_ps, 2)
                act.activation(st_dl[:, 1], st_dl[:, 2], ACT.Copy, scale=-1.0).then_inc(s_ps, 1)
                act.wait_ge(s_ps, 3)
                for h in range(LH):
                    act.activation(decay[:, h, :], st_steps, ACT.Exp, scale=st_dl[:, 1, h:h + 1]).then_inc(s_ps, 1)
                act.wait_ge(s_ps, 3 + LH)

        with nc.Block() as block:
            @block.tensor
            def _(pe):
                col = 0
                for l in range(DEPTH):
                    for g in range(4):
                        pe.matmul(psA[:, 0, col:col + 1], wqk[:, l, g, :], v("ln1_b", l), start=True, stop=True)
                        col += 1
                for l in range(DEPTH):
                    for g in range(2):
                        pe.matmul(psA[:, 0, col:col + 1], st_wvp[:, l, g, :], v("ln1_b", l), start=True, stop=True)
                        col += 1
                for l in range(DEPTH):
                    for f in range(2):
                        pe.matmul(psA[:, 0, col:col + 1], fc1[:, l, f * D:(f + 1) * D], v("ln2_b", l), start=True, stop=True)
                        col += 1
                for f in range(E * F0):
                    pe.matmul(psA[:, 0, col:col + 1], w1[0][:, f, :], v("ln_b"), start=True, stop=True)
                    col += 1
                pe.matmul(psA[:, 1, 0:TOK], center[:, :], st_pos, start=True, stop=True)
                pe.matmul(psA[0:TT, 2, 0:E], v("ln_b").to_broadcast([D, TT]), wg[:, 0, :], start=True, stop=True)
                pe.matmul(psA[:, 3, 0:E], center[:, :], v("m0_b2", 0, E), start=True, stop=True)
                pe.matmul(psB[:, 0, 0:DEPTH], center[:, :], v("fc2_b", 0, DEPTH), start=True, stop=True)
                pe.matmul(psB[:, 1, 0:D], st_coef[:, 0, :], st_coef[:, 1, :], start=True, stop=True)
                pe.matmul(psB[:, 2, 0:D], st_coef[:, 2, :], st_coef[:, 0, :], start=True, stop=True).then_inc(s_ps, 1)
                pe.wait_ge(s_ps, 4 + LH)

            @block.vector
            def _(dve):
                for h in range(LH):
                    last = dve.tensor_tensor(decay[:, h, :], decay[:, h, :], st_future, ALU.mult)
                last.then_inc(s_fold, 1)
                dve.wait_ge(s_fold, 7)

        with nc.Block() as block:
            @block.vector
            def _(dve):
                n = 4 * DEPTH
                dve.tensor_tensor(v("qk_b", 0, n), v("qk_b", 0, n), psA[:, 0, 0:n], ALU.add)
                dve.tensor_tensor(st_vb, v("v_b", 0, 2 * DEPTH), psA[:, 0, n:n + 2 * DEPTH], ALU.add)
                n += 2 * DEPTH
                dve.tensor_tensor(v("fc1_b", 0, 2 * DEPTH), v("fc1_b", 0, 2 * DEPTH), psA[:, 0, n:n + 2 * DEPTH], ALU.add)
                n += 2 * DEPTH
                dve.tensor_tensor(v("m0_b1", 0, E * F0), v("m0_b1", 0, E * F0), psA[:, 0, n:n + E * F0], ALU.add)
                dve.tensor_copy(posb[:, :], psA[:, 1, 0:TOK])
                dve.tensor_copy(gb[:, 0, :], psA[0:TT, 2, 0:E])
                dve.tensor_copy(v("m0_b2", 0, E), psA[:, 3, 0:E])
                dve.tensor_copy(v("fc2_b", 0, DEPTH), psB[:, 0, 0:DEPTH])
                dve.tensor_copy(wvb[:, :], psB[:, 1, 0:D])
                dve.tensor_scalar(wob[:, :], psB[:, 2, 0:D], v("out_scale"), None, ALU.mult)
                for l in range(DEPTH):
                    dve.tensor_scalar(wqk[:, l, :, :], wqk[:, l, :, :], v("ln1_w", l), None, ALU.mult)
                    dve.tensor_scalar(wv[:, l, :], wv[:, l, :], v("ln1_w", l), None, ALU.mult)
                    dve.tensor_scalar(fc1[:, l, :], fc1[:, l, :], v("ln2_w", l), None, ALU.mult)
                dve.tensor_scalar(wg[:, 0, :], wg[:, 0, :], v("ln_g"), None, ALU.mult)
                dve.tensor_scalar(w1[0][:, :, :], w1[0][:, :, :], v("ln_g"), None, ALU.mult).then_inc(s_fold, 1)
                dve.wait_ge(s_fold, 8)

        with nc.Block() as block:
            @block.tensor
            def _(pe):
                for l in range(DEPTH):
                    o = psA[:, 0, l:l + 1]
                    pe.matmul(o, wp[:, l, 0, :], st_vb[:, 2 * l:2 * l + 1], start=True, stop=False)
                    pe.matmul(o, wp[:, l, 1, :], st_vb[:, 2 * l + 1:2 * l + 2], start=False, stop=False)
                    last = pe.matmul(o, center[:, :], v("proj_b", l), start=False, stop=True)
                last.then_inc(s_ps, 1)
                pe.wait_ge(s_ps, 5 + LH)

        with nc.Block() as block:
            @block.vector
            def _(dve):
                dve.tensor_copy(v("proj_b", 0, DEPTH), psA[:, 0, 0:DEPTH]).then_inc(s_fold, 1)
                dve.wait_ge(s_fold, 9)

            @block.sync
            def _(sp):
                load_images(sp, groups[1], 1)
                sp.wait_ge(groups[1].x_in, XWAIT)

        with nc.Block() as block:
            @block.gpsimd
            def _(pool):
                for G in groups:
                    pool.sem_clear(G.x_in)

        def wait(eng, sem_, count):
            if count > 0:
                eng.wait_ge(sem_, count)

        def real(ap):
            return ap.rearrange("p (b n) -> p b n", b=NB)[:, :, 1:TOK]

        def bank(G, k):
            return G.ps[:, k, 0:NC]

        with nc.Fori(0, ITERS) as it:
            with nc.Block() as block:
                @block.tensor
                def _(pe):
                    for g, (engine, op, i, _, _, kind, n, rnd, counts) in ORDER:
                        if engine != "pe":
                            continue
                        G, S = groups[g], groups[g].s
                        at = {name: counts.get(name, 0) for name in NAMES}
                        ft = F0 if n == 0 else F1
                        src = G.u if kind == "moe" and n == 0 else G.z
                        if op == "conv":
                            if rnd > 0 and i == 0:
                                pe.wait_ge(G.x_in, XWAIT * rnd)
                                pe.wait_ge(S["out_sb"], at["out_sb"])
                            for j in range(HALF):
                                mm = pe.matmul(G.ps[:, i, 0:GRID * GRID], cw[:, j, :],
                                               G.x[0:CK, i, :, j:j + PATCH * (GRID - 1) + 1:PATCH],
                                               start=(j == 0), stop=(j == HALF - 1))
                            mm.then_inc(S["conv_psum"], 1)
                        elif op == "stat":
                            pe.wait_ge(S["sq"], at["sq"] + 1)
                            pe.matmul(bank(G, 0), meanm[:, :], G.sq[:, :], start=True, stop=True).then_inc(S["stat_psum"], 1)
                        elif op == "center":
                            pe.wait_ge(S["h"], at["h"])
                            pe.matmul(bank(G, 1), center[:, :], G.h[:, :], start=True, stop=True).then_inc(S["cen_psum"], 1)
                        elif op == "qk":
                            w = wqk[:, n, i, :] if kind == "qkv" else wret[:, i, :] if kind == "retention" else wlin[:, i, :]
                            pe.wait_ge(S["z"], at["z"])
                            pe.matmul(bank(G, i), w, G.z[:, :], start=True, stop=True).then_inc(S["qk_psum"], 1)
                        elif op == "v":
                            w = wv[:, n, :] if kind == "qkv" else wret[:, 2, :] if kind == "retention" else wvb[:, :]
                            b = 0 if kind == "qkv" else 2
                            pe.wait_ge(S["z"], at["z"])
                            if kind == "qkv":
                                pe.wait_ge(S["q"], at["q"] + 1)
                            for u in range(U):
                                mm = pe.matmul(G.ps[0:TT, b, u * D:(u + 1) * D], G.z[:, u * TT:(u + 1) * TT], w,
                                               start=True, stop=True)
                            mm.then_inc(S["v_psum"], 1)
                        elif op == "smax" and kind == "qkv":
                            pe.wait_ge(S["k_bf"], at["k_bf"] + i + 1)
                            pe.wait_ge(S["q_bf"], at["q_bf"] + 1 + i // 4)
                            pe.wait_ge(S["v"], at["v"] + 1)
                            if (i + 1) * NB > 2:
                                pe.wait_ge(S["k"], at["k"] + HEADS)
                            if i * NB >= 4:
                                pe.wait_ge(S["max"], at["max"] + i - 4 // NB + 1)
                            for b in range(NB):
                                for qt in range(2):
                                    mm = pe.matmul(G.ps[0:TT, (i * NB + b) % 4, qt * TOK:(qt + 1) * TOK],
                                                   G.q_bf[:, i // 4, b * TOK + qt * TT:b * TOK + (qt + 1) * TT],
                                                   G.k_bf[:, i, b * TOK:(b + 1) * TOK], start=True, stop=True)
                            mm.then_inc(S["smax_psum"], 1)
                        elif op == "max_rows":
                            pe.wait_ge(S["mt"], at["mt"] + 1)
                            for grp in range(2):
                                for u in range(U):
                                    mm = pe.matmul(G.ps[:, grp, u * TT:(u + 1) * TT], G.mt[:, u, grp, :],
                                                   identb[0:TT, 0:TT], start=True, stop=True)
                                mm.then_inc(S["mrow_psum"], 1)
                        elif op == "st" and kind == "attn":
                            grp, rest = divmod(i, 4 * NB)
                            b, j = divmod(rest, 4)
                            pe.wait_ge(S["q_aug"], at["q_aug"])
                            if i >= 2:
                                pe.wait_ge(S["exp"], at["exp"] + i - 1)
                            for kt in range(2):
                                mm = pe.matmul(G.ps[0:TT, i % 2, kt * TOK:(kt + 1) * TOK],
                                               G.k[:, 4 * grp + j, b * TOK + kt * TT:b * TOK + (kt + 1) * TT],
                                               G.q[:, grp, b * TOK:(b + 1) * TOK], start=True, stop=True)
                            mm.then_inc(S["st_psum"], 1)
                        elif op == "av" and kind == "attn":
                            grp, b = divmod(i, NB)
                            pe.wait_ge(S["v"], at["v"])
                            pe.wait_ge(S["exp"], at["exp"] + 4 * i + 4)
                            for kt in range(2):
                                for j in range(4):
                                    mm = pe.matmul(G.ps[32 * j:32 * j + 32, 2 + grp, b * TOK:(b + 1) * TOK],
                                                   G.va[:, 2 * b + kt, 4 * grp + j, :],
                                                   G.p[0:TT, (4 * i + j) % RING, kt * TOK:(kt + 1) * TOK],
                                                   start=(kt == 0), stop=(kt == 1))
                            mm.then_inc(S["av_psum"], 1)
                        elif op == "headsum":
                            pe.wait_ge(S["o"], at["o"] + i + 1)
                            pe.matmul(bank(G, 2 + i), headsum[:, :], G.o[:, i, :], start=True, stop=True)\
                                .then_inc(S["sum_psum"], 1)
                        elif op == "proj" and kind == "attn":
                            pe.wait_ge(S["exp"], at["exp"] + HEADS * NB)
                            pe.wait_ge(S["o_norm"], at["o_norm"] + i + 1)
                            mm = pe.matmul(bank(G, 0), wp[:, n, i, :], G.o[:, i, :], start=(i == 0), stop=(i == 1))
                            if i == 1:
                                mm.then_inc(S["proj_psum"], 1)
                        elif op == "fc1":
                            pe.wait_ge(S["z"], at["z"])
                            pe.matmul(bank(G, i), fc1[:, n, i * D:(i + 1) * D], G.z[:, :], start=True, stop=True)\
                                .then_inc(S["fc1_psum"], 1)
                        elif op == "fc2":
                            pe.wait_ge(S["hid"], at["hid"] + i + 1)
                            mm = pe.matmul(bank(G, 2), fc2[:, n, i, :], G.hid[:, i, :], start=(i == 0), stop=(i == 1))
                            if i == 1:
                                mm.then_inc(S["fc2_psum"], 1)
                        elif op == "smax" and kind == "retention":
                            pe.wait_ge(S["q_bf"], at["q_bf"] + 2)
                            pe.wait_ge(S["q"], at["q"] + 2)
                            for qt in range(2):
                                o = G.ps[0:TT, i, qt * TOK:(qt + 1) * TOK]
                                pe.matmul(o, G.q_bf[:, 0, i * TOK + qt * TT:i * TOK + (qt + 1) * TT],
                                          G.q_bf[:, 1, i * TOK:(i + 1) * TOK], start=True, stop=False)
                                mm = pe.matmul(o, identb[0:TT, 0:TT], mask_qk[:, qt, :], start=False, stop=True)
                            mm.then_inc(S["smax_psum"], 1)
                        elif op == "st" and kind == "retention":
                            pe.wait_ge(S["v"], at["v"] + 1)
                            pe.wait_ge(S["mt"], at["mt"] + 1)
                            for kt in range(2):
                                o = G.ps[0:TT, 2 + i, kt * TOK:(kt + 1) * TOK]
                                pe.matmul(o, G.q[:, 1, i * TOK + kt * TT:i * TOK + (kt + 1) * TT],
                                          G.q[:, 0, i * TOK:(i + 1) * TOK], start=True, stop=False)
                                pe.matmul(o, identb[0:TT, 0:TT], mask_kq[:, kt, :], start=False, stop=False)
                                for qt in range(2):
                                    for part in range(2):
                                        mm = pe.matmul(o[:, qt * TT:(qt + 1) * TT],
                                                       G.mt[:, 2 * i + qt, 0, 16 + part:17 + part].to_broadcast([TT, TT]),
                                                       identb[0:TT, 0:TT], start=False, stop=(qt == 1 and part == 1))
                            mm.then_inc(S["st_psum"], 1)
                        elif op in ("av", "probsum") and kind == "retention":
                            pe.wait_ge(S["exp"], at["exp"] + NB)
                            for b in range(NB):
                                for kt in range(2):
                                    w = G.vr[:, 2 * b + kt, :] if op == "av" else ones[0:TT, :]
                                    mm = pe.matmul(G.ps[:, 0 if op == "av" else 1, b * TOK:(b + 1) * TOK], w,
                                                   G.p[0:TT, b, kt * TOK:(kt + 1) * TOK], start=(kt == 0), stop=(kt == 1))
                            mm.then_inc(S["av_psum" if op == "av" else "sum_psum"], 1)
                        elif op == "norm":
                            pe.wait_ge(S["sq"], at["sq"] + i + 1)
                            if i == 1:
                                pe.wait_ge(S["floor"], at["floor"] + 1)
                            pe.matmul(bank(G, 3), ones[:, :], G.sq[:, :], start=True, stop=True).then_inc(S["stat_psum"], 1)
                        elif op == "st" and kind == "linear":
                            b, h = divmod(i, LH)
                            pe.wait_ge(S["q"], at["q"] + 1)
                            pe.wait_ge(S["k"], at["k"] + LH)
                            if i >= 2:
                                pe.wait_ge(S["decayed"], at["decayed"] + i - 1)
                            for kt in range(2):
                                mm = pe.matmul(G.ps[0:TT, i % 2, kt * TOK:(kt + 1) * TOK],
                                               G.k[:, h, b * TOK + kt * TT:b * TOK + (kt + 1) * TT],
                                               G.q[:, 0, b * TOK:(b + 1) * TOK], start=True, stop=True)
                            mm.then_inc(S["st_psum"], 1)
                        elif op == "av" and kind == "linear":
                            pe.wait_ge(S["v"], at["v"] + 1)
                            pe.wait_ge(S["decayed"], at["decayed"] + LH * (i + 1))
                            for kt in range(2):
                                for j in range(LH):
                                    mm = pe.matmul(G.ps[32 * j:32 * j + 32, 2, i * TOK:(i + 1) * TOK],
                                                   G.vr[:, 2 * i + kt, 32 * j:32 * j + 32],
                                                   G.p[0:TT, j, kt * TOK:(kt + 1) * TOK],
                                                   start=(kt == 0), stop=(kt == 1))
                            mm.then_inc(S["av_psum"], 1)
                        elif op == "proj" and kind == "linear":
                            pe.wait_ge(S["o"], at["o"] + 1)
                            pe.matmul(bank(G, 3), wob[:, :], G.q[:, 1, :], start=True, stop=True).then_inc(S["proj_psum"], 1)
                        elif op == "gate":
                            pe.wait_ge(S["z"], at["z"])
                            for u in range(U):
                                mm = pe.matmul(G.ps[0:TT, 3, u * E:(u + 1) * E], src[:, u * TT:(u + 1) * TT], wg[:, n, :],
                                               start=True, stop=True)
                            mm.then_inc(S["gate_psum"], 1)
                        elif op == "up":
                            r = i + i // ft
                            if r >= 2:
                                pe.wait_ge(S["up_read"], at["up_read"] + r - 1)
                            pe.matmul(bank(G, r % 2), w1[n][:, i, :], src[:, :], start=True, stop=True)\
                                .then_inc(S["up_psum"], 1)
                        elif op == "spread":
                            r = i * (ft + 1) + ft
                            pe.wait_ge(S["gateT"], at["gateT"] + 1)
                            pe.wait_ge(S["up_read"], at["up_read"] + r - 1)
                            pe.matmul(bank(G, r % 2), expertb[:, i, :], G.ct[:, :], start=True, stop=True)\
                                .then_inc(S["up_psum"], 1)
                        elif op == "gateT":
                            pe.wait_ge(S["parts"], at["parts"] + 1)
                            for u in range(U):
                                mm = pe.matmul(G.ps[:, 3, u * TT:(u + 1) * TT], G.cc[:, u, :],
                                               identb[0:TT, 0:TT], start=True, stop=True)
                            mm.then_inc(S["gateT_psum"], 1)
                        elif op == "down":
                            e, f = divmod(i, ft)
                            pe.wait_ge(S["up_read"], at["up_read"] + i + e + 1)
                            if f == 0 and e == 1:
                                pe.wait_ge(S["gateT"], at["gateT"] + 1)
                            if f == 0 and e >= 2:
                                pe.wait_ge(S["term"], at["term"] + e - 1)
                            pe.matmul(bank(G, 2 + e % 2), w2[n][:, i, :], G.hid[:, i % 4, :], start=(f == 0),
                                      stop=(f == ft - 1)).then_inc(S["down"], 1)
                        elif op == "out_turn":
                            pe.wait_ge(S["h"], at["h"] + 1)
                            for u in range(U):
                                mm = pe.transpose(G.ps[0:TT, 0, u * D:(u + 1) * D], G.h[:, u * TT:(u + 1) * TT], ident[:, :])
                            mm.then_inc(S["out_psum"], 1)
                        else:
                            raise ValueError(op)

                @block.scalar
                def _(act):
                    table = None
                    for g, (engine, op, i, _, _, kind, n, rnd, counts) in ORDER:
                        if engine != "act":
                            continue
                        G, S = groups[g], groups[g].s
                        at = {name: counts.get(name, 0) for name in NAMES}
                        ft = F0 if n == 0 else F1
                        if TABLES.get(op, table) != table:
                            table = TABLES[op]
                            if table == "log":
                                act.preload_act_table_set("natural_log_exp_and_others")
                        if op == "square":
                            act.wait_ge(S["h"], at["h"])
                            wait(act, S["stat_psum"], at["stat_psum"])
                            if kind == "ln_z":
                                act.wait_ge(S["z"], at["z"])
                            if kind == "moe0_out":
                                act.wait_ge(S["s"], at["s"] + 1)
                            act.activation(G.sq[:, :], (G.h if kind == "ln_h" else G.z)[:, :], ACT.Square).then_inc(S["sq"], 1)
                        elif op == "center_read":
                            act.wait_ge(S["cen_psum"], at["cen_psum"] + 1)
                            act.activation(G.u[:, :], bank(G, 1), ACT.Copy).then_inc(S["cen"], 1)
                            act.activation(G.sq[:, :], bank(G, 1), ACT.Square).then_inc(S["sq"], 1)
                        elif op == "rstd":
                            act.wait_ge(S["stat_psum"], at["stat_psum"] + 1)
                            act.activation(bank(G, 0), bank(G, 0), ACT.Ln, bias=eps[:, 0:1]).then_inc(S["log"], 1)
                            act.wait_ge(S["log"], at["log"] + 1)
                            act.activation(bank(G, 0), bank(G, 0), ACT.Exp, scale=-0.5).then_inc(S["rstd"], 1)
                        elif op == "q_read":
                            act.wait_ge(S["qk_psum"], at["qk_psum"] + i + 1)
                            if kind == "qkv":
                                act.activation(G.q[:, i, :], bank(G, i), ACT.Identity, bias=v("qk_b", 4 * n + i))\
                                    .then_inc(S["q"], 1)
                            else:
                                act.activation(G.q[:, i, :], bank(G, i), ACT.Copy).then_inc(S["q"], 1)
                        elif op == "k_read":
                            if n == 0 and i == 0:
                                act.wait_ge(S["zeroed"], at["zeroed"])
                            r = slice(32 * (i % 4), 32 * (i % 4) + 32)
                            act.wait_ge(S["qk_psum"], at["qk_psum"] + 3 + i // 4)
                            act.activation(real(G.k[r, i, :]), real(bank(G, 2 + i // 4)[r]), ACT.Identity,
                                           bias=v("qk_b", 4 * n + 2 + i // 4)[r]).then_inc(S["k"], 1)
                        elif op == "v_read":
                            act.wait_ge(S["v_psum"], at["v_psum"] + 1)
                            if kind == "qkv":
                                act.activation(G.va[:, :, :, 0:HD].rearrange("p u h d -> p (u h) d"),
                                               G.ps[0:TT, 0, 0:U * D].rearrange("p (uh d) -> p uh d", d=HD), ACT.Copy)\
                                    .then_inc(S["v"], 1)
                            else:
                                act.activation(G.vr[:, :, :], G.ps[0:TT, 2, 0:U * D].rearrange("p (u d) -> p u d", u=U),
                                               ACT.Copy).then_inc(S["v"], 1)
                        elif op == "exp" and kind == "attn":
                            act.wait_ge(S["st_psum"], at["st_psum"] + i + 1)
                            if i >= RING:
                                act.wait_ge(S["av_psum"], at["av_psum"] + (i - RING) // 4 + 1)
                            act.activation(G.p[0:TT, i % RING, :], G.ps[0:TT, i % 2, 0:2 * TOK], ACT.Exp,
                                           scale=HD ** -0.5).then_inc(S["exp"], 1)
                        elif op == "o_read" and kind == "attn":
                            act.wait_ge(S["av_psum"], at["av_psum"] + NB * (i + 1))
                            act.activation(G.o[:, i, :], bank(G, 2 + i), ACT.Copy).then_inc(S["o"], 1)
                        elif op == "rsum" and kind == "attn":
                            act.wait_ge(S["sum_psum"], at["sum_psum"] + i + 1)
                            act.activation(bank(G, 2 + i), bank(G, 2 + i), ACT.Ln).then_inc(S["log"], 1)
                            act.wait_ge(S["log"], at["log"] + i + 1)
                            act.activation(bank(G, 2 + i), bank(G, 2 + i), ACT.Exp, scale=-1.0).then_inc(S["rsum"], 1)
                        elif op == "gelu":
                            if n == 0:
                                wait(act, G.out_done, 16 * rnd)
                            for f in range(2):
                                act.wait_ge(S["fc1_psum"], at["fc1_psum"] + f + 1)
                                act.activation(G.hid[:, f, :], bank(G, f), ACT.Gelu, bias=v("fc1_b", 2 * n + f))\
                                    .then_inc(S["hid"], 1)
                        elif op == "exp" and kind == "retention":
                            act.wait_ge(S["st_psum"], at["st_psum"] + i + 1)
                            for kt in range(2):
                                ex = act.activation(G.p[0:TT, i, kt * TOK:(kt + 1) * TOK],
                                                    G.ps[0:TT, 2 + i, kt * TOK:(kt + 1) * TOK], ACT.Exp,
                                                    bias=key_decay[:, kt:kt + 1], scale=D ** -0.5)
                            ex.then_inc(S["exp"], 1)
                        elif op == "rsum" and kind == "retention":
                            act.wait_ge(S["sum_psum"], at["sum_psum"] + 1)
                            act.activation(bank(G, 1), bank(G, 1), ACT.Ln).then_inc(S["log"], 1)
                            act.wait_ge(S["log"], at["log"] + 1)
                            act.activation(G.sq[:, :], bank(G, 1), ACT.Exp, scale=-1.0).then_inc(S["rsum"], 1)
                        elif op == "qk_square":
                            act.wait_ge(S["qk_psum"], at["qk_psum"] + i + 1)
                            act.wait_ge(S["stat_psum"], at["stat_psum"] + i)
                            act.activation(G.sq[:, :], bank(G, i), ACT.Square).then_inc(S["sq"], 1)
                        elif op == "rnorm":
                            t = G.p[:, 4 + i, 0:NC]
                            act.wait_ge(S["floor"], at["floor"] + i + 1)
                            act.activation(t, t, ACT.Ln).then_inc(S["log"], 1)
                            act.wait_ge(S["log"], at["log"] + i + 1)
                            act.activation(t, t, ACT.Exp, bias=eps[:, 1:2], scale=-0.5).then_inc(S["rstd"], 1)
                        elif op == "o_read" and kind == "linear":
                            act.wait_ge(S["av_psum"], at["av_psum"] + NB)
                            act.activation(G.q[:, 1, :], bank(G, 2), ACT.Copy).then_inc(S["o"], 1)
                        elif op == "gap_exp":
                            act.wait_ge(S["gap"], at["gap"] + 1)
                            act.activation(G.sc[:, 1, :, 0], G.sc[:, 0, :, 0], ACT.Exp).then_inc(S["egap"], 1)
                        elif op in ("hid_tanh", "hid_relu"):
                            r = i + i // ft
                            act.wait_ge(S["up_psum"], at["up_psum"] + r + 1)
                            if i >= 4:
                                act.wait_ge(S["down"], at["down"] + i - 3)
                            act.activation(G.hid[:, i % 4, :], bank(G, r % 2),
                                           ACT.Gelu_apprx_tanh if n == 0 else ACT.Relu,
                                           bias=v("m0_b1" if n == 0 else "m1_b1", i)).then_inc(S["up_read"], 1)
                        elif op == "ct_read":
                            act.wait_ge(S["gateT_psum"], at["gateT_psum"] + 1)
                            act.activation(G.ct[:, :], bank(G, 3), ACT.Copy).then_inc(S["gateT"], 1)
                        elif op == "spread_read":
                            r = i * (ft + 1) + ft
                            act.wait_ge(S["up_psum"], at["up_psum"] + r + 1)
                            if i >= 2:
                                act.wait_ge(S["term"], at["term"] + i - 1)
                            act.activation(G.cb[:, i % 2, :], bank(G, r % 2), ACT.Copy).then_inc(S["up_read"], 1)
                        elif op == "affine":
                            act.wait_ge(S["z"], at["z"] + 1)
                            act.activation(G.sq[:, :], G.z[:, :], ACT.Identity, bias=v("out_b"), scale=v("out_g"))\
                                .then_inc(S["affine"], 1)
                        elif op == "out_read":
                            act.wait_ge(S["out_psum"], at["out_psum"] + 1)
                            act.activation(G.ob[:, :, :], G.ps[0:TT, 0, 0:U * D].rearrange("p (u d) -> p u d", u=U), ACT.Copy)\
                                .then_inc(S["out_sb"], 1)
                            act.wait_ge(S["out_sb"], rnd + 1)
                            first = (it * (NG * ROUNDS) + rnd * NG + g) * NB
                            act.dma_start(out[bass.ds(first, NB)].rearrange("b (t p) d -> p (b t) d", t=2), G.ob[:, :, :])\
                                .then_inc(G.out_done, 16)
                        else:
                            raise ValueError(op)

                @block.vector
                def _(dve):
                    for g, (engine, op, i, _, _, kind, n, rnd, counts) in ORDER:
                        if engine != "dve":
                            continue
                        G, S = groups[g], groups[g].s
                        at = {name: counts.get(name, 0) for name in NAMES}
                        ft = F0 if n == 0 else F1
                        if op == "conv_h":
                            hv = G.h[:, :].rearrange("p (b n) -> p b n", b=NB)
                            if i == 0:
                                wait(dve, S["out_psum"], at["out_psum"])
                                dve.tensor_copy(hv[:, :, 0:2], posb[:, 0:2].unsqueeze(1).to_broadcast([D, NB, 2]))\
                                    .then_inc(S["h"], 1)
                            dve.wait_ge(S["conv_psum"], at["conv_psum"] + i + 1)
                            dve.tensor_tensor(hv[:, i, 2:TOK], G.ps[:, i, 0:GRID * GRID], posb[:, 2:TOK], ALU.add)\
                                .then_inc(S["h"], 1)
                        elif op == "scale":
                            src, dst = {"ln_h": (G.h, G.z), "ln_z": (G.z, G.u), "ln_full": (G.u, G.z),
                                        "moe0_out": (G.z, G.z)}[kind]
                            dve.wait_ge(S["rstd"], at["rstd"] + 1)
                            dve.tensor_tensor(dst[:, :], src[:, :], bank(G, 0), ALU.mult).then_inc(S["z"], 1)
                        elif op == "q_round":
                            dve.wait_ge(S["q"], at["q"] + i + 1)
                            dve.tensor_copy(G.q_bf[:, i, :], G.q[:, i, :]).then_inc(S["q_bf"], 1)
                        elif op == "k_round":
                            r = slice(32 * (i % 4), 32 * (i % 4) + 32)
                            dve.wait_ge(S["k"], at["k"] + i + 1)
                            dve.tensor_copy(real(G.k_bf[r, i, :]), real(G.k[r, i, :])).then_inc(S["k_bf"], 1)
                        elif op == "max" and kind == "qkv":
                            dve.wait_ge(S["smax_psum"], at["smax_psum"] + i + 1)
                            b0 = (i * NB) % 4
                            src = G.ps[0:TT, b0:b0 + NB, 0:2 * TOK].rearrange("p b (t n) -> p b t n", t=2)[:, :, :, 1:TOK]
                            dve.tensor_reduce(G.negm[:, i], src, X, ALU.max, negate=True).then_inc(S["max"], 1)
                        elif op == "max_parts":
                            if kind == "qkv":
                                dve.wait_ge(S["max"], at["max"] + HEADS)
                                src = G.negm[:, :, :, :].rearrange("p (g j) b t -> p (b t) g j", g=2)
                                hi, lo = (G.mt[:, :, :, 16 + k::32] for k in range(2))
                            else:
                                dve.wait_ge(S["max"], at["max"] + NB)
                                src = G.negm[:, 0, :, :].rearrange("p b t -> p (b t)")
                                hi, lo = (G.mt[:, :, 0, 16 + k] for k in range(2))
                            dve.tensor_copy(hi, src).then_inc(S["mt_hi"], 1)
                            dve.wait_ge(S["mt_hi"], at["mt_hi"] + 1)
                            dve.tensor_tensor(lo, src, hi, ALU.subtract).then_inc(S["mt"], 1)
                        elif op == "q_shift":
                            dve.wait_ge(S["mrow_psum"], at["mrow_psum"] + i + 1)
                            dve.tensor_tensor(G.q[:, i, :], G.q[:, i, :], bank(G, i), ALU.add).then_inc(S["q_aug"], 1)
                        elif op == "o_scale" and kind == "attn":
                            dve.wait_ge(S["rsum"], at["rsum"] + i + 1)
                            dve.tensor_tensor(G.o[:, i, :], G.o[:, i, :], bank(G, 2 + i), ALU.mult).then_inc(S["o_norm"], 1)
                        elif op in ("proj_add", "fc2_add") and kind in ("attn", "mlp"):
                            made, src, bias = ("proj_psum", bank(G, 0), "proj_b") if kind == "attn" else \
                                ("fc2_psum", bank(G, 2), "fc2_b")
                            dve.wait_ge(S[made], at[made] + 1)
                            dve.scalar_tensor_tensor(out=real(G.h[:, :]), in0=real(src), scalar=v(bias, n),
                                                     in1=real(G.h[:, :]), op0=ALU.add, op1=ALU.add).then_inc(S["h"], 1)
                        elif op == "tower_out":
                            dve.wait_ge(S["z"], at["z"])
                            dve.tensor_scalar(G.h[:, :], G.z[:, :], v("norm_w"), v("norm_b"), ALU.mult, ALU.add)\
                                .then_inc(S["affine"], 1)
                            dve.wait_ge(S["affine"], at["affine"] + 1)
                            hv = G.h[:, :].rearrange("p (b n) -> p b n", b=NB)
                            dve.tensor_copy(hv[:, :, 0:1], v("cls_out").unsqueeze(1).to_broadcast([D, NB, 1]))\
                                .then_inc(S["h"], 1)
                        elif op == "max" and kind == "retention":
                            dve.wait_ge(S["smax_psum"], at["smax_psum"] + i + 1)
                            dve.tensor_reduce(G.negm[:, 0, i], G.ps[0:TT, i, 0:2 * TOK].rearrange("p (t n) -> p t n", t=2),
                                              X, ALU.max, negate=True).then_inc(S["max"], 1)
                        elif op == "o_scale" and kind == "retention":
                            dve.wait_ge(S["rsum"], at["rsum"] + 1)
                            dve.wait_ge(S["av_psum"], at["av_psum"] + 1)
                            dve.tensor_tensor(G.z[:, :], bank(G, 0), G.sq[:, :], ALU.mult).then_inc(S["o_norm"], 1)
                            dve.wait_ge(S["o_norm"], at["o_norm"] + 1)
                            dve.tensor_tensor(G.h[:, :], G.h[:, :], G.z[:, :], ALU.add).then_inc(S["h"], 1)
                        elif op == "top":
                            L, mx = G.lg[:, 0], G.lg[:, 1]
                            dve.wait_ge(S["gate_psum"], at["gate_psum"] + 1)
                            dve.tensor_tensor(L, G.ps[0:TT, 3, 0:U * E].rearrange("p (u e) -> p u e", u=U),
                                              gb[:, n, :].unsqueeze(1).to_broadcast([TT, U, E]), ALU.add)\
                                .then_inc(S["logit"], 1)
                            dve.wait_ge(S["logit"], at["logit"] + 1)
                            for u in range(U):
                                dve.max(mx[:, u], L[:, u]).then_inc(S["top"], 1)
                            dve.wait_ge(S["top"], at["top"] + U)
                            dve.tensor_tensor(G.sc[:, 0, :, 0:1], mx[:, :, 1:2], mx[:, :, 0:1], ALU.subtract)\
                                .then_inc(S["gap"], 1)
                            for u in range(U):
                                dve.max_index(G.ix[:, u], mx[:, u], L[:, u]).then_inc(S["topi"], 1)
                        elif op == "gates":
                            done = [0]

                            def link(ins):
                                done[0] += 1
                                ins.then_inc(S["g"], 1)
                                dve.wait_ge(S["g"], at["g"] + done[0])

                            gt, c1, c2, r1, r2 = (G.lg[:, k] for k in range(2, 7))
                            egap, total, wa, wb = (G.sc[:, k, :, 0:1] for k in range(1, 5))
                            dve.wait_ge(S["topi"], at["topi"] + U)
                            link(dve.tensor_copy(r1[:, :, 0:2], G.ix[:, :, 0:2]))
                            dve.wait_ge(S["egap"], at["egap"] + 1)
                            link(dve.tensor_scalar(total, egap, 1.0, None, ALU.add))
                            link(dve.reciprocal(wa, total))
                            link(dve.tensor_tensor(wb, wa, egap, ALU.mult))
                            io = iota[:, :].unsqueeze(1).to_broadcast([TT, U, E])
                            dve.tensor_tensor(c1, io, r1[:, :, 0:1].to_broadcast([TT, U, E]), ALU.is_equal)
                            link(dve.tensor_tensor(c2, io, r1[:, :, 1:2].to_broadcast([TT, U, E]), ALU.is_equal))
                            dve.tensor_tensor(c1, c1, wa.to_broadcast([TT, U, E]), ALU.mult)
                            link(dve.tensor_tensor(c2, c2, wb.to_broadcast([TT, U, E]), ALU.mult))
                            link(dve.tensor_tensor(gt, c1, c2, ALU.add))
                            p1, p2, p3 = (G.cc[:, :, 32 * k:32 * k + E] for k in range(3))
                            link(dve.tensor_copy(p1, gt))
                            link(dve.tensor_tensor(r2, gt, p1, ALU.subtract))
                            dve.tensor_copy(p2, r2).then_inc(S["mid"], 1)
                            dve.wait_ge(S["mid"], at["mid"] + 1)
                            dve.tensor_tensor(p3, r2, p2, ALU.subtract).then_inc(S["parts"], 1)
                        elif op == "term":
                            dve.wait_ge(S["down"], at["down"] + (i + 1) * ft)
                            dve.wait_ge(S["up_read"], at["up_read"] + (i + 1) * (ft + 1))
                            if i > 1:
                                dve.wait_ge(S["acc"], at["acc"] + i - 1)
                            dve.scalar_tensor_tensor(out=G.acc if i == 0 else G.sq[:, :], in0=bank(G, 2 + i % 2),
                                                     scalar=v("m0_b2" if n == 0 else "m1_b2", i), in1=G.cb[:, i % 2, :],
                                                     op0=ALU.add, op1=ALU.mult).then_inc(S["term"], 1)
                        elif op == "acc":
                            dve.wait_ge(S["term"], at["term"] + i + 1)
                            dve.tensor_tensor(G.acc, G.acc, G.sq[:, :], ALU.add).then_inc(S["acc"], 1)
                        elif op == "sum_z":
                            dve.wait_ge(S["acc"], at["acc"])
                            dve.tensor_tensor(G.z[:, :], G.z[:, :], G.acc, ALU.add).then_inc(S["s"], 1)
                        elif op == "out_add" and kind == "moe0_out":
                            dve.wait_ge(S["affine"], at["affine"] + 1)
                            dve.tensor_tensor(G.h[:, :], G.h[:, :], G.sq[:, :], ALU.add).then_inc(S["h"], 1)
                        elif op == "floor":
                            dve.wait_ge(S["stat_psum"], at["stat_psum"] + i + 1)
                            dve.tensor_scalar(G.p[:, 4 + i, 0:NC], bank(G, 3), TINY, LIFT, ALU.max, ALU.mult)\
                                .then_inc(S["floor"], 1)
                        elif op == "q_scale":
                            dve.wait_ge(S["rstd"], at["rstd"] + 1)
                            dve.tensor_tensor(G.q[:, 0, :], bank(G, 0), G.p[:, 4, 0:NC], ALU.mult).then_inc(S["q"], 1)
                        elif op == "k_scale":
                            dve.wait_ge(S["rstd"], at["rstd"] + 2)
                            for h in range(LH):
                                r = slice(32 * h, 32 * h + 32)
                                dve.tensor_tensor(G.k[r, h, :], bank(G, 1)[r], G.p[r, 5, 0:NC], ALU.mult).then_inc(S["k"], 1)
                        elif op == "decay":
                            b, h = divmod(i, LH)
                            dve.wait_ge(S["st_psum"], at["st_psum"] + i + 1)
                            if b > 0:
                                dve.wait_ge(S["av_psum"], at["av_psum"] + b)
                            for kt in range(2):
                                c = TT - kt * TT
                                dx = dve.tensor_tensor(G.p[0:TT, h, kt * TOK:(kt + 1) * TOK],
                                                       G.ps[0:TT, i % 2, kt * TOK:(kt + 1) * TOK],
                                                       decay[:, h, c:c + TOK], ALU.mult)
                            dx.then_inc(S["decayed"], 1)
                        elif op == "proj_add":
                            dve.wait_ge(S["proj_psum"], at["proj_psum"] + 1)
                            dve.tensor_tensor(G.h[:, :], G.h[:, :], bank(G, 3), ALU.add).then_inc(S["h"], 1)
                        elif op == "out_add":
                            dve.wait_ge(S["acc"], at["acc"])
                            dve.tensor_tensor(G.h[:, :], G.h[:, :], G.acc, ALU.add).then_inc(S["h"], 1)
                        else:
                            raise ValueError(op)

                @block.gpsimd
                def _(pool):
                    for rnd in range(ROUNDS):
                        for G in groups:
                            pool.wait_ge(G.s["conv_psum"], NB * (rnd + 1))
                            pool.memset(G.arena[:, 0:KW], 0.0).then_inc(G.s["zeroed"], 1)

                @block.sync
                def _(sp):
                    through = [counts["h"] for _, op, _, _, _, kind, n, _, counts in OPS if op == "gate" and n == 1]
                    for rnd in range(ROUNDS):
                        for g, G in enumerate(groups):
                            sp.wait_ge(G.s["h"], through[rnd])
                            load_images(sp, G, (it * (NG * ROUNDS) + (rnd + 1) * NG + g) % (BATCH // NB))
                    for G in groups:
                        sp.wait_ge(G.x_in, XWAIT * ROUNDS)
                        sp.wait_ge(G.out_done, 16 * ROUNDS)

            with nc.Block() as block:
                @block.gpsimd
                def _(pool):
                    for G in groups:
                        pool.sem_clear(range(G.x_in.num, G.out_done.num + 1))


def _layout(inputs):
    a = {k: np.asarray(v) for k, v in inputs.items()}
    t = {k[len("L0_tok_"):]: v for k, v in a.items() if k.startswith("L0_tok_")}
    f32 = np.float32

    def pad_heads(w):
        o = np.zeros((*w.shape[:-1], 2, 4, 32), f32)
        o[..., 0:HD] = w.reshape(*w.shape[:-1], 2, 4, HD)
        return o.reshape(*w.shape[:-1], 2, D)

    qkv = t["qkv_w"].reshape(DEPTH, D, 3, D)
    qkv_b = t["qkv_b"].reshape(DEPTH, 3, D)
    qk_b = pad_heads(qkv_b[:, 0:2])
    qk_b.reshape(DEPTH, 2, 2, 4, 32)[:, 1, :, :, HD:HD + 2] = 1.0
    cols = {
        "conv_b": t["conv_b"], "cls_in": t["cls_token"].reshape(-1), "cls_out": a["cls_tok"].reshape(-1),
        "norm_w": t["norm_w"], "norm_b": t["norm_b"], "ln1_w": t["ln1_w"].T, "ln1_b": t["ln1_b"].T,
        "ln2_w": t["ln2_w"].T, "ln2_b": t["ln2_b"].T, "proj_b": t["proj_b"].T, "fc2_b": t["fc2_b"].T,
        "fc1_b": t["fc1_b"].reshape(DEPTH * 2, D).T, "qk_b": qk_b.reshape(DEPTH * 4, D).T,
        "v_b": pad_heads(qkv_b[:, 2]).reshape(DEPTH * 2, D).T,
        "ln_g": a["L0_ffn_ln_g"], "ln_b": a["L0_ffn_ln_b"], "out_g": a["L0_ffn_out_g"], "out_b": a["L0_ffn_out_b"],
        "m0_b1": a["L0_ffn_b1"].reshape(E * F0, D).T, "m0_b2": a["L0_ffn_b2"].T,
        "m1_b1": a["L1_ffn_b1"].reshape(E * F1, D).T, "m1_b2": a["L1_ffn_b2"].T,
        "out_scale": np.broadcast_to(a["L1_attn_out_scale"].reshape(1), (D,)),
    }
    vecs = np.concatenate([np.reshape(cols[n], (D, w)) for n, (_, w) in VEC.items()], 1)
    o = {
        "x": a["x"], "conv_w": t["conv_w"], "pos_t": t["pos_embed"][0].T, "vecs": vecs,
        "w_qk": pad_heads(qkv[:, :, 0:2]).transpose(1, 0, 2, 3, 4).reshape(D, DEPTH, 4, D),
        "w_v": qkv[:, :, 2].transpose(1, 0, 2),
        "w_v_pad": pad_heads(qkv[:, :, 2]).transpose(1, 0, 2, 3),
        "w_p": pad_heads(t["proj_w"].transpose(0, 2, 1)).transpose(3, 0, 2, 1),
        "w_fc1": t["fc1_w"].transpose(1, 0, 2),
        "w_fc2": t["fc2_w"].reshape(DEPTH, 2, D, D).transpose(2, 0, 1, 3),
        "w_ret": np.stack([a["L0_attn_Wq"], a["L0_attn_Wk"], a["L0_attn_Wv"]], 1),
        "w_lin": np.stack([a["L1_attn_shared_q_w"], a["L1_attn_shared_k_w"]], 1),
        "coef": np.stack([a["L1_attn_basis"].T, a["L1_attn_v_coeffs"].T, a["L1_attn_o_coeffs"].T], 1),
        "gates": np.stack([a["L0_ffn_Wg"], a["L1_ffn_gate_w"]], 1),
        "gate_b": np.broadcast_to(a["L1_ffn_gate_b"], (TT, E)),
        "decay_logits": np.broadcast_to(a["L1_attn_decay_logits"], (TT, LH)),
        "m0_w1": a["L0_ffn_W1"].reshape(E, D, F0, D).transpose(1, 0, 2, 3).reshape(D, E * F0, D),
        "m0_w2": a["L0_ffn_W2"].reshape(E * F0, D, D).transpose(1, 0, 2),
        "m1_w1": a["L1_ffn_w1"].reshape(E, D, F1, D).transpose(1, 0, 2, 3).reshape(D, E * F1, D),
        "m1_w2": a["L1_ffn_w2"].reshape(E * F1, D, D).transpose(1, 0, 2),
    }
    return {k: np.ascontiguousarray(v) for k, v in o.items()}


def kernel(**inputs):
    import concourse.bacc as _bacc
    from concourse.bass_utils import run_bass_kernel_spmd as _run

    nc = _bacc.Bacc("TRN2", target_bir_lowering=False, num_devices=1)
    data, consts = _layout(inputs), constants()
    arrays, args = {}, {}
    for name, a in (*data.items(), *(("c_" + k, c) for k, c in consts.items())):
        arrays["in_" + name] = a
        args[name] = nc.dram_tensor("in_" + name, a.shape, mybir.dt.from_np(a.dtype), kind="ExternalInput").ap()
    out = nc.dram_tensor("out_0", (BATCH, TOK, D), F32, kind="ExternalOutput").ap()
    tower_kernel(nc, *(args[n] for n in data), {k: args["c_" + k] for k in consts}, out)
    r = _run(nc, [arrays], core_ids=[0])
    return r.results[0]["out_0"]
```

```python
from contextlib import ExitStack
from math import log, sqrt

import concourse.bass as bass
import numpy as np
from concourse import mybir

F32, F32R, BF16, U32 = mybir.dt.float32, mybir.dt.float32r, mybir.dt.bfloat16, mybir.dt.uint32
ALU = mybir.AluOpType
ACT = mybir.ActivationFunctionType
X = mybir.AxisListType.X

BATCH, CH, IMG, PATCH, D = 64, 3, 224, 16, 128
GRID = IMG // PATCH
DEPTH, HEADS, HD, MLP = 4, 8, 16, 256
TOK = GRID * GRID + 2
TT = TOK // 2
NB = 2
NG = 2
NC = NB * TOK
U = 2 * NB
ROUNDS = 2
ITERS = BATCH // (NB * NG * ROUNDS)
E = 8
F0, F1 = 512 // D, 256 // D
HALF = PATCH // 2
XW = IMG - HALF
CK = 2 * CH * PATCH
EPS = 1e-5
TINY = 1e-24
LIFT = 2.0 ** 20
RING = 6
LH = 4
TW = 3 * TT

VEC = {}
_at = 0
for _n, _w in (("conv_b", 1), ("cls_in", 1), ("cls_out", 1), ("norm_w", 1), ("norm_b", 1), ("ln1_w", DEPTH),
               ("ln1_b", DEPTH), ("ln2_w", DEPTH), ("ln2_b", DEPTH), ("proj_b", DEPTH), ("fc2_b", DEPTH),
               ("fc1_b", 2 * DEPTH), ("qk_b", 4 * DEPTH), ("v_b", 2 * DEPTH), ("ln_g", 1), ("ln_b", 1),
               ("out_g", 1), ("out_b", 1), ("m0_b1", E * F0), ("m0_b2", E), ("m1_b1", E * F1), ("m1_b2", E),
               ("out_scale", 1)):
    VEC[_n] = (_at, _w)
    _at += _w
NV = _at


def constants():
    p = np.arange(TT)[:, None]
    n = np.arange(TOK)[None, :]
    lg = log(0.96)
    c = {}
    c["ident"] = np.eye(D, dtype=np.float32)
    c["center"] = np.eye(D, dtype=np.float32) - np.float32(1.0 / D)
    c["mean"] = np.full((D, D), 1.0 / D, np.float32)
    c["ones"] = np.ones((D, D), np.float32)
    k = np.arange(D)
    c["headsum"] = ((k[:, None] % 32 == 16) & (k[:, None] // 32 == k[None, :] // 32)).astype(np.float32)
    c["expert"] = np.stack([np.repeat(((k % 32 == e) & (k < 96))[:, None], D, 1) for e in range(E)], 1).astype(np.float32)
    c["mask_qk"] = np.stack([np.where(n > p + TT * t, -1e30, -n * lg * sqrt(D)) for t in range(2)], 1).astype(np.float32)
    c["mask_kq"] = np.stack([np.where(n < p + TT * t, -1e30, 0.0 * n) for t in range(2)], 1).astype(np.float32)
    c["key_decay"] = np.concatenate([-(p + TT * t) * lg for t in range(2)], 1).astype(np.float32)
    diff = p - (np.arange(TW)[None, :] - TT)
    c["steps"] = np.maximum(diff - 1, 0).astype(np.float32)
    c["future"] = (diff > 0).astype(np.float32)
    low = (np.arange(D) % 32 >= HD).astype(np.float32)
    c["halves"] = np.stack([-low, 1 - low], 1)
    c["iota"] = np.broadcast_to(np.arange(E, dtype=np.float32), (TT, E)).copy()
    return c


class Group:
    pass


LONG, SHORT, LOW = 0.67, 0.34, 0.09
WIDE_A, READ_A, WIDE_V = 0.47, 0.38, 0.48
SLIM_A, SLIM_V = 0.26, 0.28


def normalized_by_image(add, after):
    sq = [add("act", "square", b, SLIM_A, after[b]) for b in range(NB)]
    st = [add("pe", "stat", b, SHORT, sq[b]) for b in range(NB)]
    r = [add("act", "rstd", b, 0.66, st[b]) for b in range(NB)]
    return [add("dve", "scale", b, SLIM_V, r[b]) for b in range(NB)]


def normalized(add, after, square=True):
    if square:
        after = add("act", "square", 0, WIDE_A, after)
    return add("dve", "scale", 0, WIDE_V, add("act", "rstd", 0, 0.99, add("pe", "stat", 0, LONG, after)))


def centered(add, after):
    after = add("act", "center_read", 0, 0.76, add("pe", "center", 0, LONG, after))
    return normalized(add, after, square=False)


def conv_ops(add, last, n):
    return [add("dve", "conv_h", b, 0.4, add("pe", "conv", b, 2.7, last)) for b in range(NB)]


def qkv_ops(add, last, n):
    prod = [add("pe", "qk", k, LONG, *last) for k in range(4)]
    q = [add("act", "q_read", k, WIDE_A, prod[k]) for k in range(2)]
    vp = add("pe", "v", 0, 0.87, q[0])
    k = [add("act", "k_read", h, WIDE_A, prod[2]) for h in range(4)]
    v = add("act", "v_read", 0, 0.48, vp)
    k += [add("act", "k_read", h, WIDE_A, prod[3]) for h in range(4, HEADS)]
    qb = [add("dve", "q_split", i, 0.95, q[i]) for i in range(2)]
    low = [add("dve", "k_low", h, 0.54, k[h]) for h in range(HEADS)]
    mx = []
    for h in range(HEADS):
        free = [v] if h == 0 else [low[-1]] if h == 1 else [mx[h - 4 // NB]]
        p = add("pe", "smax", h, 0.36, k[h], qb[h // 4], *free)
        mx.append(add("dve", "max", h, 0.88, p))
    mt = add("dve", "max_parts", 0, 0.31, mx[-1])
    rows = add("pe", "max_rows", 0, 0.35, mt)
    return [add("dve", "q_shift", g, 0.54, rows) for g in range(2)][1]


def attn_ops(add, last, n):
    e, av, dn, on = [], [], [], []

    def o_read(i):
        dn.append(add("act", "o_read", i, 0.21, av[i]))

    def headsum(i):
        dn[i] = add("pe", "headsum", i, SHORT, dn[i])

    def o_scale(i):
        on.append(add("dve", "o_scale", i, SLIM_V, add("act", "rsum", i, 0.57, dn[i])))

    beside = {7: (o_read, 0), 9: (headsum, 0), 10: (o_scale, 0), 11: (o_read, 1), 12: (headsum, 1),
              13: (o_scale, 1), 15: (o_read, 2)}
    for k in range(HEADS * NB):
        st = add("pe", "st", k, 4 * LOW, last, *e[k - 2:k - 1] if k >= 2 else [])
        e.append(add("act", "exp", k, READ_A, st, *([av[(k - RING) // 4]] if k >= RING else [])))
        if k >= 5 and k % 4 == 1:
            av.append(add("pe", "av", (k - 5) // 4, 0.82, e[k - 2], *on[:1] if k == 13 else []))
        if k in beside:
            beside[k][0](beside[k][1])
    headsum(2)
    av.append(add("pe", "av", 3, 0.82, e[-1], on[1]))
    o_scale(2)
    o_read(3)
    p = [add("pe", "proj", i, SHORT, on[i], e[-2]) for i in range(2)]
    headsum(3)
    o_scale(3)
    p += [add("pe", "proj", i, SHORT, on[i]) for i in (2, 3)]
    return [add("dve", "proj_add", b, 0.3, p[2 + b]) for b in range(NB)]


def mlp_ops(add, last, n):
    up = [add("pe", "fc1", i, SHORT, last[i // 2]) for i in range(2 * NB)]
    g = [add("act", "gelu", b, 0.62, up[2 * b + 1]) for b in range(NB)]
    dn = [add("pe", "fc2", i, SHORT, g[i // 2]) for i in range(2 * NB)]
    return [add("dve", "fc2_add", b, 0.3, dn[2 * b + 1]) for b in range(NB)]


def retention_ops(add, last, n):
    p = [add("pe", "qk", k, LONG, last) for k in range(2)]
    q = [add("act", "q_read", k, WIDE_A, p[k]) for k in range(2)]
    v = add("act", "v_read", 0, 0.48, add("pe", "v", 0, 0.87, last))
    qb = [add("dve", "q_round", k, 0.27, q[k]) for k in range(2)]
    m = [add("dve", "max", b, 0.45, add("pe", "smax", b, 4 * LOW, qb[1])) for b in range(NB)]
    mt = add("dve", "max_parts", 0, 0.2, m[-1])
    e = [add("act", "exp", b, 0.6, add("pe", "st", b, 2 * SHORT + 8 * 0.06, mt, v)) for b in range(NB)]
    av = add("pe", "av", 0, 4 * SHORT, e[-1])
    sm = add("pe", "probsum", 0, 4 * SHORT, e[-1])
    r = add("act", "rsum", 0, 0.9, sm)
    return add("dve", "o_scale", 0, 1.0, r, av)


def linear_ops(add, last, n):
    p = [add("pe", "qk", k, LONG, last) for k in range(2)]
    vp = add("pe", "v", 0, 0.87, last)
    s0 = add("act", "qk_square", 0, WIDE_A, p[0])
    v = add("act", "v_read", 0, 0.48, vp)
    n0 = add("pe", "norm", 0, LONG, s0)
    s1 = add("act", "qk_square", 1, WIDE_A, n0)
    f0 = add("dve", "floor", 0, WIDE_V, n0)
    n1 = add("pe", "norm", 1, LONG, s1, f0)
    f1 = add("dve", "floor", 1, WIDE_V, n1)
    r0 = add("act", "rnorm", 0, 1.08, f0)
    r1 = add("act", "rnorm", 1, 1.08, f1)
    q = add("dve", "q_scale", 0, WIDE_V, r0)
    k = add("dve", "k_scale", 0, 4 * WIDE_V, r1)
    d, av = [], []
    for i in range(LH * NB):
        st = add("pe", "st", i, 2 * SHORT, k, *d[i - 2:i - 1] if i >= 2 else [])
        d.append(add("dve", "decay", i, 0.55, st, *av[-1:]))
        if i % LH == LH - 1:
            av.append(add("pe", "av", i // LH, 0.82, d[-1], v))
    o = add("act", "o_read", 0, READ_A, av[-1])
    return add("dve", "proj_add", 0, WIDE_V, add("pe", "proj", 0, LONG, o))


def moe_ops(add, last, n):
    ft = F0 if n == 0 else F1
    up_name = "hid_tanh" if n == 0 else "hid_relu"
    gate = add("pe", "gate", 0, 0.59, last)
    gap = add("dve", "top", 0, 1.04, gate)
    eg = add("act", "gap_exp", 0, 0.12, gap)
    parts = add("dve", "gates", 0, 2.46, eg)
    ring, hid, down, term = [], [], [], []

    def bank_free():
        return ring[-2:-1]

    def fill_down(m):
        e = m // ft
        down.append(add("pe", "down", m, LONG, hid[m], *([term[e - 2]] if e >= 2 else [])))
        if m % ft == ft - 1:
            t = add("dve", "term", e, 0.55, down[-1], cb[e])
            term.append(t if e == 0 else add("dve", "acc", e, WIDE_V, t))

    cb = []
    for e in range(E):
        for f in range(ft):
            m = e * ft + f
            u = add("pe", "up", m, LONG, last, *bank_free())
            hid.append(add("act", up_name, m, WIDE_A, u, *([down[m - 4]] if m >= 4 else [])))
            ring.append(hid[-1])
            if m >= 2:
                fill_down(m - 2)
            if m == 1:
                ct = add("act", "ct_read", 0, READ_A, add("pe", "gateT", 0, 0.17, parts))
        c = add("pe", "spread", e, 0.18, ct, *bank_free())
        cb.append(add("act", "spread_read", e, READ_A, c, *([term[e - 2]] if e >= 2 else [])))
        ring.append(cb[-1])
    fill_down(E * ft - 2)
    fill_down(E * ft - 1)
    return term[-1]


def signals(kind, n):
    ln = {"sq": 1, "stat_psum": 1, "log": 1, "rstd": 1, "z": 1}
    ft = F0 if n == 0 else F1
    by_image = {name: NB * k for name, k in ln.items()}
    return {
        "conv": {"conv_psum": NB, "h": NB + 1, "zeroed": 6},
        "ln_h": by_image,
        "ln_z": ln,
        "ln_full": ln | {"cen_psum": 1, "cen": 1},
        "qkv": {"qk_psum": 4, "q": 2, "q_high": 2, "q_parts": 2, "k": HEADS, "k_low": HEADS, "v_psum": 1, "v": 1,
                "smax_psum": HEADS, "max": HEADS, "mt_hi": 1, "mt": 1, "mrow_psum": 2, "q_aug": 2},
        "attn": {"st_psum": HEADS * NB, "exp": HEADS * NB, "av_psum": 2 * NB, "o": 2 * NB, "sum_psum": 2 * NB,
                 "log": 2 * NB, "rsum": 2 * NB, "o_norm": 2 * NB, "proj_psum": NB, "h": NB},
        "mlp": {"fc1_psum": 2 * NB, "hid": 2 * NB, "fc2_psum": NB, "h": NB},
        "tower_out": {"affine": 1, "h": 1, "zeroed": 1},
        "retention": {"qk_psum": 2, "q": 2, "q_bf": 2, "v_psum": 1, "v": 1, "smax_psum": NB, "max": NB, "mt_hi": 1,
                      "mt": 1, "st_psum": NB, "exp": NB, "av_psum": 1, "sum_psum": 1, "log": 1, "rsum": 1,
                      "o_norm": 1, "h": 1},
        "linear": {"qk_psum": 2, "sq": 2, "stat_psum": 2, "floor": 2, "log": 2, "rstd": 2, "q": 1, "k": LH,
                   "v_psum": 1, "v": 1, "st_psum": LH * NB, "decayed": LH * NB, "av_psum": NB, "o": 1, "proj_psum": 1,
                   "h": 1},
        "moe": {"gate_psum": 1, "logit": 1, "top": U, "topi": U, "gap": 1, "egap": 1, "g": 9, "mid": 1, "parts": 1,
                "gateT_psum": 1, "gateT": 1, "up_psum": E * (ft + 1), "up_read": E * (ft + 1), "down": E * ft,
                "term": E, "acc": E - 1},
        "moe0_out": {"s": 1, "sq": 1, "stat_psum": 1, "log": 1, "rstd": 1, "z": 1, "affine": 1, "h": 1},
        "moe1_out": {"h": 1, "out_psum": 1, "out_sb": 1},
    }[kind]


def stream():
    ops, at, last = [], {}, None

    def step(kind, n, rnd, build):
        nonlocal last
        begins = dict(at)

        def add(engine, name, i, us, *follows):
            ops.append((engine, name, i, us, [f for f in follows if f is not None], kind, n, rnd, begins))
            return len(ops) - 1

        last = build(add)
        for name, k in signals(kind, n).items():
            at[name] = at.get(name, 0) + k

    for rnd in range(ROUNDS):
        step("conv", 0, rnd, lambda add: conv_ops(add, last, 0))
        for l in range(DEPTH):
            step("ln_h", l, rnd, lambda add: normalized_by_image(add, last))
            step("qkv", l, rnd, lambda add: qkv_ops(add, last, l))
            step("attn", l, rnd, lambda add: attn_ops(add, last, l))
            step("ln_h", l, rnd, lambda add: normalized_by_image(add, last))
            step("mlp", l, rnd, lambda add: mlp_ops(add, last, l))
        step("ln_h", 0, rnd, lambda add: normalized_by_image(add, last))
        step("tower_out", 0, rnd, lambda add: add("dve", "tower_out", 0, 0.6, *last))
        step("ln_full", 0, rnd, lambda add: centered(add, last))
        step("retention", 0, rnd, lambda add: retention_ops(add, last, 0))
        step("ln_full", 1, rnd, lambda add: centered(add, last))
        step("ln_z", 0, rnd, lambda add: normalized(add, last))
        step("moe", 0, rnd, lambda add: moe_ops(add, last, 0))
        step("moe0_out", 0, rnd, lambda add: add(
            "dve", "out_add", 0, WIDE_V,
            add("act", "affine", 0, WIDE_A, normalized(add, add("dve", "sum_z", 0, WIDE_V, last)))))
        step("ln_full", 2, rnd, lambda add: centered(add, last))
        step("linear", 0, rnd, lambda add: linear_ops(add, last, 0))
        step("ln_full", 3, rnd, lambda add: centered(add, last))
        step("moe", 1, rnd, lambda add: moe_ops(add, last, 1))
        step("moe1_out", 0, rnd, lambda add: add(
            "act", "out_read", 0, 0.6, add("pe", "out_turn", 0, 0.43, add("dve", "out_add", 0, WIDE_V, last))))
    return ops, sorted(at)


TABLES = {"rstd": "log", "exp": "log", "rsum": "log", "rnorm": "log", "gap_exp": "log", "gelu": "gelu", "hid_tanh": "tanh"}


HANDOVER = {("pe", "act"): 0.2, ("pe", "dve"): 0.2, ("act", "pe"): 0.28, ("dve", "pe"): 0.28, ("act", "dve"): 0.15,
            ("dve", "act"): 0.15, ("dve", "dve"): 0.13, ("act", "act"): 0.05, ("pe", "pe"): 0.0}
YIELD = 0.08
AHEAD = 16.0
FAVOUR = {"conv": -187, "ln_h": 99, "qkv": 207, "attn": -518, "mlp": -37, "ln_full": 45, "retention": 113, "ln_z": -5,
          "moe": 55, "moe0_out": 337, "linear": -52}
LOAD_COUNTS = 0.0
TABLE_LOAD = 1.4


def merged(ops):
    path = [op[3] for op in ops]
    for i in range(len(ops) - 1, -1, -1):
        for f in ops[i][4]:
            path[f] = max(path[f], ops[f][3] + HANDOVER[ops[f][0], ops[i][0]] + path[i])
    queues = [{e: [i for i, op in enumerate(ops) if op[0] == e] for e in ("pe", "act", "dve")} for _ in range(NG)]
    end = [{} for _ in range(NG)]
    free, table, order = {"pe": 0.0, "act": 0.0, "dve": 0.0}, None, []
    while any(q for qs in queues for q in qs.values()):
        heads = []
        for g in range(NG):
            for e, q in queues[g].items():
                if not q or any(f not in end[g] for f in ops[q[0]][4]):
                    continue
                _, name, _, us, follows, kind, *_ = ops[q[0]]
                ready = max([end[g][f] + HANDOVER[ops[f][0], e] for f in follows], default=0.0)
                need = TABLES.get(name)
                load = TABLE_LOAD if e == "act" and need and need != table else 0.0
                start = max(free[e], ready)
                weight = path[q[0]] + FAVOUR.get(kind, 0) + (AHEAD if g == 0 else 0.0)
                heads.append((start + LOAD_COUNTS * load, g, e, weight, start + load, us, need))
        first = best = min(heads, key=lambda head: head[:3])
        for other in heads:
            if other[2] == first[2] and other[0] < first[0] + YIELD * first[5] + 1e-9 and other[3] > best[3]:
                best = other
        _, g, e, _, start, us, need = best
        if e == "pe" and start - free[e] > 1.5:
            us *= 1.5
        i = queues[g][e].pop(0)
        free[e] = end[g][i] = start + us
        if e == "act" and need:
            table = need
        order.append((g, ops[i]))
    return order


def tower_kernel(nc, x, conv_w, pos_t, vecs, w_qk, w_v, w_v_pad, w_p, w_fc1, w_fc2, w_ret, w_lin, coef, gates, gate_b,
                 decay_logits, m0_w1, m0_w2, m1_w1, m1_w2, consts, out):
    OPS, NAMES = stream()
    ORDER = merged(OPS)

    with ExitStack() as ctx:
        def sb(name, shape, dt=F32):
            return ctx.enter_context(nc.sbuf_tensor(name, shape, dt))

        def sem(name):
            return ctx.enter_context(nc.semaphore(name))

        cw = sb("cw", [CK, HALF, D])
        vec = sb("vec", [D, NV])
        wqk = sb("wqk", [D, DEPTH, 4, D])
        wv = sb("wv", [D, DEPTH, D])
        wp = sb("wp", [D, DEPTH, 2, D])
        fc1 = sb("fc1", [D, DEPTH, MLP])
        fc2 = sb("fc2", [D, DEPTH, 2, D])
        wret = sb("wret", [D, 3, D])
        wlin = sb("wlin", [D, 2, D])
        wvb = sb("wvb", [D, D])
        wob = sb("wob", [D, D])
        wg = sb("wg", [D, 2, E])
        gb = sb("gb", [TT, 2, E])
        w1 = [sb("w1_0", [D, E * F0, D]), sb("w1_1", [D, E * F1, D])]
        w2 = [sb("w2_0", [D, E * F0, D]), sb("w2_1", [D, E * F1, D])]
        posb = sb("posb", [D, TOK])
        ident = sb("ident", [D, D])
        identb = sb("identb", [D, D], BF16)
        center = sb("center", [D, D])
        meanm = sb("meanm", [D, D])
        ones = sb("ones", [D, D])
        headsum = sb("headsum", [D, D])
        expertb = sb("expertb", [D, E, D], BF16)
        mask_qk = sb("mask_qk", [TT, 2, TOK], BF16)
        mask_kq = sb("mask_kq", [TT, 2, TOK], BF16)
        key_decay = sb("key_decay", [TT, 2])
        decay = sb("decay", [TT, LH, TW])
        iota = sb("iota", [TT, E])
        halves = sb("halves", [D, 2])
        eps = sb("eps", [D, 2])

        def v(name, k=0, n=1):
            return vec[:, VEC[name][0] + k:VEC[name][0] + k + n]

        KW = HEADS * NC
        groups = []
        for g in range(NG):
            G = Group()
            groups.append(G)
            t = "AB"[g]
            place = -(-nc.sbuf_base // 32) * 32
            G.keys = sb(f"keys{t}", [D, 2 * KW], F32R)
            G.arena = nc.alloc_sbuf_tensor_at(f"arena{t}", [D, 2 * KW], F32, offset=place)
            G.k_high, G.k_low = (G.keys[:, i * KW:(i + 1) * KW].rearrange("p (h n) -> p h n", h=HEADS) for i in range(2))
            assert NB * GRID * XW <= 2 * KW
            G.x = G.arena[:, 0:NB * GRID * XW].rearrange("p (b y w) -> p b y w", b=NB, y=GRID)
            G.k = G.arena[:, 0:KW].rearrange("p (h n) -> p h n", h=HEADS)
            G.p = G.arena[:, KW:2 * KW].rearrange("p (s n) -> p s n", s=HEADS)
            G.q_parts = sb(f"q_parts{t}", [D, 4, NC], F32R)
            G.q = sb(f"q{t}", [D, 2, NC])
            G.cb = G.q
            G.o = G.q
            G.q_bf = sb(f"q_bf{t}", [D, 2, NC], BF16)
            G.acc = G.q_bf[:, :, :].rearrange("p g n -> p (g n)").bitcast(F32)
            G.h = sb(f"h{t}", [D, NC])
            G.z = sb(f"z{t}", [D, NC])
            G.va = sb(f"va{t}", [TT, U, HEADS, 32])
            work = sb(f"work{t}", [D, RING, NC])
            G.ring = work
            G.hid, G.u, G.sq = work[:, 0:4], work[:, 4], work[:, 5]
            hflat = G.hid.rearrange("p f n -> p (f n)")
            G.vr = hflat[0:TT, 0:U * D].rearrange("p (u d) -> p u d", u=U)
            G.ob = hflat[0:TT, U * D:2 * U * D].rearrange("p (u d) -> p u d", u=U)
            G.negm = sb(f"negm{t}", [TT, HEADS, NB, 2])
            G.mt = sb(f"mt{t}", [TT, U, 2, D], BF16)
            G.lg = sb(f"lg{t}", [TT, 7, U, E])
            G.ix = sb(f"ix{t}", [TT, U, E], U32)
            G.sc = sb(f"sc{t}", [TT, 5, U, 2])
            G.cc = sb(f"cc{t}", [TT, U, D], BF16)
            G.ct = sb(f"ct{t}", [D, NC], BF16)
            G.ps = ctx.enter_context(nc.psum_tensor(f"ps{t}", [D, 4, 512], F32))
            G.x_in = sem(f"x_in_{t}")
            G.s = {n: sem(f"{n}_{t}") for n in NAMES}
            G.out_done = sem(f"out_done_{t}")
            assert G.out_done.num - G.x_in.num == len(NAMES) + 1
        s_load, s_fold, s_ps, s_const = sem("load"), sem("fold"), sem("fold_psum"), sem("const")

        def load_images(eng, G, i):
            for b in range(NB):
                for half in range(2):
                    for c in range(CH):
                        p = (half * CH + c) * PATCH
                        src = x[i * NB + b, c].rearrange("(y r) w -> r y w", r=PATCH)
                        eng.dma_start(G.x[p:p + PATCH, b], src[:, :, half * HALF:half * HALF + XW]).then_inc(G.x_in, 16)

        XWAIT = NB * 2 * CH * 16

        st_expert = groups[1].arena[:, 0:E * D].rearrange("p (e d) -> p e d", e=E)
        st_mqk = groups[1].arena[0:TT, 1024:1024 + 2 * TOK].rearrange("p (t n) -> p t n", t=2)
        st_mkq = groups[1].arena[0:TT, 1424:1424 + 2 * TOK].rearrange("p (t n) -> p t n", t=2)
        st_pos = groups[1].arena[:, 1824:1824 + TOK]
        st_steps = groups[1].arena[0:TT, 2024:2024 + TW]
        st_future = groups[1].arena[0:TT, 2324:2324 + TW]
        st_wvp = groups[1].arena[:, 2624:2624 + DEPTH * 2 * D].rearrange("p (l g d) -> p l g d", l=DEPTH, g=2)
        st_coef = groups[1].arena[:, 3648:3648 + 3 * D].rearrange("p (c d) -> p c d", c=3)
        st_mean = groups[1].arena[:, 4032:4032 + 64]
        st_dl = groups[1].arena[0:TT, 4096:4096 + 3 * LH].rearrange("p (k h) -> p k h", k=3)
        st_vb = groups[1].arena[:, 4112:4112 + 2 * DEPTH]
        psA, psB = groups[0].ps, groups[1].ps

        with nc.Block() as block:
            @block.sync
            def _(sp):
                n = 0
                for half in range(2):
                    src = conv_w.rearrange("(k h j) d -> h k j d", h=2, j=HALF)[half]
                    sp.dma_start(cw[half * CK // 2:(half + 1) * CK // 2], src).then_inc(s_load, 16)
                for dst, src in ((vec[:, :], vecs), (wqk[:, :, :, :], w_qk), (wv[:, :, :], w_v), (st_wvp, w_v_pad),
                                 (wp[:, :, :, :], w_p), (fc1[:, :, :], w_fc1), (fc2[:, :, :, :], w_fc2),
                                 (wret[:, :, :], w_ret), (wlin[:, :, :], w_lin), (st_coef, coef), (wg[:, :, :], gates),
                                 (gb[:, 1, :], gate_b), (st_dl[:, 0], decay_logits),
                                 (w1[0][:, :, :], m0_w1), (w2[0][:, :, :], m0_w2), (w1[1][:, :, :], m1_w1),
                                 (w2[1][:, :, :], m1_w2), (ident[:, :], consts["ident"]),
                                 (center[:, :], consts["center"]), (meanm[:, :], consts["mean"]),
                                 (ones[:, :], consts["ones"]), (headsum[:, :], consts["headsum"]),
                                 (st_expert, consts["expert"]), (st_mqk, consts["mask_qk"]),
                                 (st_mkq, consts["mask_kq"]), (key_decay[:, :], consts["key_decay"]),
                                 (st_steps, consts["steps"]), (st_future, consts["future"]),
                                 (iota[:, :], consts["iota"]), (halves[:, :], consts["halves"]), (st_pos[:, 1:TOK], pos_t)):
                    sp.dma_start(dst, src).then_inc(s_load, 16)
                    n += 1
                load_images(sp, groups[0], 0)
                sp.wait_ge(s_load, 16 * (n + 2))
                sp.wait_ge(groups[0].x_in, XWAIT)

            @block.gpsimd
            def _(pool):
                for G in groups:
                    pool.memset(G.va[:, :, :, :], 0.0)
                    pool.memset(G.mt[:, :, :, :], 0.0)
                    pool.memset(G.cc[:, :, :], 0.0)
                pool.memset(eps[:, 0:1], EPS)
                pool.memset(eps[:, 1:2], 0.5 * log(LIFT)).then_inc(s_const, 1)
                pool.wait_ge(s_const, 1)

        with nc.Block() as block:
            @block.vector
            def _(dve):
                for G in groups:
                    dve.memset(G.va[:, :, :, HD:HD + 1], 1.0).then_inc(s_const, 1)
                dve.wait_ge(s_const, 3)
                for G in groups:
                    for b in range(NB):
                        dve.memset(G.va[0:1, 2 * b, :, :], 0.0)
                dve.tensor_copy(identb[:, :], ident[:, :])
                dve.tensor_copy(expertb[:, :, :], st_expert)
                dve.tensor_copy(mask_qk[:, :, :], st_mqk)
                dve.tensor_copy(mask_kq[:, :, :], st_mkq)
                for w, n, at in ((cw[:, :, :], HALF, 0), (wp[:, :, :, :].rearrange("p l g d -> p (l g) d"), 2 * DEPTH, 8),
                                 (fc2[:, :, :, :].rearrange("p l g d -> p (l g) d"), 2 * DEPTH, 16),
                                 (w2[0][:, :, :], E * F0, 24)):
                    k = w.shape[0]
                    dve.tensor_reduce(st_mean[0:k, at:at + n], w, X, ALU.add).then_inc(s_fold, 1)
                dve.wait_ge(s_fold, 4)
                dve.tensor_scalar(st_mean[:, 8:56], st_mean[:, 8:56], 1.0 / D, None, ALU.mult)
                dve.tensor_scalar(st_mean[0:CK, 0:8], st_mean[0:CK, 0:8], 1.0 / D, None, ALU.mult).then_inc(s_fold, 1)
                dve.wait_ge(s_fold, 5)
                for w, n, at in ((cw[:, :, :], HALF, 0), (wp[:, :, :, :].rearrange("p l g d -> p (l g) d"), 2 * DEPTH, 8),
                                 (fc2[:, :, :, :].rearrange("p l g d -> p (l g) d"), 2 * DEPTH, 16),
                                 (w2[0][:, :, :], E * F0, 24)):
                    k = w.shape[0]
                    dve.tensor_tensor(w, w, st_mean[0:k, at:at + n].unsqueeze(2).to_broadcast([k, n, D]), ALU.subtract)
                dve.tensor_scalar(st_pos[:, 2:TOK], st_pos[:, 2:TOK], v("conv_b"), None, ALU.add)
                dve.tensor_tensor(st_pos[:, 1:2], st_pos[:, 1:2], v("cls_in"), ALU.add)
                dve.memset(st_pos[:, 0:1], 0.0).then_inc(s_fold, 1)
                dve.wait_ge(s_fold, 6)

            @block.scalar
            def _(act):
                act.preload_act_table_set("natural_log_exp_and_others")
                act.activation(st_dl[:, 1], st_dl[:, 0], ACT.Exp, scale=-1.0).then_inc(s_ps, 1)
                act.wait_ge(s_ps, 1)
                act.activation(st_dl[:, 2], st_dl[:, 1], ACT.Ln, bias=ones[0:TT, 0:1]).then_inc(s_ps, 1)
                act.wait_ge(s_ps, 2)
                act.activation(st_dl[:, 1], st_dl[:, 2], ACT.Copy, scale=-1.0).then_inc(s_ps, 1)
                act.wait_ge(s_ps, 3)
                for h in range(LH):
                    act.activation(decay[:, h, :], st_steps, ACT.Exp, scale=st_dl[:, 1, h:h + 1]).then_inc(s_ps, 1)
                act.wait_ge(s_ps, 3 + LH)

        with nc.Block() as block:
            @block.tensor
            def _(pe):
                col = 0
                for l in range(DEPTH):
                    for g in range(4):
                        pe.matmul(psA[:, 0, col:col + 1], wqk[:, l, g, :], v("ln1_b", l), start=True, stop=True)
                        col += 1
                for l in range(DEPTH):
                    for g in range(2):
                        pe.matmul(psA[:, 0, col:col + 1], st_wvp[:, l, g, :], v("ln1_b", l), start=True, stop=True)
                        col += 1
                for l in range(DEPTH):
                    for f in range(2):
                        pe.matmul(psA[:, 0, col:col + 1], fc1[:, l, f * D:(f + 1) * D], v("ln2_b", l), start=True, stop=True)
                        col += 1
                for f in range(E * F0):
                    pe.matmul(psA[:, 0, col:col + 1], w1[0][:, f, :], v("ln_b"), start=True, stop=True)
                    col += 1
                pe.matmul(psA[:, 1, 0:TOK], center[:, :], st_pos, start=True, stop=True)
                pe.matmul(psA[0:TT, 2, 0:E], v("ln_b").to_broadcast([D, TT]), wg[:, 0, :], start=True, stop=True)
                pe.matmul(psA[:, 3, 0:E], center[:, :], v("m0_b2", 0, E), start=True, stop=True)
                pe.matmul(psB[:, 0, 0:DEPTH], center[:, :], v("fc2_b", 0, DEPTH), start=True, stop=True)
                pe.matmul(psB[:, 1, 0:D], st_coef[:, 0, :], st_coef[:, 1, :], start=True, stop=True)
                pe.matmul(psB[:, 2, 0:D], st_coef[:, 2, :], st_coef[:, 0, :], start=True, stop=True).then_inc(s_ps, 1)
                pe.wait_ge(s_ps, 4 + LH)

            @block.vector
            def _(dve):
                for h in range(LH):
                    last = dve.tensor_tensor(decay[:, h, :], decay[:, h, :], st_future, ALU.mult)
                last.then_inc(s_fold, 1)
                dve.wait_ge(s_fold, 7)

        with nc.Block() as block:
            @block.vector
            def _(dve):
                n = 4 * DEPTH
                dve.tensor_tensor(v("qk_b", 0, n), v("qk_b", 0, n), psA[:, 0, 0:n], ALU.add)
                dve.tensor_tensor(st_vb, v("v_b", 0, 2 * DEPTH), psA[:, 0, n:n + 2 * DEPTH], ALU.add)
                n += 2 * DEPTH
                dve.tensor_tensor(v("fc1_b", 0, 2 * DEPTH), v("fc1_b", 0, 2 * DEPTH), psA[:, 0, n:n + 2 * DEPTH], ALU.add)
                n += 2 * DEPTH
                dve.tensor_tensor(v("m0_b1", 0, E * F0), v("m0_b1", 0, E * F0), psA[:, 0, n:n + E * F0], ALU.add)
                dve.tensor_copy(posb[:, :], psA[:, 1, 0:TOK])
                dve.tensor_copy(gb[:, 0, :], psA[0:TT, 2, 0:E])
                dve.tensor_copy(v("m0_b2", 0, E), psA[:, 3, 0:E])
                dve.tensor_copy(v("fc2_b", 0, DEPTH), psB[:, 0, 0:DEPTH])
                dve.tensor_copy(wvb[:, :], psB[:, 1, 0:D])
                dve.tensor_scalar(wob[:, :], psB[:, 2, 0:D], v("out_scale"), None, ALU.mult)
                for l in range(DEPTH):
                    dve.tensor_scalar(wqk[:, l, :, :], wqk[:, l, :, :], v("ln1_w", l), None, ALU.mult)
                    dve.tensor_scalar(wv[:, l, :], wv[:, l, :], v("ln1_w", l), None, ALU.mult)
                    dve.tensor_scalar(fc1[:, l, :], fc1[:, l, :], v("ln2_w", l), None, ALU.mult)
                dve.tensor_scalar(wg[:, 0, :], wg[:, 0, :], v("ln_g"), None, ALU.mult)
                dve.tensor_scalar(w1[0][:, :, :], w1[0][:, :, :], v("ln_g"), None, ALU.mult).then_inc(s_fold, 1)
                dve.wait_ge(s_fold, 8)

        with nc.Block() as block:
            @block.tensor
            def _(pe):
                for l in range(DEPTH):
                    o = psA[:, 0, l:l + 1]
                    pe.matmul(o, wp[:, l, 0, :], st_vb[:, 2 * l:2 * l + 1], start=True, stop=False)
                    pe.matmul(o, wp[:, l, 1, :], st_vb[:, 2 * l + 1:2 * l + 2], start=False, stop=False)
                    last = pe.matmul(o, center[:, :], v("proj_b", l), start=False, stop=True)
                last.then_inc(s_ps, 1)
                pe.wait_ge(s_ps, 5 + LH)

        with nc.Block() as block:
            @block.vector
            def _(dve):
                dve.tensor_copy(v("proj_b", 0, DEPTH), psA[:, 0, 0:DEPTH]).then_inc(s_fold, 1)
                dve.wait_ge(s_fold, 9)

            @block.sync
            def _(sp):
                load_images(sp, groups[1], 1)
                sp.wait_ge(groups[1].x_in, XWAIT)

        with nc.Block() as block:
            @block.gpsimd
            def _(pool):
                for G in groups:
                    pool.sem_clear(G.x_in)

        def wait(eng, sem_, count):
            if count > 0:
                eng.wait_ge(sem_, count)

        def real(ap):
            return ap.rearrange("p (b n) -> p b n", b=NB)[:, :, 1:TOK]

        ALL = slice(0, NC)

        def image(b):
            return slice(b * TOK, (b + 1) * TOK)

        def piece(G, first, b, k=0):
            return G.ps[:, first + b, k * TOK:(k + 1) * TOK]

        def bank(G, k):
            return G.ps[:, k, 0:NC]

        with nc.Fori(0, ITERS) as it:
            with nc.Block() as block:
                @block.tensor
                def _(pe):
                    for g, (engine, op, i, _, _, kind, n, rnd, counts) in ORDER:
                        if engine != "pe":
                            continue
                        G, S = groups[g], groups[g].s
                        at = {name: counts.get(name, 0) for name in NAMES}
                        ft = F0 if n == 0 else F1
                        src = G.u if kind == "moe" and n == 0 else G.z
                        if op == "conv":
                            if rnd > 0 and i == 0:
                                pe.wait_ge(G.x_in, XWAIT * rnd)
                                pe.wait_ge(S["out_sb"], at["out_sb"])
                            for j in range(HALF):
                                mm = pe.matmul(G.ps[:, i, 0:GRID * GRID], cw[:, j, :],
                                               G.x[0:CK, i, :, j:j + PATCH * (GRID - 1) + 1:PATCH],
                                               start=(j == 0), stop=(j == HALF - 1))
                            mm.then_inc(S["conv_psum"], 1)
                        elif op == "stat":
                            pe.wait_ge(S["sq"], at["sq"] + i + 1)
                            cols = image(i) if kind == "ln_h" else ALL
                            o = piece(G, 0, i) if kind == "ln_h" else bank(G, 0)
                            pe.matmul(o, meanm[:, :], G.sq[:, cols], start=True, stop=True)\
                                .then_inc(S["stat_psum"], 1)
                        elif op == "center":
                            pe.wait_ge(S["h"], at["h"])
                            pe.matmul(bank(G, 1), center[:, :], G.h[:, :], start=True, stop=True).then_inc(S["cen_psum"], 1)
                        elif op == "qk":
                            w = wqk[:, n, i, :] if kind == "qkv" else wret[:, i, :] if kind == "retention" else wlin[:, i, :]
                            pe.wait_ge(S["z"], at["z"])
                            pe.matmul(bank(G, i), w, G.z[:, :], start=True, stop=True).then_inc(S["qk_psum"], 1)
                        elif op == "v":
                            w = wv[:, n, :] if kind == "qkv" else wret[:, 2, :] if kind == "retention" else wvb[:, :]
                            b = 0 if kind == "qkv" else 2
                            pe.wait_ge(S["z"], at["z"])
                            if kind == "qkv":
                                pe.wait_ge(S["q"], at["q"] + 1)
                            for u in range(U):
                                mm = pe.matmul(G.ps[0:TT, b, u * D:(u + 1) * D], G.z[:, u * TT:(u + 1) * TT], w,
                                               start=True, stop=True)
                            mm.then_inc(S["v_psum"], 1)
                        elif op == "smax" and kind == "qkv":
                            pe.wait_ge(S["k"], at["k"] + i + 1)
                            pe.wait_ge(S["q_parts"], at["q_parts"] + 1 + i // 4)
                            pe.wait_ge(S["v"], at["v"] + 1)
                            if (i + 1) * NB > 2:
                                pe.wait_ge(S["k"], at["k"] + HEADS)
                                pe.wait_ge(S["k_low"], at["k_low"] + HEADS)
                            if i * NB >= 4:
                                pe.wait_ge(S["max"], at["max"] + i - 4 // NB + 1)
                            for b in range(NB):
                                for qt in range(2):
                                    mm = pe.matmul(G.ps[0:TT, (i * NB + b) % 4, qt * TOK:(qt + 1) * TOK],
                                                   G.q_parts[:, i // 4, b * TOK + qt * TT:b * TOK + (qt + 1) * TT],
                                                   G.k_high[:, i, b * TOK:(b + 1) * TOK], start=True, stop=True)
                            mm.then_inc(S["smax_psum"], 1)
                        elif op == "max_rows":
                            pe.wait_ge(S["mt"], at["mt"] + 1)
                            for grp in range(2):
                                for u in range(U):
                                    mm = pe.matmul(G.ps[:, grp, u * TT:(u + 1) * TT], G.mt[:, u, grp, :],
                                                   identb[0:TT, 0:TT], start=True, stop=True)
                                mm.then_inc(S["mrow_psum"], 1)
                        elif op == "st" and kind == "attn":
                            grp, rest = divmod(i, 4 * NB)
                            b, j = divmod(rest, 4)
                            pe.wait_ge(S["q_aug"], at["q_aug"])
                            if i >= 2:
                                pe.wait_ge(S["exp"], at["exp"] + i - 1)
                            for kt in range(2):
                                o = G.ps[0:TT, i % 2, kt * TOK:(kt + 1) * TOK]
                                keys_of = slice(b * TOK + kt * TT, b * TOK + (kt + 1) * TT)
                                pe.matmul(o, G.k_high[:, 4 * grp + j, keys_of],
                                          G.q_parts[:, grp, b * TOK:(b + 1) * TOK], start=True, stop=False)
                                mm = pe.matmul(o, G.k_low[:, 4 * grp + j, keys_of],
                                               G.q_parts[:, 2 + grp, b * TOK:(b + 1) * TOK], start=False, stop=True)
                            mm.then_inc(S["st_psum"], 1)
                        elif op == "av" and kind == "attn":
                            grp, b = divmod(i, NB)
                            pe.wait_ge(S["v"], at["v"])
                            pe.wait_ge(S["exp"], at["exp"] + 4 * i + 4)
                            if grp > 0:
                                pe.wait_ge(S["o_norm"], at["o_norm"] + b + 1)
                            for kt in range(2):
                                for j in range(4):
                                    mm = pe.matmul(piece(G, 2, b, grp)[32 * j:32 * j + 32],
                                                   G.va[:, 2 * b + kt, 4 * grp + j, :],
                                                   G.ring[0:TT, (4 * i + j) % RING, kt * TOK:(kt + 1) * TOK],
                                                   start=(kt == 0), stop=(kt == 1))
                            mm.then_inc(S["av_psum"], 1)
                        elif op == "headsum":
                            grp, b = divmod(i, NB)
                            pe.wait_ge(S["o"], at["o"] + i + 1)
                            pe.matmul(piece(G, 2, b, grp), headsum[:, :], G.o[:, grp, image(b)],
                                      start=True, stop=True).then_inc(S["sum_psum"], 1)
                        elif op == "proj" and kind == "attn":
                            grp, b = divmod(i, NB)
                            pe.wait_ge(S["exp"], at["exp"] + HEADS * NB)
                            pe.wait_ge(S["o_norm"], at["o_norm"] + i + 1)
                            mm = pe.matmul(piece(G, 0, b), wp[:, n, grp, :], G.o[:, grp, image(b)],
                                           start=(grp == 0), stop=(grp == 1))
                            if grp == 1:
                                mm.then_inc(S["proj_psum"], 1)
                        elif op == "fc1":
                            b, f = divmod(i, 2)
                            pe.wait_ge(S["z"], at["z"] - (NB - 1 - b))
                            pe.matmul(piece(G, 0, b, f), fc1[:, n, f * D:(f + 1) * D], G.z[:, image(b)],
                                      start=True, stop=True).then_inc(S["fc1_psum"], 1)
                        elif op == "fc2":
                            b, f = divmod(i, 2)
                            pe.wait_ge(S["hid"], at["hid"] + i + 1)
                            mm = pe.matmul(piece(G, 2, b), fc2[:, n, f, :], G.hid[:, f, image(b)],
                                           start=(f == 0), stop=(f == 1))
                            if f == 1:
                                mm.then_inc(S["fc2_psum"], 1)
                        elif op == "smax" and kind == "retention":
                            pe.wait_ge(S["q_bf"], at["q_bf"] + 2)
                            pe.wait_ge(S["q"], at["q"] + 2)
                            for qt in range(2):
                                o = G.ps[0:TT, i, qt * TOK:(qt + 1) * TOK]
                                pe.matmul(o, G.q_bf[:, 0, i * TOK + qt * TT:i * TOK + (qt + 1) * TT],
                                          G.q_bf[:, 1, i * TOK:(i + 1) * TOK], start=True, stop=False)
                                mm = pe.matmul(o, identb[0:TT, 0:TT], mask_qk[:, qt, :], start=False, stop=True)
                            mm.then_inc(S["smax_psum"], 1)
                        elif op == "st" and kind == "retention":
                            pe.wait_ge(S["v"], at["v"] + 1)
                            pe.wait_ge(S["mt"], at["mt"] + 1)
                            for kt in range(2):
                                o = G.ps[0:TT, 2 + i, kt * TOK:(kt + 1) * TOK]
                                pe.matmul(o, G.q[:, 1, i * TOK + kt * TT:i * TOK + (kt + 1) * TT],
                                          G.q[:, 0, i * TOK:(i + 1) * TOK], start=True, stop=False)
                                pe.matmul(o, identb[0:TT, 0:TT], mask_kq[:, kt, :], start=False, stop=False)
                                for qt in range(2):
                                    for part in range(2):
                                        mm = pe.matmul(o[:, qt * TT:(qt + 1) * TT],
                                                       G.mt[:, 2 * i + qt, 0, 16 + part:17 + part].to_broadcast([TT, TT]),
                                                       identb[0:TT, 0:TT], start=False, stop=(qt == 1 and part == 1))
                            mm.then_inc(S["st_psum"], 1)
                        elif op in ("av", "probsum") and kind == "retention":
                            pe.wait_ge(S["exp"], at["exp"] + NB)
                            for b in range(NB):
                                for kt in range(2):
                                    w = G.vr[:, 2 * b + kt, :] if op == "av" else ones[0:TT, :]
                                    mm = pe.matmul(G.ps[:, 0 if op == "av" else 1, b * TOK:(b + 1) * TOK], w,
                                                   G.p[0:TT, b, kt * TOK:(kt + 1) * TOK], start=(kt == 0), stop=(kt == 1))
                            mm.then_inc(S["av_psum" if op == "av" else "sum_psum"], 1)
                        elif op == "norm":
                            pe.wait_ge(S["sq"], at["sq"] + i + 1)
                            if i == 1:
                                pe.wait_ge(S["floor"], at["floor"] + 1)
                            pe.matmul(bank(G, 3), ones[:, :], G.sq, start=True, stop=True).then_inc(S["stat_psum"], 1)
                        elif op == "st" and kind == "linear":
                            b, h = divmod(i, LH)
                            pe.wait_ge(S["q"], at["q"] + 1)
                            pe.wait_ge(S["k"], at["k"] + LH)
                            if i >= 2:
                                pe.wait_ge(S["decayed"], at["decayed"] + i - 1)
                            for kt in range(2):
                                mm = pe.matmul(G.ps[0:TT, i % 2, kt * TOK:(kt + 1) * TOK],
                                               G.k[:, h, b * TOK + kt * TT:b * TOK + (kt + 1) * TT],
                                               G.q[:, 0, b * TOK:(b + 1) * TOK], start=True, stop=True)
                            mm.then_inc(S["st_psum"], 1)
                        elif op == "av" and kind == "linear":
                            pe.wait_ge(S["v"], at["v"] + 1)
                            pe.wait_ge(S["decayed"], at["decayed"] + LH * (i + 1))
                            for kt in range(2):
                                for j in range(LH):
                                    mm = pe.matmul(G.ps[32 * j:32 * j + 32, 2, i * TOK:(i + 1) * TOK],
                                                   G.vr[:, 2 * i + kt, 32 * j:32 * j + 32],
                                                   G.p[0:TT, j, kt * TOK:(kt + 1) * TOK],
                                                   start=(kt == 0), stop=(kt == 1))
                            mm.then_inc(S["av_psum"], 1)
                        elif op == "proj" and kind == "linear":
                            pe.wait_ge(S["o"], at["o"] + 1)
                            pe.matmul(bank(G, 3), wob[:, :], G.q[:, 1, :], start=True, stop=True).then_inc(S["proj_psum"], 1)
                        elif op == "gate":
                            pe.wait_ge(S["z"], at["z"])
                            for u in range(U):
                                mm = pe.matmul(G.ps[0:TT, 3, u * E:(u + 1) * E], src[:, u * TT:(u + 1) * TT], wg[:, n, :],
                                               start=True, stop=True)
                            mm.then_inc(S["gate_psum"], 1)
                        elif op == "up":
                            r = i + i // ft
                            if r >= 2:
                                pe.wait_ge(S["up_read"], at["up_read"] + r - 1)
                            pe.matmul(bank(G, r % 2), w1[n][:, i, :], src[:, :], start=True, stop=True)\
                                .then_inc(S["up_psum"], 1)
                        elif op == "spread":
                            r = i * (ft + 1) + ft
                            pe.wait_ge(S["gateT"], at["gateT"] + 1)
                            pe.wait_ge(S["up_read"], at["up_read"] + r - 1)
                            pe.matmul(bank(G, r % 2), expertb[:, i, :], G.ct[:, :], start=True, stop=True)\
                                .then_inc(S["up_psum"], 1)
                        elif op == "gateT":
                            pe.wait_ge(S["parts"], at["parts"] + 1)
                            for u in range(U):
                                mm = pe.matmul(G.ps[:, 3, u * TT:(u + 1) * TT], G.cc[:, u, :],
                                               identb[0:TT, 0:TT], start=True, stop=True)
                            mm.then_inc(S["gateT_psum"], 1)
                        elif op == "down":
                            e, f = divmod(i, ft)
                            pe.wait_ge(S["up_read"], at["up_read"] + i + e + 1)
                            if f == 0 and e == 1:
                                pe.wait_ge(S["gateT"], at["gateT"] + 1)
                            if f == 0 and e >= 2:
                                pe.wait_ge(S["term"], at["term"] + e - 1)
                            pe.matmul(bank(G, 2 + e % 2), w2[n][:, i, :], G.hid[:, i % 4, :], start=(f == 0),
                                      stop=(f == ft - 1)).then_inc(S["down"], 1)
                        elif op == "out_turn":
                            pe.wait_ge(S["h"], at["h"] + 1)
                            for u in range(U):
                                mm = pe.transpose(G.ps[0:TT, 0, u * D:(u + 1) * D], G.h[:, u * TT:(u + 1) * TT], ident[:, :])
                            mm.then_inc(S["out_psum"], 1)
                        else:
                            raise ValueError(op)

                @block.scalar
                def _(act):
                    table = None
                    for g, (engine, op, i, _, _, kind, n, rnd, counts) in ORDER:
                        if engine != "act":
                            continue
                        G, S = groups[g], groups[g].s
                        at = {name: counts.get(name, 0) for name in NAMES}
                        ft = F0 if n == 0 else F1
                        if TABLES.get(op, table) != table:
                            table = TABLES[op]
                            if table == "log":
                                act.preload_act_table_set("natural_log_exp_and_others")
                        if op == "square":
                            cols = image(i) if kind == "ln_h" else ALL
                            act.wait_ge(S["h"], at["h"] - (NB - 1 - i if kind == "ln_h" else 0))
                            wait(act, S["stat_psum"], at["stat_psum"])
                            if kind == "ln_z":
                                act.wait_ge(S["z"], at["z"])
                            if kind == "moe0_out":
                                act.wait_ge(S["s"], at["s"] + 1)
                            act.activation(G.sq[:, cols], (G.h if kind == "ln_h" else G.z)[:, cols], ACT.Square)\
                                .then_inc(S["sq"], 1)
                        elif op == "center_read":
                            act.wait_ge(S["cen_psum"], at["cen_psum"] + 1)
                            act.activation(G.u, bank(G, 1), ACT.Copy).then_inc(S["cen"], 1)
                            act.activation(G.sq, bank(G, 1), ACT.Square).then_inc(S["sq"], 1)
                        elif op == "rstd":
                            t = piece(G, 0, i) if kind == "ln_h" else bank(G, 0)
                            act.wait_ge(S["stat_psum"], at["stat_psum"] + i + 1)
                            act.activation(t, t, ACT.Ln, bias=eps[:, 0:1]).then_inc(S["log"], 1)
                            act.wait_ge(S["log"], at["log"] + i + 1)
                            act.activation(t, t, ACT.Exp, scale=-0.5).then_inc(S["rstd"], 1)
                        elif op == "q_read":
                            act.wait_ge(S["qk_psum"], at["qk_psum"] + i + 1)
                            if kind == "qkv":
                                act.activation(G.q[:, i, :], bank(G, i), ACT.Identity, bias=v("qk_b", 4 * n + i))\
                                    .then_inc(S["q"], 1)
                            else:
                                act.activation(G.q[:, i, :], bank(G, i), ACT.Copy).then_inc(S["q"], 1)
                        elif op == "k_read":
                            if n == 0 and i == 0:
                                act.wait_ge(S["zeroed"], at["zeroed"] - 5)
                            r = slice(32 * (i % 4), 32 * (i % 4) + 32)
                            act.wait_ge(S["qk_psum"], at["qk_psum"] + 3 + i // 4)
                            act.activation(real(G.k_high[r, i, :]), real(bank(G, 2 + i // 4)[r]), ACT.Identity,
                                           bias=v("qk_b", 4 * n + 2 + i // 4)[r]).then_inc(S["k"], 1)
                        elif op == "v_read":
                            act.wait_ge(S["v_psum"], at["v_psum"] + 1)
                            if kind == "qkv":
                                act.activation(G.va[:, :, :, 0:HD].rearrange("p u h d -> p (u h) d"),
                                               G.ps[0:TT, 0, 0:U * D].rearrange("p (uh d) -> p uh d", d=HD), ACT.Copy)\
                                    .then_inc(S["v"], 1)
                            else:
                                act.activation(G.vr[:, :, :], G.ps[0:TT, 2, 0:U * D].rearrange("p (u d) -> p u d", u=U),
                                               ACT.Copy).then_inc(S["v"], 1)
                        elif op == "exp" and kind == "attn":
                            act.wait_ge(S["st_psum"], at["st_psum"] + i + 1)
                            if i >= RING:
                                act.wait_ge(S["av_psum"], at["av_psum"] + (i - RING) // 4 + 1)
                            if n == 0 and i == 1:
                                wait(act, G.out_done, 16 * rnd)
                            act.activation(G.ring[0:TT, i % RING, :], G.ps[0:TT, i % 2, 0:2 * TOK], ACT.Exp,
                                           scale=HD ** -0.5).then_inc(S["exp"], 1)
                        elif op == "o_read" and kind == "attn":
                            grp, b = divmod(i, NB)
                            act.wait_ge(S["av_psum"], at["av_psum"] + i + 1)
                            act.activation(G.o[:, grp, image(b)], piece(G, 2, b, grp), ACT.Copy)\
                                .then_inc(S["o"], 1)
                        elif op == "rsum" and kind == "attn":
                            grp, b = divmod(i, NB)
                            t = piece(G, 2, b, grp)
                            act.wait_ge(S["sum_psum"], at["sum_psum"] + i + 1)
                            act.activation(t, t, ACT.Ln).then_inc(S["log"], 1)
                            act.wait_ge(S["log"], at["log"] + i + 1)
                            act.activation(t, t, ACT.Exp, scale=-1.0).then_inc(S["rsum"], 1)
                        elif op == "gelu":
                            act.wait_ge(S["fc1_psum"], at["fc1_psum"] + 2 * i + 2)
                            for f in range(2):
                                act.activation(G.hid[:, f, image(i)], piece(G, 0, i, f), ACT.Gelu,
                                               bias=v("fc1_b", 2 * n + f)).then_inc(S["hid"], 1)
                        elif op == "exp" and kind == "retention":
                            act.wait_ge(S["st_psum"], at["st_psum"] + i + 1)
                            for kt in range(2):
                                ex = act.activation(G.p[0:TT, i, kt * TOK:(kt + 1) * TOK],
                                                    G.ps[0:TT, 2 + i, kt * TOK:(kt + 1) * TOK], ACT.Exp,
                                                    bias=key_decay[:, kt:kt + 1], scale=D ** -0.5)
                            ex.then_inc(S["exp"], 1)
                        elif op == "rsum" and kind == "retention":
                            act.wait_ge(S["sum_psum"], at["sum_psum"] + 1)
                            act.activation(bank(G, 1), bank(G, 1), ACT.Ln).then_inc(S["log"], 1)
                            act.wait_ge(S["log"], at["log"] + 1)
                            act.activation(G.sq, bank(G, 1), ACT.Exp, scale=-1.0).then_inc(S["rsum"], 1)
                        elif op == "qk_square":
                            act.wait_ge(S["qk_psum"], at["qk_psum"] + i + 1)
                            act.wait_ge(S["stat_psum"], at["stat_psum"] + i)
                            act.activation(G.sq, bank(G, i), ACT.Square).then_inc(S["sq"], 1)
                        elif op == "rnorm":
                            t = G.p[:, 4 + i, 0:NC]
                            act.wait_ge(S["floor"], at["floor"] + i + 1)
                            act.activation(t, t, ACT.Ln).then_inc(S["log"], 1)
                            act.wait_ge(S["log"], at["log"] + i + 1)
                            act.activation(t, t, ACT.Exp, bias=eps[:, 1:2], scale=-0.5).then_inc(S["rstd"], 1)
                        elif op == "o_read" and kind == "linear":
                            act.wait_ge(S["av_psum"], at["av_psum"] + NB)
                            act.activation(G.q[:, 1, :], bank(G, 2), ACT.Copy).then_inc(S["o"], 1)
                        elif op == "gap_exp":
                            act.wait_ge(S["gap"], at["gap"] + 1)
                            act.activation(G.sc[:, 1, :, 0], G.sc[:, 0, :, 0], ACT.Exp).then_inc(S["egap"], 1)
                        elif op in ("hid_tanh", "hid_relu"):
                            r = i + i // ft
                            act.wait_ge(S["up_psum"], at["up_psum"] + r + 1)
                            if i >= 4:
                                act.wait_ge(S["down"], at["down"] + i - 3)
                            act.activation(G.hid[:, i % 4, :], bank(G, r % 2),
                                           ACT.Gelu_apprx_tanh if n == 0 else ACT.Relu,
                                           bias=v("m0_b1" if n == 0 else "m1_b1", i)).then_inc(S["up_read"], 1)
                        elif op == "ct_read":
                            act.wait_ge(S["gateT_psum"], at["gateT_psum"] + 1)
                            act.activation(G.ct[:, :], bank(G, 3), ACT.Copy).then_inc(S["gateT"], 1)
                        elif op == "spread_read":
                            r = i * (ft + 1) + ft
                            act.wait_ge(S["up_psum"], at["up_psum"] + r + 1)
                            if i >= 2:
                                act.wait_ge(S["term"], at["term"] + i - 1)
                            act.activation(G.cb[:, i % 2, :], bank(G, r % 2), ACT.Copy).then_inc(S["up_read"], 1)
                        elif op == "affine":
                            act.wait_ge(S["z"], at["z"] + 1)
                            act.activation(G.sq, G.z[:, :], ACT.Identity, bias=v("out_b"), scale=v("out_g"))\
                                .then_inc(S["affine"], 1)
                        elif op == "out_read":
                            act.wait_ge(S["out_psum"], at["out_psum"] + 1)
                            act.activation(G.ob[:, :, :], G.ps[0:TT, 0, 0:U * D].rearrange("p (u d) -> p u d", u=U), ACT.Copy)\
                                .then_inc(S["out_sb"], 1)
                            act.wait_ge(S["out_sb"], rnd + 1)
                            first = (it * (NG * ROUNDS) + rnd * NG + g) * NB
                            act.dma_start(out[bass.ds(first, NB)].rearrange("b (t p) d -> p (b t) d", t=2), G.ob[:, :, :])\
                                .then_inc(G.out_done, 16)
                        else:
                            raise ValueError(op)

                @block.vector
                def _(dve):
                    for g, (engine, op, i, _, _, kind, n, rnd, counts) in ORDER:
                        if engine != "dve":
                            continue
                        G, S = groups[g], groups[g].s
                        at = {name: counts.get(name, 0) for name in NAMES}
                        ft = F0 if n == 0 else F1
                        if op == "conv_h":
                            hv = G.h[:, :].rearrange("p (b n) -> p b n", b=NB)
                            if i == 0:
                                wait(dve, S["out_psum"], at["out_psum"])
                                dve.tensor_copy(hv[:, :, 0:2], posb[:, 0:2].unsqueeze(1).to_broadcast([D, NB, 2]))\
                                    .then_inc(S["h"], 1)
                            dve.wait_ge(S["conv_psum"], at["conv_psum"] + i + 1)
                            dve.tensor_tensor(hv[:, i, 2:TOK], G.ps[:, i, 0:GRID * GRID], posb[:, 2:TOK], ALU.add)\
                                .then_inc(S["h"], 1)
                        elif op == "scale":
                            src, dst = {"ln_h": (G.h, G.z), "ln_z": (G.z, G.u), "ln_full": (G.u, G.z),
                                        "moe0_out": (G.z, G.z)}[kind]
                            cols = image(i) if kind == "ln_h" else ALL
                            dve.wait_ge(S["rstd"], at["rstd"] + i + 1)
                            rstd = piece(G, 0, i) if kind == "ln_h" else bank(G, 0)
                            dve.tensor_tensor(dst[:, cols], src[:, cols], rstd, ALU.mult).then_inc(S["z"], 1)
                        elif op == "q_round":
                            dve.wait_ge(S["q"], at["q"] + i + 1)
                            dve.tensor_copy(G.q_bf[:, i, :], G.q[:, i, :]).then_inc(S["q_bf"], 1)
                        elif op == "q_split":
                            high, both = G.q_parts[:, 2 + i, :], G.q_parts[:, i, :]
                            dve.wait_ge(S["q"], at["q"] + i + 1)
                            dve.tensor_copy(high, G.q[:, i, :]).then_inc(S["q_high"], 1)
                            dve.wait_ge(S["q_high"], at["q_high"] + i + 1)
                            dve.scalar_tensor_tensor(out=both, in0=high.bitcast(F32), scalar=halves[:, 0:1],
                                                     in1=G.q[:, i, :], op0=ALU.mult, op1=ALU.add)\
                                .then_inc(S["q_parts"], 1)
                        elif op == "k_low":
                            r = slice(32 * (i % 4), 32 * (i % 4) + HD)
                            if n == 0 and i == 0:
                                dve.wait_ge(S["zeroed"], at["zeroed"])
                            dve.wait_ge(S["k"], at["k"] + i + 1)
                            dve.scalar_tensor_tensor(out=real(G.k_low[r, i, :]), in0=real(bank(G, 2 + i // 4)[r]),
                                                     scalar=v("qk_b", 4 * n + 2 + i // 4)[r],
                                                     in1=real(G.k_high[r, i, :]).bitcast(F32), op0=ALU.add,
                                                     op1=ALU.subtract).then_inc(S["k_low"], 1)
                        elif op == "max" and kind == "qkv":
                            dve.wait_ge(S["smax_psum"], at["smax_psum"] + i + 1)
                            b0 = (i * NB) % 4
                            src = G.ps[0:TT, b0:b0 + NB, 0:2 * TOK].rearrange("p b (t n) -> p b t n", t=2)[:, :, :, 1:TOK]
                            dve.tensor_reduce(G.negm[:, i], src, X, ALU.max, negate=True).then_inc(S["max"], 1)
                        elif op == "max_parts":
                            if kind == "qkv":
                                dve.wait_ge(S["max"], at["max"] + HEADS)
                                src = G.negm[:, :, :, :].rearrange("p (g j) b t -> p (b t) g j", g=2)
                                hi, lo = (G.mt[:, :, :, 16 + k::32] for k in range(2))
                            else:
                                dve.wait_ge(S["max"], at["max"] + NB)
                                src = G.negm[:, 0, :, :].rearrange("p b t -> p (b t)")
                                hi, lo = (G.mt[:, :, 0, 16 + k] for k in range(2))
                            dve.tensor_copy(hi, src).then_inc(S["mt_hi"], 1)
                            dve.wait_ge(S["mt_hi"], at["mt_hi"] + 1)
                            dve.tensor_tensor(lo, src, hi, ALU.subtract).then_inc(S["mt"], 1)
                        elif op == "q_shift":
                            dve.wait_ge(S["mrow_psum"], at["mrow_psum"] + i + 1)
                            dve.scalar_tensor_tensor(out=G.q_parts[:, 2 + i, :], in0=G.q[:, i, :], scalar=halves[:, 1:2],
                                                     in1=bank(G, i), op0=ALU.mult, op1=ALU.add).then_inc(S["q_aug"], 1)
                        elif op == "o_scale" and kind == "attn":
                            grp, b = divmod(i, NB)
                            dve.wait_ge(S["rsum"], at["rsum"] + i + 1)
                            dve.tensor_tensor(G.o[:, grp, image(b)], G.o[:, grp, image(b)], piece(G, 2, b, grp),
                                              ALU.mult).then_inc(S["o_norm"], 1)
                        elif op in ("proj_add", "fc2_add") and kind in ("attn", "mlp"):
                            made, src, bias = ("proj_psum", piece(G, 0, i), "proj_b") if kind == "attn" else \
                                ("fc2_psum", piece(G, 2, i), "fc2_b")
                            cols = slice(i * TOK + 1, (i + 1) * TOK)
                            dve.wait_ge(S[made], at[made] + i + 1)
                            dve.scalar_tensor_tensor(out=G.h[:, cols], in0=src[:, 1:TOK], scalar=v(bias, n),
                                                     in1=G.h[:, cols], op0=ALU.add, op1=ALU.add).then_inc(S["h"], 1)
                        elif op == "tower_out":
                            dve.wait_ge(S["z"], at["z"])
                            dve.tensor_scalar(G.h[:, :], G.z[:, :], v("norm_w"), v("norm_b"), ALU.mult, ALU.add)\
                                .then_inc(S["affine"], 1)
                            dve.wait_ge(S["affine"], at["affine"] + 1)
                            hv = G.h[:, :].rearrange("p (b n) -> p b n", b=NB)
                            dve.tensor_copy(hv[:, :, 0:1], v("cls_out").unsqueeze(1).to_broadcast([D, NB, 1]))\
                                .then_inc(S["h"], 1)
                        elif op == "max" and kind == "retention":
                            dve.wait_ge(S["smax_psum"], at["smax_psum"] + i + 1)
                            dve.tensor_reduce(G.negm[:, 0, i], G.ps[0:TT, i, 0:2 * TOK].rearrange("p (t n) -> p t n", t=2),
                                              X, ALU.max, negate=True).then_inc(S["max"], 1)
                        elif op == "o_scale" and kind == "retention":
                            dve.wait_ge(S["rsum"], at["rsum"] + 1)
                            dve.wait_ge(S["av_psum"], at["av_psum"] + 1)
                            dve.tensor_tensor(G.z[:, :], bank(G, 0), G.sq, ALU.mult).then_inc(S["o_norm"], 1)
                            dve.wait_ge(S["o_norm"], at["o_norm"] + 1)
                            dve.tensor_tensor(G.h[:, :], G.h[:, :], G.z[:, :], ALU.add).then_inc(S["h"], 1)
                        elif op == "top":
                            L, mx = G.lg[:, 0], G.lg[:, 1]
                            dve.wait_ge(S["gate_psum"], at["gate_psum"] + 1)
                            dve.tensor_tensor(L, G.ps[0:TT, 3, 0:U * E].rearrange("p (u e) -> p u e", u=U),
                                              gb[:, n, :].unsqueeze(1).to_broadcast([TT, U, E]), ALU.add)\
                                .then_inc(S["logit"], 1)
                            dve.wait_ge(S["logit"], at["logit"] + 1)
                            for u in range(U):
                                dve.max(mx[:, u], L[:, u]).then_inc(S["top"], 1)
                            dve.wait_ge(S["top"], at["top"] + U)
                            dve.tensor_tensor(G.sc[:, 0, :, 0:1], mx[:, :, 1:2], mx[:, :, 0:1], ALU.subtract)\
                                .then_inc(S["gap"], 1)
                            for u in range(U):
                                dve.max_index(G.ix[:, u], mx[:, u], L[:, u]).then_inc(S["topi"], 1)
                        elif op == "gates":
                            done = [0]

                            def link(ins):
                                done[0] += 1
                                ins.then_inc(S["g"], 1)
                                dve.wait_ge(S["g"], at["g"] + done[0])

                            gt, c1, c2, r1, r2 = (G.lg[:, k] for k in range(2, 7))
                            egap, total, wa, wb = (G.sc[:, k, :, 0:1] for k in range(1, 5))
                            dve.wait_ge(S["topi"], at["topi"] + U)
                            link(dve.tensor_copy(r1[:, :, 0:2], G.ix[:, :, 0:2]))
                            dve.wait_ge(S["egap"], at["egap"] + 1)
                            link(dve.tensor_scalar(total, egap, 1.0, None, ALU.add))
                            link(dve.reciprocal(wa, total))
                            link(dve.tensor_tensor(wb, wa, egap, ALU.mult))
                            io = iota[:, :].unsqueeze(1).to_broadcast([TT, U, E])
                            dve.tensor_tensor(c1, io, r1[:, :, 0:1].to_broadcast([TT, U, E]), ALU.is_equal)
                            link(dve.tensor_tensor(c2, io, r1[:, :, 1:2].to_broadcast([TT, U, E]), ALU.is_equal))
                            dve.tensor_tensor(c1, c1, wa.to_broadcast([TT, U, E]), ALU.mult)
                            link(dve.tensor_tensor(c2, c2, wb.to_broadcast([TT, U, E]), ALU.mult))
                            link(dve.tensor_tensor(gt, c1, c2, ALU.add))
                            p1, p2, p3 = (G.cc[:, :, 32 * k:32 * k + E] for k in range(3))
                            link(dve.tensor_copy(p1, gt))
                            link(dve.tensor_tensor(r2, gt, p1, ALU.subtract))
                            dve.tensor_copy(p2, r2).then_inc(S["mid"], 1)
                            dve.wait_ge(S["mid"], at["mid"] + 1)
                            dve.tensor_tensor(p3, r2, p2, ALU.subtract).then_inc(S["parts"], 1)
                        elif op == "term":
                            dve.wait_ge(S["down"], at["down"] + (i + 1) * ft)
                            dve.wait_ge(S["up_read"], at["up_read"] + (i + 1) * (ft + 1))
                            if i > 1:
                                dve.wait_ge(S["acc"], at["acc"] + i - 1)
                            dve.scalar_tensor_tensor(out=G.acc if i == 0 else G.sq, in0=bank(G, 2 + i % 2),
                                                     scalar=v("m0_b2" if n == 0 else "m1_b2", i), in1=G.cb[:, i % 2, :],
                                                     op0=ALU.add, op1=ALU.mult).then_inc(S["term"], 1)
                        elif op == "acc":
                            dve.wait_ge(S["term"], at["term"] + i + 1)
                            dve.tensor_tensor(G.acc, G.acc, G.sq, ALU.add).then_inc(S["acc"], 1)
                        elif op == "sum_z":
                            dve.wait_ge(S["acc"], at["acc"])
                            dve.tensor_tensor(G.z[:, :], G.z[:, :], G.acc, ALU.add).then_inc(S["s"], 1)
                        elif op == "out_add" and kind == "moe0_out":
                            dve.wait_ge(S["affine"], at["affine"] + 1)
                            dve.tensor_tensor(G.h[:, :], G.h[:, :], G.sq, ALU.add).then_inc(S["h"], 1)
                        elif op == "floor":
                            dve.wait_ge(S["stat_psum"], at["stat_psum"] + i + 1)
                            dve.tensor_scalar(G.p[:, 4 + i, 0:NC], bank(G, 3), TINY, LIFT, ALU.max, ALU.mult)\
                                .then_inc(S["floor"], 1)
                        elif op == "q_scale":
                            dve.wait_ge(S["rstd"], at["rstd"] + 1)
                            dve.tensor_tensor(G.q[:, 0, :], bank(G, 0), G.p[:, 4, 0:NC], ALU.mult).then_inc(S["q"], 1)
                        elif op == "k_scale":
                            dve.wait_ge(S["rstd"], at["rstd"] + 2)
                            dve.wait_ge(S["zeroed"], at["zeroed"])
                            for h in range(LH):
                                r = slice(32 * h, 32 * h + 32)
                                dve.tensor_tensor(G.k[r, h, :], bank(G, 1)[r], G.p[r, 5, 0:NC], ALU.mult).then_inc(S["k"], 1)
                        elif op == "decay":
                            b, h = divmod(i, LH)
                            dve.wait_ge(S["st_psum"], at["st_psum"] + i + 1)
                            if b > 0:
                                dve.wait_ge(S["av_psum"], at["av_psum"] + b)
                            for kt in range(2):
                                c = TT - kt * TT
                                dx = dve.tensor_tensor(G.p[0:TT, h, kt * TOK:(kt + 1) * TOK],
                                                       G.ps[0:TT, i % 2, kt * TOK:(kt + 1) * TOK],
                                                       decay[:, h, c:c + TOK], ALU.mult)
                            dx.then_inc(S["decayed"], 1)
                        elif op == "proj_add":
                            dve.wait_ge(S["proj_psum"], at["proj_psum"] + 1)
                            dve.tensor_tensor(G.h[:, :], G.h[:, :], bank(G, 3), ALU.add).then_inc(S["h"], 1)
                        elif op == "out_add":
                            dve.wait_ge(S["acc"], at["acc"])
                            dve.tensor_tensor(G.h[:, :], G.h[:, :], G.acc, ALU.add).then_inc(S["h"], 1)
                        else:
                            raise ValueError(op)

                @block.gpsimd
                def _(pool):
                    conv = [c for _, op, i, _, _, kind, _, _, c in OPS if op == "conv" and i == 0]
                    blocks = [c for _, op, i, _, _, kind, _, _, c in OPS if op == "tower_out"]
                    for rnd in range(ROUNDS):
                        for G in groups:
                            done = conv[rnd].get("zeroed", 0)
                            pool.wait_ge(G.s["conv_psum"], NB * (rnd + 1))
                            high, low = (G.keys[:, i * KW:(i + 1) * KW].bitcast(F32) for i in range(2))
                            pool.memset(high, 0.0).then_inc(G.s["zeroed"], 1)
                            pool.memset(low, 0.0).then_inc(G.s["zeroed"], 1)
                            low = low.rearrange("p (t j b n) -> p t j b n", t=2, j=4, b=NB)
                            for j in range(4):
                                pool.wait_ge(G.s["zeroed"], done + 2 + j)
                                pool.memset(low[32 * j:32 * j + 32, :, j, :, 1:TOK], 1.0).then_inc(G.s["zeroed"], 1)
                            pool.wait_ge(G.s["zeroed"], done + 6)
                        for G in groups:
                            pool.wait_ge(G.s["z"], blocks[rnd]["z"])
                            pool.memset(G.k[:, 0:LH, :], 0.0).then_inc(G.s["zeroed"], 1)

                @block.sync
                def _(sp):
                    through = [counts["h"] for _, op, _, _, _, kind, n, _, counts in OPS if op == "gate" and n == 1]
                    for rnd in range(ROUNDS):
                        for g, G in enumerate(groups):
                            sp.wait_ge(G.s["h"], through[rnd])
                            load_images(sp, G, (it * (NG * ROUNDS) + (rnd + 1) * NG + g) % (BATCH // NB))
                    for G in groups:
                        sp.wait_ge(G.x_in, XWAIT * ROUNDS)
                        sp.wait_ge(G.out_done, 16 * ROUNDS)

            with nc.Block() as block:
                @block.gpsimd
                def _(pool):
                    for G in groups:
                        pool.sem_clear(range(G.x_in.num, G.out_done.num + 1))


def _layout(inputs):
    a = {k: np.asarray(v) for k, v in inputs.items()}
    t = {k[len("L0_tok_"):]: v for k, v in a.items() if k.startswith("L0_tok_")}
    f32 = np.float32

    def pad_heads(w, twice=False):
        o = np.zeros((*w.shape[:-1], 2, 4, 32), f32)
        o[..., 0:HD] = w.reshape(*w.shape[:-1], 2, 4, HD)
        if twice:
            o[..., HD:] = o[..., 0:HD]
        return o.reshape(*w.shape[:-1], 2, D)

    qkv = t["qkv_w"].reshape(DEPTH, D, 3, D)
    qkv_b = t["qkv_b"].reshape(DEPTH, 3, D)
    qk_b = pad_heads(qkv_b[:, 0:2], twice=True)
    cols = {
        "conv_b": t["conv_b"], "cls_in": t["cls_token"].reshape(-1), "cls_out": a["cls_tok"].reshape(-1),
        "norm_w": t["norm_w"], "norm_b": t["norm_b"], "ln1_w": t["ln1_w"].T, "ln1_b": t["ln1_b"].T,
        "ln2_w": t["ln2_w"].T, "ln2_b": t["ln2_b"].T, "proj_b": t["proj_b"].T, "fc2_b": t["fc2_b"].T,
        "fc1_b": t["fc1_b"].reshape(DEPTH * 2, D).T, "qk_b": qk_b.reshape(DEPTH * 4, D).T,
        "v_b": pad_heads(qkv_b[:, 2]).reshape(DEPTH * 2, D).T,
        "ln_g": a["L0_ffn_ln_g"], "ln_b": a["L0_ffn_ln_b"], "out_g": a["L0_ffn_out_g"], "out_b": a["L0_ffn_out_b"],
        "m0_b1": a["L0_ffn_b1"].reshape(E * F0, D).T, "m0_b2": a["L0_ffn_b2"].T,
        "m1_b1": a["L1_ffn_b1"].reshape(E * F1, D).T, "m1_b2": a["L1_ffn_b2"].T,
        "out_scale": np.broadcast_to(a["L1_attn_out_scale"].reshape(1), (D,)),
    }
    vecs = np.concatenate([np.reshape(cols[n], (D, w)) for n, (_, w) in VEC.items()], 1)
    o = {
        "x": a["x"], "conv_w": t["conv_w"], "pos_t": t["pos_embed"][0].T, "vecs": vecs,
        "w_qk": pad_heads(qkv[:, :, 0:2], twice=True).transpose(1, 0, 2, 3, 4).reshape(D, DEPTH, 4, D),
        "w_v": qkv[:, :, 2].transpose(1, 0, 2),
        "w_v_pad": pad_heads(qkv[:, :, 2]).transpose(1, 0, 2, 3),
        "w_p": pad_heads(t["proj_w"].transpose(0, 2, 1)).transpose(3, 0, 2, 1),
        "w_fc1": t["fc1_w"].transpose(1, 0, 2),
        "w_fc2": t["fc2_w"].reshape(DEPTH, 2, D, D).transpose(2, 0, 1, 3),
        "w_ret": np.stack([a["L0_attn_Wq"], a["L0_attn_Wk"], a["L0_attn_Wv"]], 1),
        "w_lin": np.stack([a["L1_attn_shared_q_w"], a["L1_attn_shared_k_w"]], 1),
        "coef": np.stack([a["L1_attn_basis"].T, a["L1_attn_v_coeffs"].T, a["L1_attn_o_coeffs"].T], 1),
        "gates": np.stack([a["L0_ffn_Wg"], a["L1_ffn_gate_w"]], 1),
        "gate_b": np.broadcast_to(a["L1_ffn_gate_b"], (TT, E)),
        "decay_logits": np.broadcast_to(a["L1_attn_decay_logits"], (TT, LH)),
        "m0_w1": a["L0_ffn_W1"].reshape(E, D, F0, D).transpose(1, 0, 2, 3).reshape(D, E * F0, D),
        "m0_w2": a["L0_ffn_W2"].reshape(E * F0, D, D).transpose(1, 0, 2),
        "m1_w1": a["L1_ffn_w1"].reshape(E, D, F1, D).transpose(1, 0, 2, 3).reshape(D, E * F1, D),
        "m1_w2": a["L1_ffn_w2"].reshape(E * F1, D, D).transpose(1, 0, 2),
    }
    return {k: np.ascontiguousarray(v) for k, v in o.items()}


def kernel(**inputs):
    import concourse.bacc as _bacc
    from concourse.bass_utils import run_bass_kernel_spmd as _run

    nc = _bacc.Bacc("TRN2", target_bir_lowering=False, num_devices=1)
    data, consts = _layout(inputs), constants()
    arrays, args = {}, {}
    for name, a in (*data.items(), *(("c_" + k, c) for k, c in consts.items())):
        arrays["in_" + name] = a
        args[name] = nc.dram_tensor("in_" + name, a.shape, mybir.dt.from_np(a.dtype), kind="ExternalInput").ap()
    out = nc.dram_tensor("out_0", (BATCH, TOK, D), F32, kind="ExternalOutput").ap()
    tower_kernel(nc, *(args[n] for n in data), {k: args["c_" + k] for k in consts}, out)
    r = _run(nc, [arrays], core_ids=[0])
    return r.results[0]["out_0"]
```
